# Optimizing a Trainium2 kernel written in Bass

```python
import numpy as np
import jax
import jax.numpy as jnp

def _softmax(x, axis=-1):
    return jax.nn.softmax(x, axis=axis)

def _gelu(x):
    return jax.nn.gelu(x, approximate=True)

def _silu(x):
    return jax.nn.silu(x)

def _sigmoid(x):
    return jax.nn.sigmoid(x)

def _layernorm(x, axis=-1, eps=1e-05):
    m = jnp.mean(x, axis=axis, keepdims=True)
    v = jnp.var(x, axis=axis, keepdims=True)
    return (x - m) / jnp.sqrt(v + eps)

def _scatter_add(tgt, idx, src, axis=0):
    return tgt.at[idx].add(src)

def _segment_sum(src, seg, n):
    return jax.ops.segment_sum(src, seg, n)
kernel_name = 'mk_gnn_preln_d4_gnn_r8_3ec969'

def setup_inputs(seed: int=0):
    np.random.seed(seed)
    _w = jnp.asarray

    def _rec_inputs():
        import jax
        import jax.numpy as jnp
        _gk = jax.random.key(seed)
        x = -0.0005121 + 1.001 * jax.random.normal(jax.random.fold_in(_gk, 1), (12500, 32), jnp.float32)
        src = jax.random.randint(jax.random.fold_in(_gk, 2), (200000,), 0, 12500, jnp.int32)
        dst = jax.random.randint(jax.random.fold_in(_gk, 3), (200000,), 0, 12500, jnp.int32)
        _o = jnp.argsort(dst, stable=True)
        src = src[_o]
        dst = dst[_o]
        edge_attr_32 = -0.00010739 + 0.99994 * jax.random.normal(jax.random.fold_in(_gk, 12), (200000, 32), jnp.float32)
        return (x, src, dst, edge_attr_32)
    x, src, dst, edge_attr_32 = _rec_inputs()

    def _L0_gnn_setup():
        import jax, jax.numpy as jnp
        import numpy as np
        N = 12500
        E = 200000
        F_IN = 32
        F_OUT = 32
        key = jax.random.key(seed)
        k1, k2, k3, k4, k5 = jax.random.split(key, 5)
        x = jax.random.normal(k1, (N, F_IN), dtype=jnp.float32)
        edge_src = jax.random.randint(k2, (E,), 0, N, dtype=jnp.int32)
        edge_dst = jax.random.randint(k3, (E,), 0, N, dtype=jnp.int32)
        bound = 1.0 / np.sqrt(2 * F_IN)
        W = jax.random.uniform(k4, (2 * F_IN, F_OUT), minval=-bound, maxval=bound, dtype=jnp.float32)
        b = jax.random.uniform(k5, (F_OUT,), minval=-bound, maxval=bound, dtype=jnp.float32)
        return {'x': x, 'W': W, 'b': b, 'edge_src': edge_src, 'edge_dst': edge_dst}
    _L0_gnn_all = _L0_gnn_setup()
    _L0_gnn_in = {k: v for k, v in _L0_gnn_all.items() if k in ('W', 'b')}
    del _L0_gnn_all

    def _L1_gnn_setup():
        import jax, jax.numpy as jnp
        import numpy as np
        N_NODES = 12500
        N_EDGES = 50000
        D = 32
        EH = 128
        STEPS = 6

        def _gru_cell(x, h, wih, whh, bih, bhh):
            gi = x @ wih.T + bih
            gh = h @ whh.T + bhh
            ir, iz, inn = jnp.split(gi, 3, axis=-1)
            hr, hz, hn = jnp.split(gh, 3, axis=-1)
            r = jax.nn.sigmoid(ir + hr)
            z = jax.nn.sigmoid(iz + hz)
            n = jnp.tanh(inn + r * hn)
            return (1.0 - z) * n + z * h
        key = jax.random.key(seed)
        ks = jax.random.split(key, 12)
        s = 0.05
        return {'n_feat': jax.random.normal(ks[0], (N_NODES, D), jnp.float32), 'e_feat': jax.random.normal(ks[1], (N_EDGES, D), jnp.float32), 'src': jax.random.randint(ks[2], (N_EDGES,), 0, N_NODES, jnp.int32), 'dst': jax.random.randint(ks[3], (N_EDGES,), 0, N_NODES, jnp.int32), 'lin0_w': jax.random.normal(ks[4], (D, D), jnp.float32) * s, 'lin0_b': jnp.zeros((D,), jnp.float32), 'en1_w': jax.random.normal(ks[5], (EH, D), jnp.float32) * s, 'en1_b': jnp.zeros((EH,), jnp.float32), 'en2_w': jax.random.normal(ks[6], (D * D, EH), jnp.float32) * s, 'en2_b': jnp.zeros((D * D,), jnp.float32), 'conv_bias': jnp.zeros((D,), jnp.float32), 'gru_wih': jax.random.normal(ks[7], (3 * D, D), jnp.float32) * s, 'gru_whh': jax.random.normal(ks[8], (3 * D, D), jnp.float32) * s, 'gru_bih': jnp.zeros((3 * D,), jnp.float32), 'gru_bhh': jnp.zeros((3 * D,), jnp.float32)}
    _L1_gnn_all = _L1_gnn_setup()
    _L1_gnn_in = {k: v for k, v in _L1_gnn_all.items() if k in ('lin0_w', 'lin0_b', 'en1_w', 'en1_b', 'en2_w', 'en2_b', 'conv_bias', 'gru_wih', 'gru_whh', 'gru_bih', 'gru_bhh')}
    del _L1_gnn_all

    def _L2_gnn_setup():
        import jax, jax.numpy as jnp
        import numpy as np
        N_NODES = 6250
        N_EDGES = 200000
        D_FEAT = 32
        key = jax.random.key(seed)
        k1, k2, k3, k4 = jax.random.split(key, 4)
        node_feat = jax.random.normal(k1, (N_NODES, D_FEAT), dtype=jnp.float32)
        edge_feat = jax.random.normal(k2, (N_EDGES, D_FEAT), dtype=jnp.float32)
        eps = jnp.zeros((1,), dtype=jnp.float32)
        src = jax.random.randint(k3, (N_EDGES,), 0, N_NODES, dtype=jnp.int64)
        dst = jax.random.randint(k4, (N_EDGES,), 0, N_NODES, dtype=jnp.int64)
        return {'node_feat': node_feat, 'edge_feat': edge_feat, 'eps': eps, 'src': src, 'dst': dst}
    _L2_gnn_all = _L2_gnn_setup()
    _L2_gnn_in = {k: v for k, v in _L2_gnn_all.items() if k in ('eps',)}
    del _L2_gnn_all

    def _L3_gnn_setup():
        import jax, jax.numpy as jnp
        import numpy as np
        key = jax.random.key(seed)
        k1, k2 = jax.random.split(key)
        N, E, F = (12500, 200000, 32)
        edge_index = jax.random.randint(k1, (2, E), 0, N, dtype=jnp.int64)
        input_feature = jax.random.normal(k2, (N, F), dtype=jnp.float32)
        return {'edge_index': edge_index, 'input_feature': input_feature}
    _L3_gnn_all = _L3_gnn_setup()
    _L3_gnn_in = {k: v for k, v in _L3_gnn_all.items() if k in ()}
    del _L3_gnn_all
    return {'x': x, 'src': src, 'dst': dst, 'edge_attr_32': edge_attr_32, 'L0_gnn_W': _L0_gnn_in['W'], 'L0_gnn_b': _L0_gnn_in['b'], 'L1_gnn_lin0_w': _L1_gnn_in['lin0_w'], 'L1_gnn_lin0_b': _L1_gnn_in['lin0_b'], 'L1_gnn_en1_w': _L1_gnn_in['en1_w'], 'L1_gnn_en1_b': _L1_gnn_in['en1_b'], 'L1_gnn_en2_w': _L1_gnn_in['en2_w'], 'L1_gnn_en2_b': _L1_gnn_in['en2_b'], 'L1_gnn_conv_bias': _L1_gnn_in['conv_bias'], 'L1_gnn_gru_wih': _L1_gnn_in['gru_wih'], 'L1_gnn_gru_whh': _L1_gnn_in['gru_whh'], 'L1_gnn_gru_bih': _L1_gnn_in['gru_bih'], 'L1_gnn_gru_bhh': _L1_gnn_in['gru_bhh'], 'L2_gnn_eps': _L2_gnn_in['eps']}

def reference(x, src, dst, edge_attr_32, L0_gnn_W, L0_gnn_b, L1_gnn_lin0_w, L1_gnn_lin0_b, L1_gnn_en1_w, L1_gnn_en1_b, L1_gnn_en2_w, L1_gnn_en2_b, L1_gnn_conv_bias, L1_gnn_gru_wih, L1_gnn_gru_whh, L1_gnn_gru_bih, L1_gnn_gru_bhh, L2_gnn_eps):
    import jax
    import jax.numpy as jnp

    def _L0_gnn_ref(x, W, b, edge_src, edge_dst):
        import jax, jax.numpy as jnp
        import numpy as np
        N = 12500
        E = 200000
        F_IN = 32
        F_OUT = 32
        n = x.shape[0]
        msgs = x[edge_src]
        summed = jax.ops.segment_sum(msgs, edge_dst, num_segments=n)
        cnt = jax.ops.segment_sum(jnp.ones_like(edge_dst, dtype=x.dtype), edge_dst, num_segments=n)
        neigh_mean = summed / jnp.maximum(cnt, 1.0)[:, None]
        h = jnp.concatenate([x, neigh_mean], axis=1)
        return jax.nn.relu(h @ W + b)

    def _L1_gnn_ref(n_feat, e_feat, src, dst, lin0_w, lin0_b, en1_w, en1_b, en2_w, en2_b, conv_bias, gru_wih, gru_whh, gru_bih, gru_bhh):
        import jax, jax.numpy as jnp
        import numpy as np
        N_NODES = 12500
        N_EDGES = 50000
        D = 32
        EH = 128
        STEPS = 6

        def _gru_cell(x, h, wih, whh, bih, bhh):
            gi = x @ wih.T + bih
            gh = h @ whh.T + bhh
            ir, iz, inn = jnp.split(gi, 3, axis=-1)
            hr, hz, hn = jnp.split(gh, 3, axis=-1)
            r = jax.nn.sigmoid(ir + hr)
            z = jax.nn.sigmoid(iz + hz)
            n = jnp.tanh(inn + r * hn)
            return (1.0 - z) * n + z * h
        n_nodes = n_feat.shape[0]
        out = jax.nn.relu(n_feat @ lin0_w.T + lin0_b)
        h = out
        eh = jax.nn.relu(e_feat @ en1_w.T + en1_b)
        w_e = (eh @ en2_w.T + en2_b).reshape(-1, D, D)
        for _ in range(STEPS):
            msg = jnp.einsum('ei,eio->eo', out[src], w_e)
            agg = jax.ops.segment_sum(msg, dst, num_segments=n_nodes) + conv_bias
            m = jax.nn.relu(agg)
            h = _gru_cell(m, h, gru_wih, gru_whh, gru_bih, gru_bhh)
            out = h
        return out

    def _L2_gnn_ref(node_feat, edge_feat, eps, src, dst):
        import jax, jax.numpy as jnp
        import numpy as np
        N_NODES = 6250
        N_EDGES = 200000
        D_FEAT = 32
        m = jax.nn.relu(node_feat[src] + edge_feat)
        neigh = jax.ops.segment_sum(m, dst, num_segments=node_feat.shape[0])
        return (1.0 + eps[0]) * node_feat + neigh

    def _L3_gnn_ref(edge_index, input_feature):
        import jax, jax.numpy as jnp
        import numpy as np
        N = input_feature.shape[0]
        row, col = (edge_index[0], edge_index[1])
        w = jnp.where(row != col, 1.0, 0.0).astype(input_feature.dtype)
        loop = jnp.arange(N, dtype=row.dtype)
        row_f = jnp.concatenate([row, loop])
        col_f = jnp.concatenate([col, loop])
        w_f = jnp.concatenate([w, jnp.ones((N,), dtype=input_feature.dtype)])
        deg = jax.ops.segment_sum(w_f, col_f, num_segments=N)
        dis = jnp.where(deg > 0, jax.lax.rsqrt(deg), 0.0)
        ew = dis[row_f] * w_f * dis[col_f]
        out = jax.ops.segment_sum(ew[:, None] * input_feature[row_f], col_f, num_segments=N)
        return out
    edge_index = jnp.stack([src, dst])
    h = jnp.maximum(_layernorm(x, axis=-1), 0.0)
    x = x + _L0_gnn_ref(h, L0_gnn_W, L0_gnn_b, src, dst)
    h = jnp.maximum(_layernorm(x, axis=-1), 0.0)
    x = x + _L1_gnn_ref(h, edge_attr_32, src, dst, L1_gnn_lin0_w, L1_gnn_lin0_b, L1_gnn_en1_w, L1_gnn_en1_b, L1_gnn_en2_w, L1_gnn_en2_b, L1_gnn_conv_bias, L1_gnn_gru_wih, L1_gnn_gru_whh, L1_gnn_gru_bih, L1_gnn_gru_bhh)
    h = jnp.maximum(_layernorm(x, axis=-1), 0.0)
    x = x + _L2_gnn_ref(h, edge_attr_32, L2_gnn_eps, src, dst)
    h = jnp.maximum(_layernorm(x, axis=-1), 0.0)
    x = x + _L3_gnn_ref(edge_index, h)
    return x

_drawn_inputs = setup_inputs


def setup_inputs(seed=0):
    import zlib

    import numpy as np

    out = dict(_drawn_inputs(seed))
    spreads = {'L1_gnn_lin0_b': (0.0, 0.286),
     'L1_gnn_en1_b': (0.0, 0.1),
     'L1_gnn_en2_b': (0.0, 0.1),
     'L1_gnn_conv_bias': (0.0, 0.424),
     'L1_gnn_gru_bih': (0.0, 0.1),
     'L1_gnn_gru_bhh': (0.0, 0.267)}
    factors = {'L1_gnn_lin0_w': 4.257}
    for name, (base, spread) in spreads.items():
        noise = np.random.default_rng([zlib.crc32(name.encode()), seed]).standard_normal(out[name].shape)
        drawn = base * np.exp(spread * noise) if base else spread * noise
        out[name] = jnp.asarray(drawn.astype(out[name].dtype))
    for name, factor in factors.items():
        out[name] = (out[name] * factor).astype(out[name].dtype)
    return out
```

```python
import concourse.bass as bass
from concourse import mybir
from contextlib import ExitStack

N, E, D, KF, STEPS = 12500, 200000, 32, 128, 6
EDGES = 128
W = 12
GT = 10
SL = W * GT
T_REAL = -(-E // EDGES)
G = -(-T_REAL // GT)
G += G % 2
T = G * GT
RB = -(-T // 128)
MAXP = -(-EDGES // W)
P = 125
NB = N // P
NC2 = NB + 2
ZROW = G * SL
PAD_DST = 1 << 20
EPS = 1e-5


def bass_gnn(nc, x, srcg, src_t, dst_t, dst_rows, ef_e, ef_t, w0, b0, lin0, lin0_b, en1, en1_b,
             en2, en2_b, conv_b, wih, whh, bih, bhh, eps, out):
    f32, i32 = mybir.dt.float32, mybir.dt.int32
    ALU, ACT, AX = mybir.AluOpType, mybir.ActivationFunctionType, mybir.AxisListType
    with ExitStack() as ctx:
        def sb(name, shape, dt=f32):
            return ctx.enter_context(nc.sbuf_tensor(name, shape, dt))

        def sem(name):
            return ctx.enter_context(nc.semaphore(name))

        def dram(name, shape, dt=f32):
            return nc.dram_tensor(name, shape, dt, kind="Internal").ap()

        feat = dram("feat", (N, D))
        slots33 = dram("slots33", (ZROW + 1, D + 1))
        slots32 = dram("slots32", (ZROW + 1, D))
        ehid = dram("ehid", (G, 128, GT * KF))
        rowtab = dram("rowtab", (RB * 128, 2 * EDGES))
        slotnode = dram("slotnode", (MAXP, (G + 1) * SL))
        homes = dram("homes", (MAXP, P, NB), i32)

        ident = sb("ident", [128, 128])
        iota_w = sb("iota_w", [128, W])
        rank_t = sb("rank_t", [128, T])
        w_t = sb("w_t", [128, T])
        xcur = sb("xcur", [P, NB, D])
        hcur = sb("hcur", [P, NB, D])
        agg = sb("agg", [P, NB, D + 1])
        gat = sb("gat", [P, NB, D + 1])
        tmp = sb("tmp", [P, NB, D])
        home = sb("home", [P, NB], i32)
        cnt = sb("cnt", [P, NB])
        dis = sb("dis", [P, NB])
        mean = sb("mean", [P, NB])
        rstd = sb("rstd", [P, NB])
        eps_sb = sb("eps_sb", [P, 1])
        ln_eps = sb("ln_eps", [P, 1])
        w2 = sb("w2", [128, D, D])
        b2 = sb("b2", [D, D])
        last_tile = sb("last_tile", [SL, SL])
        npass = sb("npass", [1, 1], i32)
        pool_tick = sb("pool_tick", [1, 4])
        zrow = sb("zrow", [1, 256])
        bd_a = sb("bd_a", [128, 4 * D])
        bd_b = sb("bd_b", [128, 4 * D])
        bd_lin = sb("bd_lin", [128, 4 * D])
        bd_ih = sb("bd_ih", [128, 4 * 3 * D])
        bd_hh = sb("bd_hh", [128, 4 * 3 * D])
        bias0 = sb("bias0", [P, D])
        bias_lin = sb("bias_lin", [P, D])
        bias_conv = sb("bias_conv", [P, D])
        bias_ih = sb("bias_ih", [P, 3 * D])
        bias_hh = sb("bias_hh", [P, 3 * D])

        ps = [ctx.enter_context(nc.psum_tensor(f"bank{k}", [128, 512], f32)) for k in range(8)]

        def wait(eng, s, v):
            if not isinstance(v, int) or v > 0:
                eng.wait_ge(s, v)

        def close(sems, gathers=()):
            for s in gathers:
                nc.gpsimd.dma_reset(range(s.num, s.num + 1))
                nc.gpsimd.sem_clear(s)
            for s in sems:
                nc.gpsimd.sem_clear(s)
            nc.all_engine_barrier()

        class Chain:

            def __init__(self, eng, s):
                self.eng, self.s, self.n = eng, s, 0

            def __call__(self, ins):
                ins.then_inc(self.s, 1)
                self.n += 1
                self.eng.wait_ge(self.s, self.n)

        with ExitStack() as ph:
            def sbp(name, shape, dt=f32):
                return ph.enter_context(nc.sbuf_tensor(name, shape, dt))

            drow_i = sbp("drow_i", [128, RB, EDGES], i32)
            fnode = sbp("fnode", [128, RB, EDGES])
            rank = sbp("rank", [128, RB, EDGES])
            slotn = sbp("slotn", [128, RB, W])
            junk = sbp("junk", [128, EDGES])
            t0n = sbp("t0n", [P, NC2])
            c1 = sbp("c1", [P, NC2])
            d1 = sbp("d1", [P, NC2])
            idx1 = sbp("idx1", [P, NC2], i32)
            nodeid = sbp("nodeid", [P, NC2])
            rp = sbp("rp", [P, NC2])
            rr = sbp("rr", [P, NB])
            crosses = sbp("crosses", [P, NB])
            f_a = sbp("f_a", [P, NB])
            f_b = sbp("f_b", [P, NB])
            f_c = sbp("f_c", [P, NB])
            fint = sbp("fint", [P, NB], i32)

            s_in, s_zero, s_pool, s_ch, s_rk, s_tr, s_rt, s_done = [
                sem(n) for n in ("inputs_in", "zeroed", "pool_made", "dve_chain", "ranks_ready",
                                 "rank_transposed", "row_table_written", "setup_stored")]
            s_fb, s_t1, s_g1, s_u1, s_ev = [sem(n) for n in (
                "firsts_in", "tile_of_node", "tile_row_in", "tile_row_used", "rank_evacuated")]
            s_bd = sem("diagonals_in")
            sub = ExitStack()
            drow = sub.enter_context(nc.sbuf_tensor("drow", [128, RB, EDGES], f32))
            first = sub.enter_context(nc.sbuf_tensor("first", [128, RB, EDGES], f32))
            fdst = sub.enter_context(nc.sbuf_tensor("fdst", [128, RB, EDGES], f32))
            tcol_i = sub.enter_context(nc.sbuf_tensor("tcol_i", [128, 2, T], i32))
            with nc.Block() as block:
                @block.sync
                def _(sp):
                    sp.dma_start(drow_i[:, :, :], dst_rows.rearrange("(r p) e -> p r e", p=128)).then_inc(s_in, 16)
                    sp.dma_start(tcol_i[:, 0, :], src_t[:, :]).then_inc(s_in, 16)
                    sp.dma_start(tcol_i[:, 1, :], dst_t[:, :]).then_inc(s_in, 16)
                    sp.dma_start(xcur[:, :, :], x.rearrange("(p b) d -> p b d", p=P)).then_inc(s_in, 16)
                    for dst, vec in ((bias0, b0), (bias_lin, lin0_b), (bias_conv, conv_b),
                                     (bias_ih, bih), (bias_hh, bhh), (eps_sb, eps)):
                        sp.dma_start(dst[:, :], vec[None, :].to_broadcast([P, vec.shape[0]])).then_inc(s_in, 16)
                    sp.dma_start(w2[:, :, :].rearrange("k i o -> k (i o)"), en2[:, :]).then_inc(s_in, 16)
                    sp.dma_start(b2[:, :], en2_b.rearrange("(i o) -> i o", o=D)).then_inc(s_in, 16)
                    sp.wait_ge(s_zero, 5)
                    for j in range(4):
                        rows = slice(D * j, D * j + D)
                        for bd, w_in in ((bd_a, w0[0:D, :]), (bd_b, w0[D:2 * D, :]), (bd_lin, lin0)):
                            sp.dma_start(bd[rows, D * j:D * j + D], w_in).then_inc(s_bd, 16)
                        for bd, w_in in ((bd_ih, wih), (bd_hh, whh)):
                            sp.dma_start(bd[rows, 2 * D * j:2 * D * j + 2 * D], w_in[:, 0:2 * D]).then_inc(s_bd, 16)
                            sp.dma_start(bd[rows, 8 * D + D * j:8 * D + D * j + D], w_in[:, 2 * D:3 * D]).then_inc(s_bd, 16)
                    sp.wait_ge(s_rk, 1)
                    rt = rowtab.rearrange("(r p) (h e) -> p r h e", p=128, h=2)
                    sp.dma_start(rt[:, :, 0, :], drow[:, :, :]).then_inc(s_rt, 16)
                    sp.dma_start(rt[:, :, 1, :], fdst[:, :, :]).then_inc(s_rt, 16)
                    sp.wait_ge(s_zero, 6)
                    sp.dma_start(slots33[ZROW:ZROW + 1, :], zrow[0:1, 0:D + 1]).then_inc(s_done, 16)
                    sp.dma_start(slots32[ZROW:ZROW + 1, :], zrow[0:1, 0:D]).then_inc(s_done, 16)
                    sp.wait_ge(s_rt, 32)
                    sp.wait_ge(s_done, 32)
                    sp.wait_ge(s_bd, 16 * 28)

                @block.gpsimd
                def _(pool):
                    pool.memset(ident[:, :], 0.0).then_inc(s_pool, 1)
                    pool.memset(last_tile[:, :], 1.0).then_inc(s_pool, 1)
                    pool.memset(pool_tick[:, :], 0.0).then_inc(s_pool, 1)
                    pool.iota(iota_w[:, :], [[1, W]], base=0, channel_multiplier=0,
                              allow_small_or_imprecise_dtypes=True).then_inc(s_pool, 1)
                    pool.iota(nodeid[:, :], [[1, NC2]], base=0, channel_multiplier=NB,
                              allow_small_or_imprecise_dtypes=True).then_inc(s_pool, 1)
                    pool.wait_ge(s_pool, 5)
                    pool.affine_select(out=ident[:, :], in_=ident[:, :], compare_op=ALU.not_equal, fill=1.0,
                                       base=0, pattern=[[-1, 128]], channel_multiplier=1).then_inc(s_pool, 1)
                    pool.affine_select(out=last_tile[:, :], in_=last_tile[:, :], compare_op=ALU.is_ge, fill=0.0,
                                       base=-(SL - W), pattern=[[0, SL]], channel_multiplier=1).then_inc(s_pool, 1)
                    pool.wait_ge(s_pool, 7)

                @block.vector
                def _(dve):
                    link = Chain(dve, s_ch)
                    for t in (bd_a, bd_b, bd_lin, bd_ih, bd_hh):
                        dve.memset(t[:, :], 0.0).then_inc(s_zero, 1)
                    dve.memset(zrow[:, :], 0.0).then_inc(s_zero, 1)
                    dve.memset(ln_eps[:, :], EPS)
                    dve.memset(agg[:, :, :], 0.0)
                    dve.memset(first[:, :, 0:1], 0.0)
                    link(dve.memset(junk[:, :], 1.0))
                    dve.wait_ge(s_in, 16 * 12)
                    dve.tensor_tensor(w_t[:, :], tcol_i[:, 0, :], tcol_i[:, 1, :], ALU.not_equal)
                    link(dve.tensor_copy(drow[:, :, :], drow_i[:, :, :]))
                    link(dve.tensor_tensor(first[:, :, 1:EDGES], drow[:, :, 1:EDGES], drow[:, :, 0:EDGES - 1],
                                           ALU.not_equal))
                    for r in range(RB):
                        last = dve.tensor_tensor_scan(rank[:, r, :], junk[:, :], first[:, r, :], 0.0, ALU.mult, ALU.add)
                    link(last)
                    link(dve.tensor_scalar(fdst[:, :, :], drow[:, :, :], float(PAD_DST // 2), -5000.0,
                                           ALU.is_ge, ALU.mult))
                    dve.memset(first[:, :, 0:1], 1.0)
                    link(dve.tensor_tensor(rank[:, :, :], rank[:, :, :], fdst[:, :, :], ALU.add))
                    link(dve.scalar_tensor_tensor(fnode[:, :, :], drow[:, :, :], 1.0, first[:, :, :], ALU.add, ALU.mult))
                    link(dve.tensor_scalar(fdst[:, :, :], first[:, :, :], -float(PAD_DST + 1), float(PAD_DST),
                                           ALU.mult, ALU.add))
                    dve.tensor_tensor(fdst[:, :, :], fdst[:, :, :], fnode[:, :, :], ALU.add).then_inc(s_rk, 1)
                    for r in range(RB):
                        n = min(128, T - 128 * r)
                        dve.wait_ge(s_tr, r + 1)
                        last = dve.tensor_copy(rank_t[:, 128 * r:128 * r + n], ps[r % 8][:, 0:n])
                        last.then_inc(s_ev, 1)
                    dve.wait_ge(s_ev, RB)

                @block.tensor
                def _(pe):
                    pe.wait_ge(s_pool, 7)
                    pe.wait_ge(s_rk, 1)
                    for r in range(RB):
                        if r >= 8:
                            pe.wait_ge(s_ev, r - 7)
                        pe.transpose(ps[r % 8][:, 0:128], rank[:, r, :], ident[:, :]).then_inc(s_tr, 1)
            sub.close()

            tfirst = sbp("tfirst", [P, T])
            tfirst_i = sbp("tfirst_i", [P, T], i32)
            junk2 = sbp("junk2", [P, T])
            rows = sbp("rows", [P, 4, 2 * EDGES])
            junk3 = sbp("junk3", [P, 2, EDGES])
            rmax = sbp("rmax", [128, 1])
            rall = sbp("rall", [128, 1])
            thr = sbp("thr", [1, MAXP - 1])
            npf = sbp("npf", [1, 1])
            s_ch2, s_rm, s_ra, s_th = [sem(n) for n in ("dve_chain_2", "rank_max", "rank_max_all", "thresholds")]
            s_row = [sem(f"row_gathered{k}") for k in range(4)]
            with nc.Block() as block:
                @block.sync
                def _(sp):
                    sp.dma_start(tfirst_i[:, :], dst_t[0:1, :].to_broadcast([P, T])).then_inc(s_fb, 16)

                @block.gpsimd
                def _(pool):
                    pool.iota(thr[:, :], [[W, MAXP - 1]], base=W, channel_multiplier=0,
                              allow_small_or_imprecise_dtypes=True).then_inc(s_th, 1)
                    pool.wait_ge(s_rm, 1)
                    pool.partition_all_reduce(rall[:, :], rmax[:, :], 128, bass.bass_isa.ReduceOp.max).then_inc(s_ra, 1)
                    for c in range(NB + 1):
                        if c == 0:
                            pool.wait_ge(s_t1, 1)
                        if c >= 4:
                            pool.wait_ge(s_u1, c - 3)
                        pool.indirect_dma_start(out=rows[:, c % 4, :], out_offset=None, in_=rowtab[:, :],
                                                in_offset=bass.IndirectOffsetOnAxis(ap=idx1[:, c:c + 1], axis=0)
                                                ).then_inc(s_row[c % 4], 16)

                @block.vector
                def _(dve):
                    link = Chain(dve, s_ch2)
                    dve.tensor_reduce(rmax[:, :], rank[:, :, :], AX.XY, ALU.max).then_inc(s_rm, 1)
                    dve.memset(d1[:, :], 0.0)
                    dve.wait_ge(s_fb, 16)
                    link(dve.tensor_copy(tfirst[:, :], tfirst_i[:, :]))
                    for c in range(NB + 1):
                        last = dve.tensor_scalar(junk2[:, :], tfirst[:, :], nodeid[:, c:c + 1], 0.0, ALU.is_lt, ALU.add,
                                                 accum_out=t0n[:, c:c + 1])
                        link(last)
                    C = NB + 1
                    link(dve.tensor_scalar(t0n[:, 0:C], t0n[:, 0:C], -1.0, 0.0, ALU.add, ALU.max))
                    dve.tensor_copy(idx1[:, 0:C], t0n[:, 0:C]).then_inc(s_t1, 1)
                    for c in range(C):
                        dve.wait_ge(s_row[c % 4], 16 * (c // 4 + 1))
                        if c >= 1:
                            dve.wait_ge(s_u1, c)
                        link(dve.tensor_scalar(junk3[:, 0, :], rows[:, c % 4, 0:EDGES], nodeid[:, c:c + 1], 0.0,
                                               ALU.is_lt, ALU.add, accum_out=c1[:, c:c + 1]))
                        dve.tensor_scalar(junk3[:, 1, :], rows[:, c % 4, EDGES:2 * EDGES], nodeid[:, c:c + 1], 0.0,
                                          ALU.is_lt, ALU.add, accum_out=d1[:, c:c + 1]).then_inc(s_u1, 1)
                    dve.wait_ge(s_u1, C)
                    link(dve.scalar_tensor_tensor(rp[:, 0:C], t0n[:, 0:C], float(EDGES), c1[:, 0:C], ALU.mult, ALU.add))
                    link(dve.tensor_tensor(cnt[:, :], rp[:, 1:C], rp[:, 0:NB], ALU.subtract))
                    link(dve.tensor_scalar(f_a[:, :], c1[:, 0:NB], float(EDGES), None, ALU.is_equal))
                    link(dve.tensor_tensor(f_b[:, :], d1[:, 0:NB], f_a[:, :], ALU.mult))
                    dve.tensor_tensor(rr[:, :], d1[:, 0:NB], f_b[:, :], ALU.subtract)
                    link(dve.tensor_tensor(f_c[:, :], t0n[:, 0:NB], f_a[:, :], ALU.add))
                    dve.tensor_tensor(crosses[:, :], t0n[:, 1:C], f_c[:, :], ALU.is_gt)
                    link(dve.tensor_scalar(d1[:, 0:NB], f_c[:, :], float(W), -float(ZROW), ALU.mult, ALU.add))
                    link(dve.tensor_scalar(c1[:, 0:NB], t0n[:, 1:C], float(W), -float(ZROW), ALU.mult, ALU.add))
                    link(dve.tensor_scalar(t0n[:, 0:NB], cnt[:, :], 0.0, None, ALU.is_gt))
                    dve.wait_ge(s_ra, 1)
                    dve.wait_ge(s_th, 1)
                    link(dve.tensor_scalar(thr[:, :], thr[:, :], rall[0:1, 0:1], 0.0, ALU.is_le, ALU.add,
                                           accum_out=npf[:, :]))
                    link(dve.tensor_scalar(npass[:, :], npf[:, :], 1.0, None, ALU.add))
            nc.all_engine_barrier()
            passes = nc.values_load(npass[0:1, 0:1], min_val=1, max_val=MAXP)

            s_sn, s_fh, s_ch3, s_pp = [sem(n) for n in ("slot_nodes_ready", "homes_ready", "dve_chain_3", "pass_tables_written")]
            neg = sbp("neg", [1, SL])
            slots_sems = (s_sn, s_fh, s_ch3, s_pp)
            with nc.Fori(0, passes) as p:
                with nc.Block() as block:
                    @block.vector
                    def _(dve):
                        link = Chain(dve, s_ch3)
                        dve.memset(neg[:, :], -7.0).then_inc(s_sn, 1)
                        for r in range(RB):
                            for w in range(W):
                                last = dve.scalar_tensor_tensor(junk[:, :], rank[:, r, :], float(w), fnode[:, r, :],
                                                                ALU.is_equal, ALU.mult,
                                                                accum_out=slotn[:, r, w:w + 1])
                                link(last)
                        dve.memset(junk[:, 0:1], 0.0).then_inc(s_sn, 1)
                        link(dve.tensor_scalar(f_a[:, :], rr[:, :], 0.0, None, ALU.is_ge))
                        link(dve.tensor_scalar(f_b[:, :], rr[:, :], float(W), None, ALU.is_lt))
                        link(dve.tensor_tensor(f_a[:, :], f_a[:, :], f_b[:, :], ALU.mult))
                        link(dve.tensor_tensor(f_b[:, :], f_a[:, :], crosses[:, :], ALU.mult))
                        link(dve.tensor_tensor(f_a[:, :], f_a[:, :], f_b[:, :], ALU.subtract))
                        link(dve.tensor_tensor(f_b[:, :], d1[:, 0:NB], rr[:, :], ALU.add))
                        link(dve.tensor_tensor(f_a[:, :], f_a[:, :], f_b[:, :], ALU.mult))
                        link(dve.tensor_tensor(f_b[:, :], crosses[:, :], c1[:, 0:NB], ALU.mult))
                        link(dve.tensor_tensor(f_a[:, :], f_a[:, :], f_b[:, :], ALU.add))
                        link(dve.tensor_tensor(f_a[:, :], f_a[:, :], t0n[:, 0:NB], ALU.mult))
                        link(dve.tensor_scalar(f_a[:, :], f_a[:, :], float(ZROW), None, ALU.add))
                        dve.tensor_copy(fint[:, :], f_a[:, :]).then_inc(s_fh, 1)
                        dve.memset(crosses[:, :], 0.0)
                        link(dve.tensor_scalar(rr[:, :], rr[:, :], -float(W), None, ALU.add))
                        link(dve.tensor_scalar(rank[:, :, :], rank[:, :, :], -float(W), None, ALU.add))

                    @block.sync
                    def _(sp):
                        sp.wait_ge(s_sn, 2)
                        for r in range(RB):
                            n = min(128, T - 128 * r)
                            sp.dma_start(slotnode[bass.ds(p, 1), SL + 128 * r * W:SL + (128 * r + n) * W].rearrange(
                                "o (t w) -> (o t) w", w=W), slotn[0:n, r, :]).then_inc(s_pp, 16)
                        sp.dma_start(slotnode[bass.ds(p, 1), 0:SL], neg[:, :]).then_inc(s_pp, 16)
                        sp.wait_ge(s_fh, 1)
                        sp.dma_start(homes[bass.ds(p, 1), :, :].rearrange("o q b -> (o q) b"), fint[:, :]).then_inc(s_pp, 16)
                        sp.wait_ge(s_pp, 16 * (RB + 2))
                close(slots_sems)

        with ExitStack() as ph:
            eft = ph.enter_context(nc.sbuf_tensor("eft", [65, 2, 5 * 128], f32))
            en1_bd = ph.enter_context(nc.sbuf_tensor("en1_bd", [65, 256], f32))
            ehb = ph.enter_context(nc.sbuf_tensor("ehb", [128, 2, GT * KF], f32))
            s_w, s_z, s_mm, s_rl = [sem(n) for n in ("en1_in", "en1_zeroed", "hidden_in_psum", "hidden_ready")]
            s_ef = [sem(f"edge_features_in{b}") for b in range(2)]
            s_st = [sem(f"hidden_stored{b}") for b in range(2)]
            widths = (512, 512, 256)
            with nc.Block() as block:
                @block.sync
                def _(sp):
                    sp.wait_ge(s_z, 2)
                    for j in range(2):
                        sp.dma_start(en1_bd[D * j:D * j + D, KF * j:KF * j + KF], en1[:, :]).then_inc(s_w, 16)
                        sp.dma_start(en1_bd[64:65, KF * j:KF * j + KF], en1_b[None, :]).then_inc(s_w, 16)

                    def group(g, i, b, first):
                        if not first:
                            sp.wait_ge(s_mm, g - 1)
                        sp.dma_start(eft[0:64, b, :], ef_t[bass.ds(g, 1), :, :].rearrange("o q n -> (o q) n")
                                     ).then_inc(s_ef[b], 16)

                    for b in range(2):
                        group(b, 0, b, True)
                    with sp.Fori(1, G // 2) as i:
                        for b in range(2):
                            group(i * 2 + b, i, b, False)

                @block.tensor
                def _(pe):
                    def group(g, i, b, first):
                        pe.wait_ge(s_ef[b], (i + 1) * 16)
                        if not first:
                            pe.wait_ge(s_rl, g - 1)
                        for q in range(5):
                            last = pe.matmul(ps[3 * b + q // 2][:, 256 * (q % 2):256 * (q % 2) + 256],
                                             lhsT=eft[:, b, 128 * q:128 * q + 128], rhs=en1_bd[:, :],
                                             start=True, stop=True)
                        last.then_inc(s_mm, 1)

                    pe.wait_ge(s_w, 64)
                    for b in range(2):
                        group(b, 0, b, True)
                    with pe.Fori(1, G // 2) as i:
                        for b in range(2):
                            group(i * 2 + b, i, b, False)

                @block.vector
                def _(dve):
                    dve.memset(en1_bd[:, :], 0.0).then_inc(s_z, 1)
                    dve.memset(eft[64:65, :, :], 1.0).then_inc(s_z, 1)

                @block.scalar
                def _(act):
                    def group(g, i, b, first):
                        act.wait_ge(s_mm, g + 1)
                        if not first:
                            act.wait_ge(s_st[b], i * 16)
                        at = 0
                        for q, n in enumerate(widths):
                            last = act.activation(ehb[:, b, at:at + n], ps[3 * b + q][:, 0:n], ACT.Relu)
                            at += n
                        last.then_inc(s_rl, 1)
                        act.wait_ge(s_rl, g + 1)
                        act.dma_start(ehid[bass.ds(g, 1), :, :].rearrange("o q n -> (o q) n"), ehb[:, b, :]
                                      ).then_inc(s_st[b], 16)

                    for b in range(2):
                        group(b, 0, b, True)
                    with act.Fori(1, G // 2) as i:
                        for b in range(2):
                            group(i * 2 + b, i, b, False)
                    for b in range(2):
                        act.wait_ge(s_st[b], 16 * (G // 2))

        idxb = sb("idxb", [128, 2, GT], i32)
        xg = sb("xg", [128, 2, GT, D + 1])
        ehg = sb("ehg", [128, 2, GT * KF])
        nrow = sb("nrow", [SL, 2, SL])
        ncol = sb("ncol", [SL, 2, 2])
        rk = sb("rk", [128, 2, GT])
        onehot = sb("onehot", [128, 2, SL])
        same = sb("same", [SL, 2, SL])
        carry = sb("carry", [SL, 2, SL])
        xm = sb("xm", [128, 2, D * W])
        gb = sb("gb", [128, 2, D, SL])
        sxs = sb("sxs", [D + 1, 2, SL])
        cs = sb("cs", [SL, 2, D + 1])
        cp = sb("cp", [SL, 2, D + 1])
        e_idx = [sem(f"indices_in{b}") for b in range(2)]
        e_ld = [sem(f"group_in{b}") for b in range(2)]
        e_ga = [sem(f"sources_gathered{b}") for b in range(2)]
        e_st = [sem(f"slots_stored{b}") for b in range(2)]
        (e_rk, e_oh, e_mat, e_pay, e_xm, e_pt, e_s1, e_g, e_sx, e_s2, e_cs, e_ch, e_cp, e_cz, e_tk) = [sem(n) for n in (
            "ranks_copied", "onehot_ready", "slot_matrices_ready", "payload_ready", "spread_ready", "outer_in_psum",
            "tile_sums_done", "outer_evacuated", "slot_sums_evacuated", "group_in_psum", "group_evacuated",
            "chained_in_psum", "chained_ready", "chain_zeroed", "pool_ticked")]
        edge_sems = (*e_idx, *e_ld, *e_st, e_rk, e_oh, e_mat, e_pay, e_xm, e_pt, e_s1, e_g, e_sx, e_s2, e_cs,
                     e_ch, e_cp, e_cz, e_tk)

        def edge_phase(kind, p):
            DW = D + 1 if kind == 0 else D
            slots = slots33 if kind == 0 else slots32
            n_ld = 3 if kind in (1, 2) else 2

            def sweep(eng, step):
                for s in range(4):
                    step(s, s // 2, s % 2)
                with eng.Fori(2, G // 2) as i:
                    for b in range(2):
                        step(i * 2 + b, i, b)
                for s in range(G, G + 2):
                    step(s, s // 2, s % 2)

            def inside(g):
                return not isinstance(g, int) or 0 <= g < G

            with nc.Block() as block:
                @block.sync
                def _(sp):
                    def step(g, i, b):
                        if not inside(g):
                            return
                        wait(sp, e_ga[b], i * (16 * GT))
                        sp.dma_start(idxb[:, b, :], srcg[bass.ds(g, 1), :, :].rearrange("o q t -> (o q) t")
                                     ).then_inc(e_idx[b], 16)
                        wait(sp, e_mat, g - 1)
                        sp.dma_start(nrow[:, b, :], slotnode[bass.ds(p, 1), bass.ds(g * SL + SL, SL)].to_broadcast([SL, SL])
                                     ).then_inc(e_ld[b], 16)
                        sp.dma_start(ncol[:, b, :], slotnode[bass.ds(p, 1), bass.ds(g * SL, 2 * SL)].rearrange(
                            "o (c a) -> (o a) c", c=2),
                                     allow_slow_non_contiguous=True).then_inc(e_ld[b], 16)
                        if kind == 1:
                            wait(sp, e_s1, g - 1)
                            sp.dma_start(ehg[:, b, :], ehid[bass.ds(g, 1), :, :].rearrange("o q n -> (o q) n")
                                         ).then_inc(e_ld[b], 16)
                        if kind == 2:
                            wait(sp, e_pay, g - 1)
                            sp.dma_start(ehg[:, b, 0:GT * D], ef_e[bass.ds(g, 1), :, :].rearrange("o q n -> (o q) n")
                                         ).then_inc(e_ld[b], 16)
                    sweep(sp, step)

                @block.gpsimd
                def _(pool):
                    def step(g, i, b):
                        if not inside(g):
                            return
                        wait(pool, e_s1, g - 1)
                        wait(pool, e_idx[b], (i + 1) * 16)
                        wait(pool, e_tk, g - 1)
                        pool.tensor_tensor(pool_tick[0:1, b:b + 1], pool_tick[0:1, 2:3], pool_tick[0:1, 3:4], ALU.add
                                           ).then_inc(e_tk, 1)
                        for j in range(GT):
                            pool.indirect_dma_start(out=xg[:, b, j, 0:D], out_offset=None, in_=feat[:, :],
                                                    in_offset=bass.IndirectOffsetOnAxis(ap=idxb[:, b, j:j + 1], axis=0)
                                                    ).then_inc(e_ga[b], 16)
                    sweep(pool, step)
                    for b in range(2):
                        pool.wait_ge(e_ga[b], 16 * GT * (G // 2))

                @block.vector
                def _(dve):
                    dve.memset(cp[:, :, :], 0.0).then_inc(e_cz, 1)

                    def matrices(g, i, b):
                        wait(dve, e_ld[b], (i + 1) * (16 * n_ld))
                        wait(dve, e_ch, g - 1)
                        dve.tensor_scalar(same[:, b, :], nrow[:, b, :], ncol[:, b, 1:2], None, ALU.is_equal)
                        dve.scalar_tensor_tensor(carry[:, b, :], nrow[:, b, :], ncol[:, b, 0:1], last_tile[:, :],
                                                 ALU.is_equal, ALU.mult).then_inc(e_mat, 1)

                    def payload(g, i, b):
                        wait(dve, e_s1, g - 1)
                        dve.tensor_copy(rk[:, b, :], rank_t[:, bass.ds(g * GT, GT)]).then_inc(e_rk, 1)
                        wait(dve, e_rk, g + 1)
                        dve.tensor_tensor(onehot[:, b, :].rearrange("p (j w) -> p j w", w=W),
                                          rk[:, b, :, None].to_broadcast([128, GT, W]),
                                          iota_w[:, None, :].to_broadcast([128, GT, W]), ALU.is_equal).then_inc(e_oh, 1)
                        if kind == 0:
                            dve.tensor_copy(xg[:, b, :, D:D + 1].rearrange("p j o -> p (j o)"),
                                            w_t[:, bass.ds(g * GT, GT)]).then_inc(e_pay, 1)
                        wait(dve, e_ga[b], (i + 1) * (16 * GT))
                        if kind == 1:
                            for j in range(GT):
                                wait(dve, e_pt, g * GT + (j - 1))
                                dve.scalar_tensor_tensor(
                                    xm[:, j % 2, :].rearrange("p (i w) -> p i w", w=W),
                                    iota_w[:, None, :].to_broadcast([128, D, W]), rk[:, b, j:j + 1],
                                    xg[:, b, j, 0:D, None].to_broadcast([128, D, W]),
                                    ALU.is_equal, ALU.mult).then_inc(e_xm, 1)
                        if kind == 2:
                            wait(dve, e_ld[b], (i + 1) * (16 * n_ld))
                            dve.tensor_tensor(xg[:, b, :, 0:D], xg[:, b, :, 0:D],
                                              ehg[:, b, 0:GT * D].rearrange("p (j d) -> p j d", d=D), ALU.add
                                              ).then_inc(e_xm, 1)
                            wait(dve, e_xm, g + 1)
                            dve.tensor_scalar(xg[:, b, :, 0:D], xg[:, b, :, 0:D], 0.0, None, ALU.max).then_inc(e_pay, 1)
                        if kind == 3:
                            dve.tensor_tensor(xg[:, b, :, 0:D], xg[:, b, :, 0:D],
                                              w_t[:, bass.ds(g * GT, GT), None].to_broadcast([128, GT, D]), ALU.mult
                                              ).then_inc(e_pay, 1)

                    def step(s, i, b):
                        if inside(s):
                            payload(s, i, b)
                        if not isinstance(s, int) or inside(s - 1):
                            matrices(s - 1, i - 1 + b, 1 - b)
                    sweep(dve, step)

                @block.tensor
                def _(pe):
                    pe.wait_ge(e_cz, 1)

                    def tiles(g, i, b):
                        pe.wait_ge(e_oh, g + 1)
                        pe.wait_ge(e_ga[b], (i + 1) * (16 * GT))
                        if kind != 1:
                            pe.wait_ge(e_pay, g + 1)
                        wait(pe, e_sx, g - 1)
                        if kind == 1:
                            pe.wait_ge(e_ld[b], (i + 1) * (16 * n_ld))
                        for j in range(GT):
                            if kind == 1:
                                q = (GT * b + j) % 4
                                pe.wait_ge(e_xm, g * GT + (j + 1))
                                wait(pe, e_g, g * GT + (j - 3))
                                pe.matmul(ps[q][:, 0:D * W], lhsT=ehg[:, b, KF * j:KF * j + KF], rhs=xm[:, j % 2, :],
                                          start=True, stop=True).then_inc(e_pt, 1)
                            last = pe.matmul(ps[4 + b][0:DW, W * j:W * j + W], lhsT=xg[:, b, j, 0:DW],
                                             rhs=onehot[:, b, W * j:W * j + W], start=True, stop=True)
                        last.then_inc(e_s1, 1)

                    def combine(g, b):
                        pe.wait_ge(e_sx, g + 1)
                        wait(pe, e_cs, g)
                        out_c = ps[6][0:SL, 0:DW]
                        if kind == 1:
                            pe.wait_ge(e_g, g * GT + GT)
                            for k in range(D):
                                pe.matmul(out_c, lhsT=gb[:, b, k, :], rhs=w2[:, k, :], start=(k == 0), stop=False)
                            last = pe.matmul(out_c, lhsT=sxs[0:D, b, :], rhs=b2[:, :], start=False, stop=True)
                        else:
                            last = pe.matmul(out_c, lhsT=sxs[0:DW, b, :], rhs=ident[0:DW, 0:DW], start=True, stop=True)
                        last.then_inc(e_s2, 1)

                    def chain(g, b):
                        pe.wait_ge(e_cs, g + 1)
                        pe.wait_ge(e_mat, g + 1)
                        wait(pe, e_cp, g)
                        out_c = ps[7][0:SL, 0:DW]
                        pe.matmul(out_c, lhsT=same[:, b, :], rhs=cs[:, b, 0:DW], start=True, stop=False)
                        pe.matmul(out_c, lhsT=carry[:, b, :], rhs=cp[:, 1 - b, 0:DW], start=False, stop=True
                                  ).then_inc(e_ch, 1)

                    def step(s, i, b):
                        if inside(s):
                            tiles(s, i, b)
                        if inside(s - 1) if isinstance(s, int) else True:
                            combine(s - 1, 1 - b)
                        if inside(s - 2) if isinstance(s, int) else True:
                            chain(s - 2, b)
                    sweep(pe, step)

                @block.scalar
                def _(act):
                    act.wait_ge(e_cz, 1)

                    def step(s, i, b):
                        if inside(s):
                            if kind == 1:
                                wait(act, e_s2, s - 1)
                                for j in range(GT):
                                    act.wait_ge(e_pt, s * GT + (j + 1))
                                    act.activation(gb[:, b, :, W * j:W * j + W],
                                                   ps[(GT * b + j) % 4][:, 0:D * W].rearrange("p (i w) -> p i w", w=W),
                                                   ACT.Copy).then_inc(e_g, 1)
                            elif not isinstance(s, int) or s >= 2:
                                wait(act, e_s2, s - 1)
                            act.wait_ge(e_s1, s + 1)
                            act.activation(sxs[0:DW, b, :], ps[4 + b][0:DW, 0:SL], ACT.Copy).then_inc(e_sx, 1)
                        if not isinstance(s, int) or inside(s - 1):
                            g, c = s - 1, 1 - b
                            act.wait_ge(e_s2, g + 1)
                            wait(act, e_ch, g - 1)
                            act.activation(cs[:, c, 0:DW], ps[6][0:SL, 0:DW], ACT.Copy).then_inc(e_cs, 1)
                        if not isinstance(s, int) or inside(s - 2):
                            g = s - 2
                            act.wait_ge(e_ch, g + 1)
                            wait(act, e_st[b], (i - 1) * 16)
                            act.activation(cp[:, b, 0:DW], ps[7][0:SL, 0:DW], ACT.Copy).then_inc(e_cp, 1)
                            act.wait_ge(e_cp, g + 1)
                            act.dma_start(slots[bass.ds(g * SL, SL), :], cp[:, b, 0:DW]).then_inc(e_st[b], 16)
                    sweep(act, step)
                    for b in range(2):
                        act.wait_ge(e_st[b], 16 * (G // 2))
            close(edge_sems, e_ga)

        n_hm, n_ga, n_ad = [sem(n) for n in ("homes_in", "sums_gathered", "window_moved")]

        def bring_home(kind, p):
            DW = D + 1 if kind == 0 else D
            slots = slots33 if kind == 0 else slots32
            with nc.Block() as block:
                @block.sync
                def _(sp):
                    sp.dma_start(home[:, :], homes[bass.ds(p, 1), :, :].rearrange("o q b -> (o q) b")).then_inc(n_hm, 16)

                @block.gpsimd
                def _(pool):
                    pool.wait_ge(n_hm, 16)
                    for c in range(NB):
                        pool.indirect_dma_start(out=gat[:, c, 0:DW], out_offset=None, in_=slots[:, :],
                                                in_offset=bass.IndirectOffsetOnAxis(ap=home[:, c:c + 1], axis=0)
                                                ).then_inc(n_ga, 16)
                    pool.wait_ge(n_ga, 16 * NB)

                @block.vector
                def _(dve):
                    dve.tensor_scalar(iota_w[:, :], iota_w[:, :], float(W), None, ALU.add).then_inc(n_ad, 1)
                    dve.wait_ge(n_ga, 16 * NB)
                    dve.tensor_tensor(agg[:, :, 0:DW], agg[:, :, 0:DW], gat[:, :, 0:DW], ALU.add).then_inc(n_ad, 1)
                    dve.wait_ge(n_ad, 2)
            close((n_hm, n_ad), (n_ga,))

        m_ch, m_ac, m_ra, m_tr, m_tc, m_mm, m_mc, m_st, m_pw = [sem(n) for n in (
            "node_dve_chain", "node_act_done", "node_act_asked", "node_transposed", "node_transposed_copied",
            "node_products", "node_products_read", "features_stored", "window_reset")]
        node_sems = (m_ch, m_ac, m_ra, m_tr, m_tc, m_mm, m_mc, m_st, m_pw)
        tp = sb("tp", [128, 2, 2, P])
        QB = NB // 4
        Fl = "p b d -> p (b d)"

        def rows_of(t, q):
            return t[:, 4 * q:4 * q + 4, 0:D].rearrange(Fl) if t is not agg else t[:, 4 * q:4 * q + 4, 0:D]

        def products(block, operands, weights, n_cols, evac, ready):
            @block.tensor
            def _(pe):
                pe.wait_ge(m_ra, ready)
                for q in range(QB + 1):
                    if q < QB:
                        if q >= 2:
                            pe.wait_ge(m_tc, q - 1)
                        for k, t in enumerate(operands):
                            last = pe.transpose(ps[q % 2][:, 128 * k:128 * k + P], rows_of(t, q), ident[0:P, 0:P])
                        last.then_inc(m_tr, 1)
                    if q >= 1:
                        c = q - 1
                        pe.wait_ge(m_tc, c + 1)
                        if c >= 2:
                            pe.wait_ge(m_mc, c - 1)
                        for at, width, k, wt, first, stop in weights:
                            last = pe.matmul(ps[2 + c % 2][0:P, at:at + width], lhsT=tp[:, c % 2, k, :], rhs=wt,
                                             start=first, stop=stop)
                        last.then_inc(m_mm, 1)

            @block.scalar
            def _(act):
                for q in range(QB):
                    act.wait_ge(m_tr, q + 1)
                    if q >= 2:
                        act.wait_ge(m_mm, q - 1)
                    act.activation(tp[:, q % 2, 0:len(operands), :],
                                   ps[q % 2][:, 0:128 * len(operands)].rearrange("p (k n) -> p k n", n=128)[:, :, 0:P],
                                   ACT.Copy).then_inc(m_tc, 1)
                evac(act)

        def bcast_d(t):
            return t[:, :, None].to_broadcast([P, NB, D])

        def bcast_b(t):
            return t[:, None, :].to_broadcast([P, NB, D])

        def norm(dve, link, n_act):
            link(dve.tensor_reduce(mean[:, :], xcur[:, :, :], AX.X, ALU.add))
            link(dve.tensor_scalar(mean[:, :], mean[:, :], 1.0 / D, None, ALU.mult))
            link(dve.tensor_tensor(hcur[:, :, :], xcur[:, :, :], bcast_d(mean), ALU.subtract))
            link(dve.tensor_tensor(tmp[:, :, :], hcur[:, :, :], hcur[:, :, :], ALU.mult))
            dve.tensor_reduce(rstd[:, :], tmp[:, :, :], AX.X, ALU.add).then_inc(m_pw, 1)
            dve.wait_ge(m_ac, n_act)
            link(dve.reciprocal(rstd[:, :], rstd[:, :]))
            link(dve.tensor_tensor(hcur[:, :, :], hcur[:, :, :], bcast_d(rstd), ALU.mult))
            link(dve.tensor_scalar(hcur[:, :, :], hcur[:, :, :], 0.0, None, ALU.max))

        def root(act, n):
            act.wait_ge(m_pw, n)
            act.activation(rstd[:, :], rstd[:, :], ACT.Sqrt, bias=ln_eps[:, 0:1], scale=1.0 / D).then_inc(m_ac, 1)

        def store_features(sp, t, n):
            sp.wait_ge(m_st, n)
            sp.dma_start(feat.rearrange("(p b) d -> p b d", p=P), t[:, :, :]).then_inc(m_st, 16)
            sp.wait_ge(m_st, 16 + n)

        def reset_window(dve):
            return dve.tensor_scalar(iota_w[:, :], iota_w[:, :], iota_w[:, 0:1], None, ALU.subtract)

        with nc.Block() as block:
            @block.vector
            def _(dve):
                link = Chain(dve, m_ch)
                norm(dve, link, 1)
                dve.memset(mean[:, 0:1], 0.0).then_inc(m_st, 1)

            @block.scalar
            def _(act):
                root(act, 1)

            @block.sync
            def _(sp):
                store_features(sp, hcur, 1)
        close(node_sems)

        with nc.Fori(0, passes) as p:
            edge_phase(0, p)
            bring_home(0, p)

        iw0 = sb("iw0", [128, 1])
        with nc.Block() as block:
            @block.vector
            def _(dve):
                link = Chain(dve, m_ch)
                link(dve.tensor_copy(iw0[:, :], iota_w[:, 0:1]))
                link(dve.tensor_scalar(iota_w[:, :], iota_w[:, :], iw0[:, 0:1], None, ALU.subtract))
                link(dve.tensor_scalar(dis[:, :], agg[:, :, D:D + 1].rearrange(Fl), 1.0, None, ALU.add))
                link(dve.tensor_scalar(cnt[:, :], cnt[:, :], 1.0, None, ALU.max))
                link(dve.reciprocal(cnt[:, :], cnt[:, :]))
                link(dve.tensor_tensor(tmp[:, :, :], agg[:, :, 0:D], bcast_d(cnt), ALU.mult))
                dve.memset(agg[:, :, :], 0.0).then_inc(m_ra, 1)
                for q in range(QB):
                    dve.wait_ge(m_mm, q + 1)
                    dve.tensor_tensor(gat[:, 4 * q:4 * q + 4, 0:D],
                                      ps[2 + q % 2][0:P, 0:4 * D].rearrange("p (b d) -> p b d", d=D),
                                      bias0[:, None, :].to_broadcast([P, 4, D]), ALU.add).then_inc(m_mc, 1)
                dve.wait_ge(m_mc, QB)
                link(dve.scalar_tensor_tensor(xcur[:, :, :], gat[:, :, 0:D], 0.0, xcur[:, :, :], ALU.max, ALU.add))
                norm(dve, link, 2)
                dve.memset(mean[:, 0:1], 0.0).then_inc(m_st, 1)

            def scalars(act):
                act.wait_ge(m_ra, 1)
                act.activation(dis[:, :], dis[:, :], ACT.Sqrt).then_inc(m_ac, 1)
                root(act, 1)

            products(block, (hcur, tmp), ((0, 4 * D, 0, bd_a[:, :], True, False), (0, 4 * D, 1, bd_b[:, :], False, True)),
                     4 * D, scalars, 1)
        close(node_sems)

        with nc.Block() as block:
            @block.vector
            def _(dve):
                link = Chain(dve, m_ch)
                dve.reciprocal(dis[:, :], dis[:, :]).then_inc(m_ra, 1)
                for q in range(QB):
                    dve.wait_ge(m_mm, q + 1)
                    dve.tensor_tensor(tmp[:, 4 * q:4 * q + 4, :],
                                      ps[2 + q % 2][0:P, 0:4 * D].rearrange("p (b d) -> p b d", d=D),
                                      bias_lin[:, None, :].to_broadcast([P, 4, D]), ALU.add).then_inc(m_mc, 1)
                dve.wait_ge(m_mc, QB)
                dve.tensor_scalar(hcur[:, :, :], tmp[:, :, :], 0.0, None, ALU.max).then_inc(m_st, 1)

            @block.sync
            def _(sp):
                store_features(sp, hcur, 1)
            products(block, (hcur,), ((0, 4 * D, 0, bd_lin[:, :], True, True),), 4 * D, lambda act: None, 1)
        close(node_sems)

        gview = gb[0:P, :, :, :].rearrange("p a i s -> p (a i s)")
        RZ = gview[:, 0:NB * 2 * D].rearrange("p (b c d) -> p b c d", c=2, d=D)
        inn = gat
        hn = sb("hn", [P, NB, D])
        with nc.Fori(0, STEPS) as _step:
            with nc.Fori(0, passes) as p:
                edge_phase(1, p)
                bring_home(1, p)
            with nc.Block() as block:
                @block.vector
                def _(dve):
                    link = Chain(dve, m_ch)
                    link(dve.tensor_copy(iw0[:, :], iota_w[:, 0:1]))
                    link(dve.tensor_scalar(iota_w[:, :], iota_w[:, :], iw0[:, 0:1], None, ALU.subtract))
                    link(dve.tensor_tensor(tmp[:, :, :], agg[:, :, 0:D], bcast_b(bias_conv), ALU.add))
                    dve.memset(agg[:, :, :], 0.0)
                    dve.tensor_scalar(tmp[:, :, :], tmp[:, :, :], 0.0, None, ALU.max).then_inc(m_ra, 1)
                    for q in range(QB):
                        bank = ps[2 + q % 2]
                        bs = slice(4 * q, 4 * q + 4)
                        dve.wait_ge(m_mm, q + 1)
                        dve.tensor_tensor(RZ[:, bs, :, :].rearrange("p b c d -> p b (c d)"),
                                          bank[0:P, 0:8 * D].rearrange("p (b c) -> p b c", c=2 * D),
                                          bias_ih[:, None, 0:2 * D].to_broadcast([P, 4, 2 * D]), ALU.add)
                        dve.tensor_tensor(inn[:, bs, 0:D], bank[0:P, 8 * D:12 * D].rearrange("p (b d) -> p b d", d=D),
                                          bias_ih[:, None, 2 * D:3 * D].to_broadcast([P, 4, D]), ALU.add)
                        dve.tensor_tensor(hn[:, bs, :], bank[0:P, 12 * D:16 * D].rearrange("p (b d) -> p b d", d=D),
                                          bias_hh[:, None, 2 * D:3 * D].to_broadcast([P, 4, D]), ALU.add).then_inc(m_mc, 1)
                    dve.wait_ge(m_mc, QB)
                    dve.tensor_tensor(RZ.rearrange("p b c d -> p b (c d)"), RZ.rearrange("p b c d -> p b (c d)"),
                                      bias_hh[:, None, 0:2 * D].to_broadcast([P, NB, 2 * D]), ALU.add).then_inc(m_pw, 1)
                    dve.wait_ge(m_ac, 1)
                    link(dve.tensor_tensor(hn[:, :, :], RZ[:, :, 0, :], hn[:, :, :], ALU.mult))
                    dve.tensor_tensor(hn[:, :, :], hn[:, :, :], inn[:, :, 0:D], ALU.add).then_inc(m_pw, 1)
                    dve.wait_ge(m_ac, 2)
                    link(dve.tensor_tensor(tmp[:, :, :], hcur[:, :, :], hn[:, :, :], ALU.subtract))
                    link(dve.tensor_tensor(tmp[:, :, :], tmp[:, :, :], RZ[:, :, 1, :], ALU.mult))
                    dve.tensor_tensor(hcur[:, :, :], tmp[:, :, :], hn[:, :, :], ALU.add).then_inc(m_st, 1)

                @block.sync
                def _(sp):
                    store_features(sp, hcur, 1)

                def gate_functions(act):
                    act.wait_ge(m_pw, 1)
                    act.activation(gview[:, 0:NB * 2 * D], gview[:, 0:NB * 2 * D], ACT.Sigmoid).then_inc(m_ac, 1)
                    act.wait_ge(m_pw, 2)
                    act.activation(hn[:, :, :], hn[:, :, :], ACT.Tanh).then_inc(m_ac, 1)

                products(block, (tmp, hcur), (
                    (0, 8 * D, 0, bd_ih[:, 0:8 * D], True, False), (0, 8 * D, 1, bd_hh[:, 0:8 * D], False, True),
                    (8 * D, 4 * D, 0, bd_ih[:, 8 * D:12 * D], True, True),
                    (12 * D, 4 * D, 1, bd_hh[:, 8 * D:12 * D], True, True)), 16 * D, gate_functions, 1)
            close(node_sems)

        with nc.Block() as block:
            @block.vector
            def _(dve):
                link = Chain(dve, m_ch)
                link(dve.tensor_tensor(xcur[:, :, :], xcur[:, :, :], hcur[:, :, :], ALU.add))
                link(dve.tensor_scalar(eps_sb[:, :], eps_sb[:, :], 1.0, None, ALU.add))
                norm(dve, link, 1)
                dve.memset(mean[:, 0:1], 0.0).then_inc(m_st, 1)

            @block.scalar
            def _(act):
                root(act, 1)

            @block.sync
            def _(sp):
                store_features(sp, hcur, 1)
        close(node_sems)
        with nc.Fori(0, passes) as p:
            edge_phase(2, p)
            bring_home(2, p)

        with nc.Block() as block:
            @block.vector
            def _(dve):
                link = Chain(dve, m_ch)
                link(dve.tensor_copy(iw0[:, :], iota_w[:, 0:1]))
                link(dve.tensor_scalar(iota_w[:, :], iota_w[:, :], iw0[:, 0:1], None, ALU.subtract))
                link(dve.scalar_tensor_tensor(tmp[:, :, :], hcur[:, :, :], eps_sb[:, 0:1], agg[:, :, 0:D],
                                              ALU.mult, ALU.add))
                link(dve.tensor_tensor(xcur[:, :, :], xcur[:, :, :], tmp[:, :, :], ALU.add))
                link(dve.memset(agg[:, :, :], 0.0))
                norm(dve, link, 1)
                dve.tensor_tensor(hcur[:, :, :], hcur[:, :, :], bcast_d(dis), ALU.mult).then_inc(m_st, 1)

            @block.scalar
            def _(act):
                root(act, 1)

            @block.sync
            def _(sp):
                store_features(sp, hcur, 1)
        close(node_sems)
        with nc.Fori(0, passes) as p:
            edge_phase(3, p)
            bring_home(3, p)

        with nc.Block() as block:
            @block.vector
            def _(dve):
                link = Chain(dve, m_ch)
                link(dve.tensor_tensor(tmp[:, :, :], agg[:, :, 0:D], hcur[:, :, :], ALU.add))
                link(dve.tensor_tensor(tmp[:, :, :], tmp[:, :, :], bcast_d(dis), ALU.mult))
                dve.tensor_tensor(xcur[:, :, :], xcur[:, :, :], tmp[:, :, :], ALU.add).then_inc(m_st, 1)

            @block.sync
            def _(sp):
                sp.wait_ge(m_st, 1)
                sp.dma_start(out.rearrange("(p b) d -> p b d", p=P), xcur[:, :, :]).then_inc(m_st, 16)
                sp.wait_ge(m_st, 17)


def kernel(x, src, dst, edge_attr_32, L0_gnn_W, L0_gnn_b, L1_gnn_lin0_w, L1_gnn_lin0_b, L1_gnn_en1_w, L1_gnn_en1_b,
           L1_gnn_en2_w, L1_gnn_en2_b, L1_gnn_conv_bias, L1_gnn_gru_wih, L1_gnn_gru_whh, L1_gnn_gru_bih,
           L1_gnn_gru_bhh, L2_gnn_eps):
    import numpy as np
    import concourse.bacc as bacc
    from concourse.bass_utils import run_bass_kernel_spmd

    src, dst, ef = np.asarray(src), np.asarray(dst), np.asarray(edge_attr_32)
    src_p = np.zeros((T, EDGES), np.int32)
    src_p.reshape(-1)[:E] = src
    dst_p = np.full((RB * 128, EDGES), PAD_DST, np.int32)
    dst_p.reshape(-1)[:E] = dst
    ef_p = np.zeros((T * EDGES, D), np.float32)
    ef_p[:E] = ef
    ef_p = ef_p.reshape(G, GT, EDGES, D)
    ins = [
        ("x", x), ("srcg", src_p.reshape(G, GT, EDGES).transpose(0, 2, 1)), ("src_t", src_p.T), ("dst_t", dst_p[:T].T),
        ("dst_rows", dst_p),
        ("ef_e", ef_p.transpose(0, 2, 1, 3).reshape(G, EDGES, GT * D)),
        ("ef_t", ef_p.reshape(G, GT // 2, 2, EDGES, D).transpose(0, 2, 4, 1, 3).reshape(G, 2 * D, GT // 2 * EDGES)),
        ("w0", L0_gnn_W), ("b0", L0_gnn_b), ("lin0", np.asarray(L1_gnn_lin0_w).T), ("lin0_b", L1_gnn_lin0_b),
        ("en1", np.asarray(L1_gnn_en1_w).T), ("en1_b", L1_gnn_en1_b), ("en2", np.asarray(L1_gnn_en2_w).T),
        ("en2_b", L1_gnn_en2_b), ("conv_b", L1_gnn_conv_bias), ("wih", np.asarray(L1_gnn_gru_wih).T),
        ("whh", np.asarray(L1_gnn_gru_whh).T), ("bih", L1_gnn_gru_bih), ("bhh", L1_gnn_gru_bhh), ("eps", L2_gnn_eps),
    ]
    nc = bacc.Bacc("TRN2", target_bir_lowering=False, num_devices=1)
    arrays, args = {}, []
    for name, a in ins:
        a = np.ascontiguousarray(a)
        arrays[f"in_{name}"] = a
        args.append(nc.dram_tensor(f"in_{name}", a.shape, mybir.dt.from_np(a.dtype), kind="ExternalInput").ap())
    args.append(nc.dram_tensor("out_0", (N, D), mybir.dt.float32, kind="ExternalOutput").ap())
    bass_gnn(nc, *args)
    return run_bass_kernel_spmd(nc, [arrays], core_ids=[0]).results[0]["out_0"]
```

```python
import concourse.bass as bass
from concourse import mybir
from contextlib import ExitStack

N, E, D, KF, STEPS = 12500, 200000, 32, 128, 6
EDGES = 128
W = 12
GT = 10
SL = W * GT
T_REAL = -(-E // EDGES)
G = -(-T_REAL // GT)
G += G % 2
T = G * GT
RB = -(-T // 128)
MAXP = -(-EDGES // W)
P = 125
NB = N // P
NC2 = NB + 2
ZROW = G * SL
PAD_DST = 1 << 20
EPS = 1e-5


def bass_gnn(nc, x, srcg, src_t, dst_t, dst_rows, ef_e, ef_t, w0, b0, lin0, lin0_b, en1, en1_b,
             en2, en2_b, conv_b, wih, whh, bih, bhh, eps, out):
    f32, i32 = mybir.dt.float32, mybir.dt.int32
    ALU, ACT, AX = mybir.AluOpType, mybir.ActivationFunctionType, mybir.AxisListType
    with ExitStack() as ctx:
        def sb(name, shape, dt=f32):
            return ctx.enter_context(nc.sbuf_tensor(name, shape, dt))

        def sem(name):
            return ctx.enter_context(nc.semaphore(name))

        def dram(name, shape, dt=f32):
            return nc.dram_tensor(name, shape, dt, kind="Internal").ap()

        feat = dram("feat", (N, D))
        slots33 = dram("slots33", (ZROW + 1, D + 1))
        slots32 = dram("slots32", (ZROW + 1, D))
        ehid = dram("ehid", (G, 128, GT * KF))
        rowtab = dram("rowtab", (RB * 128, 2 * EDGES))
        slotnode = dram("slotnode", (MAXP, (G + 1) * SL))
        homes = dram("homes", (MAXP, P, NB), i32)

        ident = sb("ident", [128, 128])
        iota_w = sb("iota_w", [128, W])
        rank_t = sb("rank_t", [128, T])
        w_t = sb("w_t", [128, T])
        xcur = sb("xcur", [P, NB, D])
        hcur = sb("hcur", [P, NB, D])
        agg = sb("agg", [P, NB, D + 1])
        gat = sb("gat", [P, NB, D + 1])
        tmp = sb("tmp", [P, NB, D])
        home = sb("home", [P, NB], i32)
        cnt = sb("cnt", [P, NB])
        dis = sb("dis", [P, NB])
        mean = sb("mean", [P, NB])
        rstd = sb("rstd", [P, NB])
        eps_sb = sb("eps_sb", [P, 1])
        ln_eps = sb("ln_eps", [P, 1])
        w2 = sb("w2", [128, D, D])
        b2x4 = sb("b2x4", [4 * D, D])
        last_tile = sb("last_tile", [SL, SL])
        npass = sb("npass", [1, 1], i32)
        pool_tick = sb("pool_tick", [1, 4])
        zrow = sb("zrow", [1, 256])
        bd_a = sb("bd_a", [128, 4 * D])
        bd_b = sb("bd_b", [128, 4 * D])
        bd_lin = sb("bd_lin", [128, 4 * D])
        bd_ih = sb("bd_ih", [128, 4 * 3 * D])
        bd_hh = sb("bd_hh", [128, 4 * 3 * D])
        bias0 = sb("bias0", [P, D])
        bias_lin = sb("bias_lin", [P, D])
        bias_conv = sb("bias_conv", [P, D])
        bias_ih = sb("bias_ih", [P, 3 * D])
        bias_hh = sb("bias_hh", [P, 3 * D])

        ps = [ctx.enter_context(nc.psum_tensor(f"bank{k}", [128, 512], f32)) for k in range(8)]

        def wait(eng, s, v):
            if not isinstance(v, int) or v > 0:
                eng.wait_ge(s, v)

        def close(sems, gathers=()):
            for s in gathers:
                nc.gpsimd.dma_reset(range(s.num, s.num + 1))
                nc.gpsimd.sem_clear(s)
            for s in sems:
                nc.gpsimd.sem_clear(s)
            nc.all_engine_barrier()

        class Chain:

            def __init__(self, eng, s):
                self.eng, self.s, self.n = eng, s, 0

            def __call__(self, ins):
                ins.then_inc(self.s, 1)
                self.n += 1
                self.eng.wait_ge(self.s, self.n)

        with ExitStack() as ph:
            def sbp(name, shape, dt=f32):
                return ph.enter_context(nc.sbuf_tensor(name, shape, dt))

            drow_i = sbp("drow_i", [128, RB, EDGES], i32)
            fnode = sbp("fnode", [128, RB, EDGES])
            rank = sbp("rank", [128, RB, EDGES])
            slotn = sbp("slotn", [128, RB, W])
            junk = sbp("junk", [128, EDGES])
            t0n = sbp("t0n", [P, NC2])
            c1 = sbp("c1", [P, NC2])
            d1 = sbp("d1", [P, NC2])
            idx1 = sbp("idx1", [P, NC2], i32)
            nodeid = sbp("nodeid", [P, NC2])
            rp = sbp("rp", [P, NC2])
            rr = sbp("rr", [P, NB])
            crosses = sbp("crosses", [P, NB])
            f_a = sbp("f_a", [P, NB])
            f_b = sbp("f_b", [P, NB])
            f_c = sbp("f_c", [P, NB])
            fint = sbp("fint", [P, NB], i32)

            s_in, s_zero, s_pool, s_ch, s_rk, s_tr, s_rt, s_done = [
                sem(n) for n in ("inputs_in", "zeroed", "pool_made", "dve_chain", "ranks_ready",
                                 "rank_transposed", "row_table_written", "setup_stored")]
            s_fb, s_t1, s_g1, s_u1, s_ev = [sem(n) for n in (
                "firsts_in", "tile_of_node", "tile_row_in", "tile_row_used", "rank_evacuated")]
            s_bd = sem("diagonals_in")
            sub = ExitStack()
            drow = sub.enter_context(nc.sbuf_tensor("drow", [128, RB, EDGES], f32))
            first = sub.enter_context(nc.sbuf_tensor("first", [128, RB, EDGES], f32))
            fdst = sub.enter_context(nc.sbuf_tensor("fdst", [128, RB, EDGES], f32))
            tcol_i = sub.enter_context(nc.sbuf_tensor("tcol_i", [128, 2, T], i32))
            with nc.Block() as block:
                @block.sync
                def _(sp):
                    sp.dma_start(drow_i[:, :, :], dst_rows.rearrange("(r p) e -> p r e", p=128)).then_inc(s_in, 16)
                    sp.dma_start(tcol_i[:, 0, :], src_t[:, :]).then_inc(s_in, 16)
                    sp.dma_start(tcol_i[:, 1, :], dst_t[:, :]).then_inc(s_in, 16)
                    sp.dma_start(xcur[:, :, :], x.rearrange("(p b) d -> p b d", p=P)).then_inc(s_in, 16)
                    for dst, vec in ((bias0, b0), (bias_lin, lin0_b), (bias_conv, conv_b),
                                     (bias_ih, bih), (bias_hh, bhh), (eps_sb, eps)):
                        sp.dma_start(dst[:, :], vec[None, :].to_broadcast([P, vec.shape[0]])).then_inc(s_in, 16)
                    sp.dma_start(w2[:, :, :].rearrange("k i o -> k (i o)"), en2[:, :]).then_inc(s_in, 16)
                    for c in range(4):
                        sp.dma_start(b2x4[D * c:D * c + D, :], en2_b.rearrange("(i o) -> i o", o=D)).then_inc(s_in, 16)
                    sp.wait_ge(s_zero, 5)
                    for j in range(4):
                        rows = slice(D * j, D * j + D)
                        for bd, w_in in ((bd_a, w0[0:D, :]), (bd_b, w0[D:2 * D, :]), (bd_lin, lin0)):
                            sp.dma_start(bd[rows, D * j:D * j + D], w_in).then_inc(s_bd, 16)
                        for bd, w_in in ((bd_ih, wih), (bd_hh, whh)):
                            sp.dma_start(bd[rows, 2 * D * j:2 * D * j + 2 * D], w_in[:, 0:2 * D]).then_inc(s_bd, 16)
                            sp.dma_start(bd[rows, 8 * D + D * j:8 * D + D * j + D], w_in[:, 2 * D:3 * D]).then_inc(s_bd, 16)
                    sp.wait_ge(s_rk, 1)
                    rt = rowtab.rearrange("(r p) (h e) -> p r h e", p=128, h=2)
                    sp.dma_start(rt[:, :, 0, :], drow[:, :, :]).then_inc(s_rt, 16)
                    sp.dma_start(rt[:, :, 1, :], fdst[:, :, :]).then_inc(s_rt, 16)
                    sp.wait_ge(s_zero, 6)
                    sp.dma_start(slots33[ZROW:ZROW + 1, :], zrow[0:1, 0:D + 1]).then_inc(s_done, 16)
                    sp.dma_start(slots32[ZROW:ZROW + 1, :], zrow[0:1, 0:D]).then_inc(s_done, 16)
                    sp.wait_ge(s_rt, 32)
                    sp.wait_ge(s_done, 32)
                    sp.wait_ge(s_bd, 16 * 28)

                @block.gpsimd
                def _(pool):
                    pool.memset(ident[:, :], 0.0).then_inc(s_pool, 1)
                    pool.memset(last_tile[:, :], 1.0).then_inc(s_pool, 1)
                    pool.memset(pool_tick[:, :], 0.0).then_inc(s_pool, 1)
                    pool.iota(iota_w[:, :], [[1, W]], base=0, channel_multiplier=0,
                              allow_small_or_imprecise_dtypes=True).then_inc(s_pool, 1)
                    pool.iota(nodeid[:, :], [[1, NC2]], base=0, channel_multiplier=NB,
                              allow_small_or_imprecise_dtypes=True).then_inc(s_pool, 1)
                    pool.wait_ge(s_pool, 5)
                    pool.affine_select(out=ident[:, :], in_=ident[:, :], compare_op=ALU.not_equal, fill=1.0,
                                       base=0, pattern=[[-1, 128]], channel_multiplier=1).then_inc(s_pool, 1)
                    pool.affine_select(out=last_tile[:, :], in_=last_tile[:, :], compare_op=ALU.is_ge, fill=0.0,
                                       base=-(SL - W), pattern=[[0, SL]], channel_multiplier=1).then_inc(s_pool, 1)
                    pool.wait_ge(s_pool, 7)

                @block.vector
                def _(dve):
                    link = Chain(dve, s_ch)
                    for t in (bd_a, bd_b, bd_lin, bd_ih, bd_hh):
                        dve.memset(t[:, :], 0.0).then_inc(s_zero, 1)
                    dve.memset(zrow[:, :], 0.0).then_inc(s_zero, 1)
                    dve.memset(ln_eps[:, :], EPS)
                    dve.memset(agg[:, :, :], 0.0)
                    dve.memset(first[:, :, 0:1], 0.0)
                    link(dve.memset(junk[:, :], 1.0))
                    dve.wait_ge(s_in, 16 * 15)
                    dve.tensor_tensor(w_t[:, :], tcol_i[:, 0, :], tcol_i[:, 1, :], ALU.not_equal)
                    link(dve.tensor_copy(drow[:, :, :], drow_i[:, :, :]))
                    link(dve.tensor_tensor(first[:, :, 1:EDGES], drow[:, :, 1:EDGES], drow[:, :, 0:EDGES - 1],
                                           ALU.not_equal))
                    for r in range(RB):
                        last = dve.tensor_tensor_scan(rank[:, r, :], junk[:, :], first[:, r, :], 0.0, ALU.mult, ALU.add)
                    link(last)
                    link(dve.tensor_scalar(fdst[:, :, :], drow[:, :, :], float(PAD_DST // 2), -5000.0,
                                           ALU.is_ge, ALU.mult))
                    dve.memset(first[:, :, 0:1], 1.0)
                    link(dve.tensor_tensor(rank[:, :, :], rank[:, :, :], fdst[:, :, :], ALU.add))
                    link(dve.scalar_tensor_tensor(fnode[:, :, :], drow[:, :, :], 1.0, first[:, :, :], ALU.add, ALU.mult))
                    link(dve.tensor_scalar(fdst[:, :, :], first[:, :, :], -float(PAD_DST + 1), float(PAD_DST),
                                           ALU.mult, ALU.add))
                    dve.tensor_tensor(fdst[:, :, :], fdst[:, :, :], fnode[:, :, :], ALU.add).then_inc(s_rk, 1)
                    for r in range(RB):
                        n = min(128, T - 128 * r)
                        dve.wait_ge(s_tr, r + 1)
                        last = dve.tensor_copy(rank_t[:, 128 * r:128 * r + n], ps[r % 8][:, 0:n])
                        last.then_inc(s_ev, 1)
                    dve.wait_ge(s_ev, RB)

                @block.tensor
                def _(pe):
                    pe.wait_ge(s_pool, 7)
                    pe.wait_ge(s_rk, 1)
                    for r in range(RB):
                        if r >= 8:
                            pe.wait_ge(s_ev, r - 7)
                        pe.transpose(ps[r % 8][:, 0:128], rank[:, r, :], ident[:, :]).then_inc(s_tr, 1)
            sub.close()

            tfirst = sbp("tfirst", [P, T])
            tfirst_i = sbp("tfirst_i", [P, T], i32)
            junk2 = sbp("junk2", [P, T])
            rows = sbp("rows", [P, 4, 2 * EDGES])
            junk3 = sbp("junk3", [P, 2, EDGES])
            rmax = sbp("rmax", [128, 1])
            rall = sbp("rall", [128, 1])
            thr = sbp("thr", [1, MAXP - 1])
            npf = sbp("npf", [1, 1])
            s_ch2, s_rm, s_ra, s_th = [sem(n) for n in ("dve_chain_2", "rank_max", "rank_max_all", "thresholds")]
            s_row = [sem(f"row_gathered{k}") for k in range(4)]
            with nc.Block() as block:
                @block.sync
                def _(sp):
                    sp.dma_start(tfirst_i[:, :], dst_t[0:1, :].to_broadcast([P, T])).then_inc(s_fb, 16)

                @block.gpsimd
                def _(pool):
                    pool.iota(thr[:, :], [[W, MAXP - 1]], base=W, channel_multiplier=0,
                              allow_small_or_imprecise_dtypes=True).then_inc(s_th, 1)
                    pool.wait_ge(s_rm, 1)
                    pool.partition_all_reduce(rall[:, :], rmax[:, :], 128, bass.bass_isa.ReduceOp.max).then_inc(s_ra, 1)
                    for c in range(NB + 1):
                        if c == 0:
                            pool.wait_ge(s_t1, 1)
                        if c >= 4:
                            pool.wait_ge(s_u1, c - 3)
                        pool.indirect_dma_start(out=rows[:, c % 4, :], out_offset=None, in_=rowtab[:, :],
                                                in_offset=bass.IndirectOffsetOnAxis(ap=idx1[:, c:c + 1], axis=0)
                                                ).then_inc(s_row[c % 4], 16)

                @block.vector
                def _(dve):
                    link = Chain(dve, s_ch2)
                    dve.tensor_reduce(rmax[:, :], rank[:, :, :], AX.XY, ALU.max).then_inc(s_rm, 1)
                    dve.memset(d1[:, :], 0.0)
                    dve.wait_ge(s_fb, 16)
                    link(dve.tensor_copy(tfirst[:, :], tfirst_i[:, :]))
                    for c in range(NB + 1):
                        last = dve.tensor_scalar(junk2[:, :], tfirst[:, :], nodeid[:, c:c + 1], 0.0, ALU.is_lt, ALU.add,
                                                 accum_out=t0n[:, c:c + 1])
                        link(last)
                    C = NB + 1
                    link(dve.tensor_scalar(t0n[:, 0:C], t0n[:, 0:C], -1.0, 0.0, ALU.add, ALU.max))
                    dve.tensor_copy(idx1[:, 0:C], t0n[:, 0:C]).then_inc(s_t1, 1)
                    for c in range(C):
                        dve.wait_ge(s_row[c % 4], 16 * (c // 4 + 1))
                        if c >= 1:
                            dve.wait_ge(s_u1, c)
                        link(dve.tensor_scalar(junk3[:, 0, :], rows[:, c % 4, 0:EDGES], nodeid[:, c:c + 1], 0.0,
                                               ALU.is_lt, ALU.add, accum_out=c1[:, c:c + 1]))
                        dve.tensor_scalar(junk3[:, 1, :], rows[:, c % 4, EDGES:2 * EDGES], nodeid[:, c:c + 1], 0.0,
                                          ALU.is_lt, ALU.add, accum_out=d1[:, c:c + 1]).then_inc(s_u1, 1)
                    dve.wait_ge(s_u1, C)
                    link(dve.scalar_tensor_tensor(rp[:, 0:C], t0n[:, 0:C], float(EDGES), c1[:, 0:C], ALU.mult, ALU.add))
                    link(dve.tensor_tensor(cnt[:, :], rp[:, 1:C], rp[:, 0:NB], ALU.subtract))
                    link(dve.tensor_scalar(f_a[:, :], c1[:, 0:NB], float(EDGES), None, ALU.is_equal))
                    link(dve.tensor_tensor(f_b[:, :], d1[:, 0:NB], f_a[:, :], ALU.mult))
                    dve.tensor_tensor(rr[:, :], d1[:, 0:NB], f_b[:, :], ALU.subtract)
                    link(dve.tensor_tensor(f_c[:, :], t0n[:, 0:NB], f_a[:, :], ALU.add))
                    dve.tensor_tensor(crosses[:, :], t0n[:, 1:C], f_c[:, :], ALU.is_gt)
                    link(dve.tensor_scalar(d1[:, 0:NB], f_c[:, :], float(W), -float(ZROW), ALU.mult, ALU.add))
                    link(dve.tensor_scalar(c1[:, 0:NB], t0n[:, 1:C], float(W), -float(ZROW), ALU.mult, ALU.add))
                    link(dve.tensor_scalar(t0n[:, 0:NB], cnt[:, :], 0.0, None, ALU.is_gt))
                    dve.wait_ge(s_ra, 1)
                    dve.wait_ge(s_th, 1)
                    link(dve.tensor_scalar(thr[:, :], thr[:, :], rall[0:1, 0:1], 0.0, ALU.is_le, ALU.add,
                                           accum_out=npf[:, :]))
                    link(dve.tensor_scalar(npass[:, :], npf[:, :], 1.0, None, ALU.add))
            nc.all_engine_barrier()
            passes = nc.values_load(npass[0:1, 0:1], min_val=1, max_val=MAXP)

            s_sn, s_fh, s_ch3, s_pp = [sem(n) for n in ("slot_nodes_ready", "homes_ready", "dve_chain_3", "pass_tables_written")]
            neg = sbp("neg", [1, SL])
            slots_sems = (s_sn, s_fh, s_ch3, s_pp)
            with nc.Fori(0, passes) as p:
                with nc.Block() as block:
                    @block.vector
                    def _(dve):
                        link = Chain(dve, s_ch3)
                        dve.memset(neg[:, :], -7.0).then_inc(s_sn, 1)
                        for r in range(RB):
                            for w in range(W):
                                last = dve.scalar_tensor_tensor(junk[:, :], rank[:, r, :], float(w), fnode[:, r, :],
                                                                ALU.is_equal, ALU.mult,
                                                                accum_out=slotn[:, r, w:w + 1])
                                link(last)
                        dve.memset(junk[:, 0:1], 0.0).then_inc(s_sn, 1)
                        link(dve.tensor_scalar(f_a[:, :], rr[:, :], 0.0, None, ALU.is_ge))
                        link(dve.tensor_scalar(f_b[:, :], rr[:, :], float(W), None, ALU.is_lt))
                        link(dve.tensor_tensor(f_a[:, :], f_a[:, :], f_b[:, :], ALU.mult))
                        link(dve.tensor_tensor(f_b[:, :], f_a[:, :], crosses[:, :], ALU.mult))
                        link(dve.tensor_tensor(f_a[:, :], f_a[:, :], f_b[:, :], ALU.subtract))
                        link(dve.tensor_tensor(f_b[:, :], d1[:, 0:NB], rr[:, :], ALU.add))
                        link(dve.tensor_tensor(f_a[:, :], f_a[:, :], f_b[:, :], ALU.mult))
                        link(dve.tensor_tensor(f_b[:, :], crosses[:, :], c1[:, 0:NB], ALU.mult))
                        link(dve.tensor_tensor(f_a[:, :], f_a[:, :], f_b[:, :], ALU.add))
                        link(dve.tensor_tensor(f_a[:, :], f_a[:, :], t0n[:, 0:NB], ALU.mult))
                        link(dve.tensor_scalar(f_a[:, :], f_a[:, :], float(ZROW), None, ALU.add))
                        dve.tensor_copy(fint[:, :], f_a[:, :]).then_inc(s_fh, 1)
                        dve.memset(crosses[:, :], 0.0)
                        link(dve.tensor_scalar(rr[:, :], rr[:, :], -float(W), None, ALU.add))
                        link(dve.tensor_scalar(rank[:, :, :], rank[:, :, :], -float(W), None, ALU.add))

                    @block.sync
                    def _(sp):
                        sp.wait_ge(s_sn, 2)
                        for r in range(RB):
                            n = min(128, T - 128 * r)
                            sp.dma_start(slotnode[bass.ds(p, 1), SL + 128 * r * W:SL + (128 * r + n) * W].rearrange(
                                "o (t w) -> (o t) w", w=W), slotn[0:n, r, :]).then_inc(s_pp, 16)
                        sp.dma_start(slotnode[bass.ds(p, 1), 0:SL], neg[:, :]).then_inc(s_pp, 16)
                        sp.wait_ge(s_fh, 1)
                        sp.dma_start(homes[bass.ds(p, 1), :, :].rearrange("o q b -> (o q) b"), fint[:, :]).then_inc(s_pp, 16)
                        sp.wait_ge(s_pp, 16 * (RB + 2))
                close(slots_sems)

        idxb = sb("idxb", [128, 4, GT], i32)
        xg = sb("xg", [128, 4, GT, D])
        wcol = sb("wcol", [128, 2, GT])
        eft = sb("eft", [2 * D + 1, 2, GT // 2 * EDGES])
        en1_bd = sb("en1_bd", [2 * D + 1, 2 * KF])
        ehg = sb("ehg", [128, 2, GT * KF])
        nrow = sb("nrow", [SL, 2, SL])
        ncol = sb("ncol", [SL, 2, 2])
        rk = sb("rk", [128, 2, GT])
        onehot = sb("onehot", [128, 2, SL])
        same = sb("same", [SL, 2, SL])
        carry = sb("carry", [SL, 2, SL])
        xm = sb("xm", [128, 4, D * W])
        gb = sb("gb", [128, 2, D, SL])
        sxs = sb("sxs", [D + 1, 2, SL])
        ct = sb("ct", [4 * D, 2, SL])
        ident4 = sb("ident4", [4 * D, D])
        sx4 = sb("sx4", [4 * D, 2, SL])
        cs = sb("cs", [SL, 2, D + 1])
        cp = sb("cp", [SL, 2, D + 1])
        e_idx = [sem(f"indices_in{r}") for r in range(4)]
        e_ld = [sem(f"group_in{b}") for b in range(2)]
        e_ga = [sem(f"sources_gathered{r}") for r in range(4)]
        e_ef = [sem(f"edge_features_in{b}") for b in range(2)]
        e_hs = [sem(f"hidden_stored{b}") for b in range(2)]
        e_nc = [sem(f"slot_nodes_in{b}") for b in range(2)]
        e_st = [sem(f"slots_stored{b}") for b in range(2)]
        (e_rk, e_oh, e_mat, e_pay, e_xm, e_pt, e_s1, e_g, e_sx, e_s2, e_cs, e_ch, e_cp, e_cz, e_tk, e_hp, e_hr, e_w1, e_cq, e_ct) = [sem(n) for n in (
            "ranks_copied", "onehot_ready", "slot_matrices_ready", "payload_ready", "spread_ready", "outer_in_psum",
            "tile_sums_done", "outer_evacuated", "slot_sums_evacuated", "group_in_psum", "group_evacuated",
            "chained_in_psum", "chained_ready", "chain_zeroed", "pool_ticked",
            "hidden_in_psum", "hidden_ready", "en1_in", "transposed_in_psum", "transposed_evacuated")]
        edge_sems = (*e_idx, *e_ld, *e_ef, *e_hs, *e_nc, e_hp, e_hr, e_cq, e_ct, *e_st, e_rk, e_oh, e_mat, e_pay, e_xm, e_pt, e_s1, e_g, e_sx, e_s2, e_cs,
                     e_ch, e_cp, e_cz, e_tk)

        def edge_phase(kind, p):
            DW = D + 1 if kind == 0 else D
            slots = slots33 if kind == 0 else slots32
            
            def sweep(eng, step):
                def one(s):
                    step(s, s // 2, s % 2, s // 4, s % 4)

                for s in range(8):
                    one(s)
                with eng.Fori(2, G // 4) as m:
                    for r in range(4):
                        step(m * 4 + r, m * 2 + r // 2, r % 2, m, r)
                for s in range(G // 4 * 4, G + 3):
                    one(s)

            def back(k, n, b):
                return n + (b - k) // 2, (b - k) % 2

            def inside(g):
                return not isinstance(g, int) or 0 <= g < G

            with nc.Block() as block:
                @block.sync
                def _(sp):
                    def indices(g, m, r):
                        wait(sp, e_ga[r], m * (16 * GT))
                        sp.dma_start(idxb[:, r, :], srcg[bass.ds(g, 1), :, :].rearrange("o q t -> (o q) t")
                                     ).then_inc(e_idx[r], 16)

                    def features(g, b):
                        if kind == 0:
                            wait(sp, e_hp, g - 1)
                            sp.dma_start(eft[0:2 * D, b, :], ef_t[bass.ds(g, 1), :, :].rearrange("o q n -> (o q) n")
                                         ).then_inc(e_ef[b], 16)
                        if kind == 1:
                            wait(sp, e_s1, g - 1)
                            sp.dma_start(ehg[:, b, :], ehid[bass.ds(g, 1), :, :].rearrange("o q n -> (o q) n")
                                         ).then_inc(e_ld[b], 16)
                        if kind == 2:
                            wait(sp, e_pay, g - 1)
                            sp.dma_start(ehg[:, b, 0:GT * D], ef_e[bass.ds(g, 1), :, :].rearrange("o q n -> (o q) n")
                                         ).then_inc(e_ld[b], 16)

                    def slot_nodes(g, b):
                        wait(sp, e_mat, g - 1)
                        sp.dma_start(nrow[:, b, :], slotnode[bass.ds(p, 1), bass.ds(g * SL + SL, SL)].to_broadcast([SL, SL])
                                     ).then_inc(e_nc[b], 16)
                        sp.dma_start(ncol[:, b, :], slotnode[bass.ds(p, 1), bass.ds(g * SL, 2 * SL)].rearrange(
                            "o (c a) -> (o a) c", c=2),
                                     allow_slow_non_contiguous=True).then_inc(e_nc[b], 16)

                    def step(s, n, b, m, r):
                        if isinstance(s, int) and s == 0:
                            indices(0, 0, 0)
                        if inside(s + 1):
                            indices(s + 1, m + (r == 3), (r + 1) % 4)
                        if inside(s):
                            features(s, b)
                        if inside(s - 1):
                            slot_nodes(s - 1, 1 - b)
                    sweep(sp, step)

                @block.gpsimd
                def _(pool):
                    def step(g, i, b, m, r):
                        if not inside(g):
                            return
                        wait(pool, e_s1, g - 3)
                        wait(pool, e_idx[r], (m + 1) * 16)
                        wait(pool, e_tk, g - 1)
                        pool.tensor_tensor(pool_tick[0:1, b:b + 1], pool_tick[0:1, 2:3], pool_tick[0:1, 3:4], ALU.add
                                           ).then_inc(e_tk, 1)
                        for j in range(GT):
                            pool.indirect_dma_start(out=xg[:, r, j, 0:D], out_offset=None, in_=feat[:, :],
                                                    in_offset=bass.IndirectOffsetOnAxis(ap=idxb[:, r, j:j + 1], axis=0)
                                                    ).then_inc(e_ga[r], 16)
                    sweep(pool, step)
                    for r in range(4):
                        pool.wait_ge(e_ga[r], 16 * GT * len(range(r, G, 4)))

                @block.vector
                def _(dve):
                    dve.memset(cp[:, :, :], 0.0).then_inc(e_cz, 1)
                    if kind == 1:
                        dve.memset(sx4[:, :, :], 0.0).then_inc(e_cz, 1)

                    def matrices(g, i, b):
                        wait(dve, e_nc[b], (i + 1) * 32)
                        wait(dve, e_ch, g - 1)
                        dve.tensor_scalar(same[:, b, :], nrow[:, b, :], ncol[:, b, 1:2], None, ALU.is_equal)
                        dve.scalar_tensor_tensor(carry[:, b, :], nrow[:, b, :], ncol[:, b, 0:1], last_tile[:, :],
                                                 ALU.is_equal, ALU.mult).then_inc(e_mat, 1)

                    def payload(g, i, b, m, r):
                        wait(dve, e_s1, g - 1)
                        dve.tensor_copy(rk[:, b, :], rank_t[:, bass.ds(g * GT, GT)]).then_inc(e_rk, 1)
                        wait(dve, e_rk, g + 1)
                        dve.tensor_tensor(onehot[:, b, :].rearrange("p (j w) -> p j w", w=W),
                                          rk[:, b, :, None].to_broadcast([128, GT, W]),
                                          iota_w[:, None, :].to_broadcast([128, GT, W]), ALU.is_equal).then_inc(e_oh, 1)
                        if kind == 0:
                            dve.tensor_copy(wcol[:, b, :],
                                            w_t[:, bass.ds(g * GT, GT)]).then_inc(e_pay, 1)
                        wait(dve, e_ga[r], (m + 1) * (16 * GT))
                        if kind == 1:
                            for j in range(GT):
                                q = (GT * b + j) % 4
                                wait(dve, e_pt, g * GT + (j - 3))
                                dve.scalar_tensor_tensor(
                                    xm[:, q, :].rearrange("p (i w) -> p i w", w=W),
                                    iota_w[:, None, :].to_broadcast([128, D, W]), rk[:, b, j:j + 1],
                                    xg[:, r, j, 0:D, None].to_broadcast([128, D, W]),
                                    ALU.is_equal, ALU.mult).then_inc(e_xm, 1)
                        if kind == 2:
                            wait(dve, e_ld[b], (i + 1) * 16)
                            dve.tensor_tensor(xg[:, r, :, 0:D], xg[:, r, :, 0:D],
                                              ehg[:, b, 0:GT * D].rearrange("p (j d) -> p j d", d=D), ALU.add
                                              ).then_inc(e_xm, 1)
                            wait(dve, e_xm, g + 1)
                            dve.tensor_scalar(xg[:, r, :, 0:D], xg[:, r, :, 0:D], 0.0, None, ALU.max).then_inc(e_pay, 1)
                        if kind == 3:
                            dve.tensor_tensor(xg[:, r, :, 0:D], xg[:, r, :, 0:D],
                                              w_t[:, bass.ds(g * GT, GT), None].to_broadcast([128, GT, D]), ALU.mult
                                              ).then_inc(e_pay, 1)

                    def step(s, i, b, m, r):
                        if inside(s):
                            payload(s, i, b, m, r)
                        if inside(s - 2):
                            matrices(s - 2, i - 1, b)
                    sweep(dve, step)

                @block.tensor
                def _(pe):
                    pe.wait_ge(e_cz, 1)
                    if kind == 0:
                        pe.wait_ge(e_w1, 16 * 4 + 2)

                    def tiles(g, i, b, m, r):
                        pe.wait_ge(e_oh, g + 1)
                        pe.wait_ge(e_ga[r], (m + 1) * (16 * GT))
                        if kind != 1:
                            pe.wait_ge(e_pay, g + 1)
                        if kind != 1:
                            wait(pe, e_sx, g)
                        if kind == 1:
                            pe.wait_ge(e_ld[b], (i + 1) * 16)
                        for j in range(GT):
                            if kind == 1:
                                q = (GT * b + j) % 4
                                pe.wait_ge(e_xm, g * GT + (j + 1))
                                wait(pe, e_g, g * GT + (j - 3))
                                pe.matmul(ps[q][:, 0:D * W], lhsT=ehg[:, b, KF * j:KF * j + KF], rhs=xm[:, q, :],
                                          start=True, stop=True).then_inc(e_pt, 1)
                            if kind != 1:
                                last = pe.matmul(ps[4][0:D, W * j:W * j + W], lhsT=xg[:, r, j, :],
                                                 rhs=onehot[:, b, W * j:W * j + W], start=True, stop=True)
                            if kind == 0:
                                last = pe.matmul(ps[4][D:D + 1, W * j:W * j + W], lhsT=wcol[:, b, j:j + 1],
                                                 rhs=onehot[:, b, W * j:W * j + W], start=True, stop=True)
                        if kind == 1:
                            wait(pe, e_sx, g)
                            for j in range(0, GT, 4):
                                n = min(4, GT - j)
                                last = pe.matmul(ps[4][0:D * n, W * j:W * (j + n)], lhsT=xg[:, r, j:j + n, :].rearrange("p j d -> p (j d)"),
                                                 rhs=onehot[:, b, W * j:W * (j + n)], start=True, stop=True)
                        last.then_inc(e_s1, 1)

                    def combine(g, b):
                        pe.wait_ge(e_g, g * GT + GT)
                        wait(pe, e_ct, g)
                        for k in range(0, D, 4):
                            for c in range(4):
                                last = pe.matmul(ps[5][D * c:D * c + D, 0:SL], lhsT=w2[:, k + c, :],
                                                 rhs=gb[:, b, k + c, :], start=(k == 0), stop=(k == D - 4))
                        last.then_inc(e_cq, 1)

                    def fold(g, b):
                        pe.wait_ge(e_sx, g + 1)
                        wait(pe, e_cs, g)
                        out_c = ps[6][0:SL, 0:DW]
                        if kind == 1:
                            pe.wait_ge(e_ct, g + 1)
                            pe.matmul(out_c, lhsT=sx4[:, b, :], rhs=b2x4[:, :], start=True, stop=False)
                            last = pe.matmul(out_c, lhsT=ct[:, b, :], rhs=ident4[:, :], start=False, stop=True)
                        else:
                            last = pe.matmul(out_c, lhsT=sxs[0:DW, b, :], rhs=ident[0:DW, 0:DW], start=True, stop=True)
                        last.then_inc(e_s2, 1)

                    def chain(g, b):
                        pe.wait_ge(e_cs, g + 1)
                        pe.wait_ge(e_mat, g + 1)
                        wait(pe, e_cp, g)
                        out_c = ps[7][0:SL, 0:DW]
                        pe.matmul(out_c, lhsT=same[:, b, :], rhs=cs[:, b, 0:DW], start=True, stop=False)
                        pe.matmul(out_c, lhsT=carry[:, b, :], rhs=cp[:, 1 - b, 0:DW], start=False, stop=True
                                  ).then_inc(e_ch, 1)

                    def hidden(g, i, b):
                        pe.wait_ge(e_ef[b], (i + 1) * 16)
                        wait(pe, e_hr, g)
                        for q in range(GT // 2):
                            last = pe.matmul(ps[q // 2][:, 2 * KF * (q % 2):2 * KF * (q % 2) + 2 * KF],
                                             lhsT=eft[:, b, EDGES * q:EDGES * q + EDGES], rhs=en1_bd[:, :],
                                             start=True, stop=True)
                        last.then_inc(e_hp, 1)

                    def step(s, i, b, m, r):
                        if kind == 0 and inside(s):
                            hidden(s, i, b)
                        if inside(s):
                            tiles(s, i, b, m, r)
                        if kind == 1 and inside(s - 1):
                            combine(s - 1, 1 - b)
                        if inside(s - 2):
                            fold(s - 2, b)
                        if inside(s - 3):
                            chain(s - 3, 1 - b)
                    sweep(pe, step)

                @block.scalar
                def _(act):
                    act.wait_ge(e_cz, 1)

                    if kind == 1:
                        act.wait_ge(e_cz, 2)

                    def step(s, i, b, m, r):
                        if inside(s):
                            if kind == 0:
                                act.wait_ge(e_hp, s + 1)
                                wait(act, e_hs[b], i * 16)
                                for q in range(-(-GT // 4)):
                                    n = min(4 * KF, GT * KF - 4 * KF * q)
                                    last = act.activation(ehg[:, b, 4 * KF * q:4 * KF * q + n], ps[q][:, 0:n], ACT.Relu)
                                last.then_inc(e_hr, 1)
                                act.wait_ge(e_hr, s + 1)
                                act.dma_start(ehid[bass.ds(s, 1), :, :].rearrange("o q n -> (o q) n"), ehg[:, b, :]
                                              ).then_inc(e_hs[b], 16)
                            if kind == 1:
                                wait(act, e_cq, s - 1)
                                for j in range(GT):
                                    act.wait_ge(e_pt, s * GT + (j + 1))
                                    act.activation(gb[:, b, :, W * j:W * j + W],
                                                   ps[(GT * b + j) % 4][:, 0:D * W].rearrange("p (i w) -> p i w", w=W),
                                                   ACT.Copy).then_inc(e_g, 1)
                            wait(act, e_s2, s - 1)
                            act.wait_ge(e_s1, s + 1)
                            if kind == 1:
                                for c in range(4):
                                    rows = slice(D * c, D * c + D)
                                    cols = lambda t: t.rearrange("p (j w) -> p j w", w=W)[:, c:GT:4, :]
                                    last = act.activation(cols(sx4[rows, b, :]), cols(ps[4][rows, 0:SL]), ACT.Copy)
                                last.then_inc(e_sx, 1)
                            else:
                                act.activation(sxs[0:DW, b, :], ps[4][0:DW, 0:SL], ACT.Copy).then_inc(e_sx, 1)
                        if kind == 1 and inside(s - 1):
                            g, c = s - 1, 1 - b
                            act.wait_ge(e_cq, g + 1)
                            wait(act, e_s2, g - 1)
                            act.activation(ct[:, c, :], ps[5][:, 0:SL], ACT.Copy).then_inc(e_ct, 1)
                        if inside(s - 2):
                            g = s - 2
                            act.wait_ge(e_s2, g + 1)
                            wait(act, e_ch, g - 1)
                            act.activation(cs[:, b, 0:DW], ps[6][0:SL, 0:DW], ACT.Copy).then_inc(e_cs, 1)
                        if inside(s - 3):
                            g, (n, c) = s - 3, back(3, i, b)
                            act.wait_ge(e_ch, g + 1)
                            wait(act, e_st[c], n * 16)
                            act.activation(cp[:, c, 0:DW], ps[7][0:SL, 0:DW], ACT.Copy).then_inc(e_cp, 1)
                            act.wait_ge(e_cp, g + 1)
                            act.dma_start(slots[bass.ds(g * SL, SL), :], cp[:, c, 0:DW]).then_inc(e_st[c], 16)
                    sweep(act, step)
                    if kind == 0:
                        for b in range(2):
                            act.wait_ge(e_hs[b], 16 * (G // 2))
                    for b in range(2):
                        act.wait_ge(e_st[b], 16 * (G // 2))
            close(edge_sems, e_ga)

        n_hm, n_ga, n_ad = [sem(n) for n in ("homes_in", "sums_gathered", "window_moved")]

        def bring_home(kind, p):
            DW = D + 1 if kind == 0 else D
            slots = slots33 if kind == 0 else slots32
            with nc.Block() as block:
                @block.sync
                def _(sp):
                    sp.dma_start(home[:, :], homes[bass.ds(p, 1), :, :].rearrange("o q b -> (o q) b")).then_inc(n_hm, 16)

                @block.gpsimd
                def _(pool):
                    pool.wait_ge(n_hm, 16)
                    for c in range(NB):
                        pool.indirect_dma_start(out=gat[:, c, 0:DW], out_offset=None, in_=slots[:, :],
                                                in_offset=bass.IndirectOffsetOnAxis(ap=home[:, c:c + 1], axis=0)
                                                ).then_inc(n_ga, 16)
                    pool.wait_ge(n_ga, 16 * NB)

                @block.vector
                def _(dve):
                    dve.tensor_scalar(iota_w[:, :], iota_w[:, :], float(W), None, ALU.add).then_inc(n_ad, 1)
                    dve.wait_ge(n_ga, 16 * NB)
                    dve.tensor_tensor(agg[:, :, 0:DW], agg[:, :, 0:DW], gat[:, :, 0:DW], ALU.add).then_inc(n_ad, 1)
                    dve.wait_ge(n_ad, 2)
            close((n_hm, n_ad), (n_ga,))

        m_ch, m_ac, m_ra, m_tr, m_tc, m_mm, m_mc, m_st, m_pw = [sem(n) for n in (
            "node_dve_chain", "node_act_done", "node_act_asked", "node_transposed", "node_transposed_copied",
            "node_products", "node_products_read", "features_stored", "window_reset")]
        node_sems = (m_ch, m_ac, m_ra, m_tr, m_tc, m_mm, m_mc, m_st, m_pw)
        tp = sb("tp", [128, 2, 2, P])
        QB = NB // 4
        Fl = "p b d -> p (b d)"

        def rows_of(t, q):
            return t[:, 4 * q:4 * q + 4, 0:D].rearrange(Fl) if t is not agg else t[:, 4 * q:4 * q + 4, 0:D]

        def products(block, operands, weights, n_cols, evac, ready):
            @block.tensor
            def _(pe):
                pe.wait_ge(m_ra, ready)
                for q in range(QB + 1):
                    if q < QB:
                        if q >= 2:
                            pe.wait_ge(m_tc, q - 1)
                        for k, t in enumerate(operands):
                            last = pe.transpose(ps[q % 2][:, 128 * k:128 * k + P], rows_of(t, q), ident[0:P, 0:P])
                        last.then_inc(m_tr, 1)
                    if q >= 1:
                        c = q - 1
                        pe.wait_ge(m_tc, c + 1)
                        if c >= 2:
                            pe.wait_ge(m_mc, c - 1)
                        for at, width, k, wt, first, stop in weights:
                            last = pe.matmul(ps[2 + c % 2][0:P, at:at + width], lhsT=tp[:, c % 2, k, :], rhs=wt,
                                             start=first, stop=stop)
                        last.then_inc(m_mm, 1)

            @block.scalar
            def _(act):
                for q in range(QB):
                    act.wait_ge(m_tr, q + 1)
                    if q >= 2:
                        act.wait_ge(m_mm, q - 1)
                    act.activation(tp[:, q % 2, 0:len(operands), :],
                                   ps[q % 2][:, 0:128 * len(operands)].rearrange("p (k n) -> p k n", n=128)[:, :, 0:P],
                                   ACT.Copy).then_inc(m_tc, 1)
                evac(act)

        def bcast_d(t):
            return t[:, :, None].to_broadcast([P, NB, D])

        def bcast_b(t):
            return t[:, None, :].to_broadcast([P, NB, D])

        def norm(dve, link, n_act):
            link(dve.tensor_reduce(mean[:, :], xcur[:, :, :], AX.X, ALU.add))
            link(dve.tensor_scalar(mean[:, :], mean[:, :], 1.0 / D, None, ALU.mult))
            link(dve.tensor_tensor(hcur[:, :, :], xcur[:, :, :], bcast_d(mean), ALU.subtract))
            link(dve.tensor_tensor(tmp[:, :, :], hcur[:, :, :], hcur[:, :, :], ALU.mult))
            dve.tensor_reduce(rstd[:, :], tmp[:, :, :], AX.X, ALU.add).then_inc(m_pw, 1)
            dve.wait_ge(m_ac, n_act)
            link(dve.reciprocal(rstd[:, :], rstd[:, :]))
            link(dve.tensor_tensor(hcur[:, :, :], hcur[:, :, :], bcast_d(rstd), ALU.mult))
            link(dve.tensor_scalar(hcur[:, :, :], hcur[:, :, :], 0.0, None, ALU.max))

        def root(act, n):
            act.wait_ge(m_pw, n)
            act.activation(rstd[:, :], rstd[:, :], ACT.Sqrt, bias=ln_eps[:, 0:1], scale=1.0 / D).then_inc(m_ac, 1)

        def store_features(sp, t, n):
            sp.wait_ge(m_st, n)
            sp.dma_start(feat.rearrange("(p b) d -> p b d", p=P), t[:, :, :]).then_inc(m_st, 16)
            sp.wait_ge(m_st, 16 + n)

        def reset_window(dve):
            return dve.tensor_scalar(iota_w[:, :], iota_w[:, :], iota_w[:, 0:1], None, ALU.subtract)

        with nc.Block() as block:
            @block.vector
            def _(dve):
                link = Chain(dve, m_ch)
                dve.memset(en1_bd[:, :], 0.0).then_inc(e_w1, 1)
                for c in range(4):
                    dve.tensor_copy(ident4[D * c:D * c + D, :], ident[D * c:D * c + D, D * c:D * c + D])
                dve.memset(eft[2 * D:2 * D + 1, :, :], 1.0).then_inc(e_w1, 1)
                norm(dve, link, 1)
                dve.memset(mean[:, 0:1], 0.0).then_inc(m_st, 1)

            @block.scalar
            def _(act):
                root(act, 1)

            @block.sync
            def _(sp):
                sp.wait_ge(e_w1, 2)
                for j in range(2):
                    sp.dma_start(en1_bd[D * j:D * j + D, KF * j:KF * j + KF], en1[:, :]).then_inc(e_w1, 16)
                    sp.dma_start(en1_bd[2 * D:2 * D + 1, KF * j:KF * j + KF], en1_b[None, :]).then_inc(e_w1, 16)
                store_features(sp, hcur, 1)
        close(node_sems)

        with nc.Fori(0, passes) as p:
            edge_phase(0, p)
            bring_home(0, p)

        iw0 = sb("iw0", [128, 1])
        with nc.Block() as block:
            @block.vector
            def _(dve):
                link = Chain(dve, m_ch)
                link(dve.tensor_copy(iw0[:, :], iota_w[:, 0:1]))
                link(dve.tensor_scalar(iota_w[:, :], iota_w[:, :], iw0[:, 0:1], None, ALU.subtract))
                link(dve.tensor_scalar(dis[:, :], agg[:, :, D:D + 1].rearrange(Fl), 1.0, None, ALU.add))
                link(dve.tensor_scalar(cnt[:, :], cnt[:, :], 1.0, None, ALU.max))
                link(dve.reciprocal(cnt[:, :], cnt[:, :]))
                link(dve.tensor_tensor(tmp[:, :, :], agg[:, :, 0:D], bcast_d(cnt), ALU.mult))
                dve.memset(agg[:, :, :], 0.0).then_inc(m_ra, 1)
                for q in range(QB):
                    dve.wait_ge(m_mm, q + 1)
                    dve.tensor_tensor(gat[:, 4 * q:4 * q + 4, 0:D],
                                      ps[2 + q % 2][0:P, 0:4 * D].rearrange("p (b d) -> p b d", d=D),
                                      bias0[:, None, :].to_broadcast([P, 4, D]), ALU.add).then_inc(m_mc, 1)
                dve.wait_ge(m_mc, QB)
                link(dve.scalar_tensor_tensor(xcur[:, :, :], gat[:, :, 0:D], 0.0, xcur[:, :, :], ALU.max, ALU.add))
                norm(dve, link, 2)
                dve.memset(mean[:, 0:1], 0.0).then_inc(m_st, 1)

            def scalars(act):
                act.wait_ge(m_ra, 1)
                act.activation(dis[:, :], dis[:, :], ACT.Sqrt).then_inc(m_ac, 1)
                root(act, 1)

            products(block, (hcur, tmp), ((0, 4 * D, 0, bd_a[:, :], True, False), (0, 4 * D, 1, bd_b[:, :], False, True)),
                     4 * D, scalars, 1)
        close(node_sems)

        with nc.Block() as block:
            @block.vector
            def _(dve):
                link = Chain(dve, m_ch)
                dve.reciprocal(dis[:, :], dis[:, :]).then_inc(m_ra, 1)
                for q in range(QB):
                    dve.wait_ge(m_mm, q + 1)
                    dve.tensor_tensor(tmp[:, 4 * q:4 * q + 4, :],
                                      ps[2 + q % 2][0:P, 0:4 * D].rearrange("p (b d) -> p b d", d=D),
                                      bias_lin[:, None, :].to_broadcast([P, 4, D]), ALU.add).then_inc(m_mc, 1)
                dve.wait_ge(m_mc, QB)
                dve.tensor_scalar(hcur[:, :, :], tmp[:, :, :], 0.0, None, ALU.max).then_inc(m_st, 1)

            @block.sync
            def _(sp):
                store_features(sp, hcur, 1)
            products(block, (hcur,), ((0, 4 * D, 0, bd_lin[:, :], True, True),), 4 * D, lambda act: None, 1)
        close(node_sems)

        gview = gb[0:P, :, :, :].rearrange("p a i s -> p (a i s)")
        RZ = gview[:, 0:NB * 2 * D].rearrange("p (b c d) -> p b c d", c=2, d=D)
        inn = gat
        hn = sb("hn", [P, NB, D])
        with nc.Fori(0, STEPS) as _step:
            with nc.Fori(0, passes) as p:
                edge_phase(1, p)
                bring_home(1, p)
            with nc.Block() as block:
                @block.vector
                def _(dve):
                    link = Chain(dve, m_ch)
                    link(dve.tensor_copy(iw0[:, :], iota_w[:, 0:1]))
                    link(dve.tensor_scalar(iota_w[:, :], iota_w[:, :], iw0[:, 0:1], None, ALU.subtract))
                    link(dve.tensor_tensor(tmp[:, :, :], agg[:, :, 0:D], bcast_b(bias_conv), ALU.add))
                    dve.memset(agg[:, :, :], 0.0)
                    dve.tensor_scalar(tmp[:, :, :], tmp[:, :, :], 0.0, None, ALU.max).then_inc(m_ra, 1)
                    for q in range(QB):
                        bank = ps[2 + q % 2]
                        bs = slice(4 * q, 4 * q + 4)
                        dve.wait_ge(m_mm, q + 1)
                        dve.tensor_tensor(RZ[:, bs, :, :].rearrange("p b c d -> p b (c d)"),
                                          bank[0:P, 0:8 * D].rearrange("p (b c) -> p b c", c=2 * D),
                                          bias_ih[:, None, 0:2 * D].to_broadcast([P, 4, 2 * D]), ALU.add)
                        dve.tensor_tensor(inn[:, bs, 0:D], bank[0:P, 8 * D:12 * D].rearrange("p (b d) -> p b d", d=D),
                                          bias_ih[:, None, 2 * D:3 * D].to_broadcast([P, 4, D]), ALU.add)
                        dve.tensor_tensor(hn[:, bs, :], bank[0:P, 12 * D:16 * D].rearrange("p (b d) -> p b d", d=D),
                                          bias_hh[:, None, 2 * D:3 * D].to_broadcast([P, 4, D]), ALU.add).then_inc(m_mc, 1)
                    dve.wait_ge(m_mc, QB)
                    dve.tensor_tensor(RZ.rearrange("p b c d -> p b (c d)"), RZ.rearrange("p b c d -> p b (c d)"),
                                      bias_hh[:, None, 0:2 * D].to_broadcast([P, NB, 2 * D]), ALU.add).then_inc(m_pw, 1)
                    dve.wait_ge(m_ac, 1)
                    link(dve.tensor_tensor(hn[:, :, :], RZ[:, :, 0, :], hn[:, :, :], ALU.mult))
                    dve.tensor_tensor(hn[:, :, :], hn[:, :, :], inn[:, :, 0:D], ALU.add).then_inc(m_pw, 1)
                    dve.wait_ge(m_ac, 2)
                    link(dve.tensor_tensor(tmp[:, :, :], hcur[:, :, :], hn[:, :, :], ALU.subtract))
                    link(dve.tensor_tensor(tmp[:, :, :], tmp[:, :, :], RZ[:, :, 1, :], ALU.mult))
                    dve.tensor_tensor(hcur[:, :, :], tmp[:, :, :], hn[:, :, :], ALU.add).then_inc(m_st, 1)

                @block.sync
                def _(sp):
                    store_features(sp, hcur, 1)

                def gate_functions(act):
                    act.wait_ge(m_pw, 1)
                    act.activation(gview[:, 0:NB * 2 * D], gview[:, 0:NB * 2 * D], ACT.Sigmoid).then_inc(m_ac, 1)
                    act.wait_ge(m_pw, 2)
                    act.activation(hn[:, :, :], hn[:, :, :], ACT.Tanh).then_inc(m_ac, 1)

                products(block, (tmp, hcur), (
                    (0, 8 * D, 0, bd_ih[:, 0:8 * D], True, False), (0, 8 * D, 1, bd_hh[:, 0:8 * D], False, True),
                    (8 * D, 4 * D, 0, bd_ih[:, 8 * D:12 * D], True, True),
                    (12 * D, 4 * D, 1, bd_hh[:, 8 * D:12 * D], True, True)), 16 * D, gate_functions, 1)
            close(node_sems)

        with nc.Block() as block:
            @block.vector
            def _(dve):
                link = Chain(dve, m_ch)
                link(dve.tensor_tensor(xcur[:, :, :], xcur[:, :, :], hcur[:, :, :], ALU.add))
                link(dve.tensor_scalar(eps_sb[:, :], eps_sb[:, :], 1.0, None, ALU.add))
                norm(dve, link, 1)
                dve.memset(mean[:, 0:1], 0.0).then_inc(m_st, 1)

            @block.scalar
            def _(act):
                root(act, 1)

            @block.sync
            def _(sp):
                store_features(sp, hcur, 1)
        close(node_sems)
        with nc.Fori(0, passes) as p:
            edge_phase(2, p)
            bring_home(2, p)

        with nc.Block() as block:
            @block.vector
            def _(dve):
                link = Chain(dve, m_ch)
                link(dve.tensor_copy(iw0[:, :], iota_w[:, 0:1]))
                link(dve.tensor_scalar(iota_w[:, :], iota_w[:, :], iw0[:, 0:1], None, ALU.subtract))
                link(dve.scalar_tensor_tensor(tmp[:, :, :], hcur[:, :, :], eps_sb[:, 0:1], agg[:, :, 0:D],
                                              ALU.mult, ALU.add))
                link(dve.tensor_tensor(xcur[:, :, :], xcur[:, :, :], tmp[:, :, :], ALU.add))
                link(dve.memset(agg[:, :, :], 0.0))
                norm(dve, link, 1)
                dve.tensor_tensor(hcur[:, :, :], hcur[:, :, :], bcast_d(dis), ALU.mult).then_inc(m_st, 1)

            @block.scalar
            def _(act):
                root(act, 1)

            @block.sync
            def _(sp):
                store_features(sp, hcur, 1)
        close(node_sems)
        with nc.Fori(0, passes) as p:
            edge_phase(3, p)
            bring_home(3, p)

        with nc.Block() as block:
            @block.vector
            def _(dve):
                link = Chain(dve, m_ch)
                link(dve.tensor_tensor(tmp[:, :, :], agg[:, :, 0:D], hcur[:, :, :], ALU.add))
                link(dve.tensor_tensor(tmp[:, :, :], tmp[:, :, :], bcast_d(dis), ALU.mult))
                dve.tensor_tensor(xcur[:, :, :], xcur[:, :, :], tmp[:, :, :], ALU.add).then_inc(m_st, 1)

            @block.sync
            def _(sp):
                sp.wait_ge(m_st, 1)
                sp.dma_start(out.rearrange("(p b) d -> p b d", p=P), xcur[:, :, :]).then_inc(m_st, 16)
                sp.wait_ge(m_st, 17)


def kernel(x, src, dst, edge_attr_32, L0_gnn_W, L0_gnn_b, L1_gnn_lin0_w, L1_gnn_lin0_b, L1_gnn_en1_w, L1_gnn_en1_b,
           L1_gnn_en2_w, L1_gnn_en2_b, L1_gnn_conv_bias, L1_gnn_gru_wih, L1_gnn_gru_whh, L1_gnn_gru_bih,
           L1_gnn_gru_bhh, L2_gnn_eps):
    import numpy as np
    import concourse.bacc as bacc
    from concourse.bass_utils import run_bass_kernel_spmd

    src, dst, ef = np.asarray(src), np.asarray(dst), np.asarray(edge_attr_32)
    src_p = np.zeros((T, EDGES), np.int32)
    src_p.reshape(-1)[:E] = src
    dst_p = np.full((RB * 128, EDGES), PAD_DST, np.int32)
    dst_p.reshape(-1)[:E] = dst
    ef_p = np.zeros((T * EDGES, D), np.float32)
    ef_p[:E] = ef
    ef_p = ef_p.reshape(G, GT, EDGES, D)
    ins = [
        ("x", x), ("srcg", src_p.reshape(G, GT, EDGES).transpose(0, 2, 1)), ("src_t", src_p.T), ("dst_t", dst_p[:T].T),
        ("dst_rows", dst_p),
        ("ef_e", ef_p.transpose(0, 2, 1, 3).reshape(G, EDGES, GT * D)),
        ("ef_t", ef_p.reshape(G, GT // 2, 2, EDGES, D).transpose(0, 2, 4, 1, 3).reshape(G, 2 * D, GT // 2 * EDGES)),
        ("w0", L0_gnn_W), ("b0", L0_gnn_b), ("lin0", np.asarray(L1_gnn_lin0_w).T), ("lin0_b", L1_gnn_lin0_b),
        ("en1", np.asarray(L1_gnn_en1_w).T), ("en1_b", L1_gnn_en1_b), ("en2", np.asarray(L1_gnn_en2_w).T),
        ("en2_b", L1_gnn_en2_b), ("conv_b", L1_gnn_conv_bias), ("wih", np.asarray(L1_gnn_gru_wih).T),
        ("whh", np.asarray(L1_gnn_gru_whh).T), ("bih", L1_gnn_gru_bih), ("bhh", L1_gnn_gru_bhh), ("eps", L2_gnn_eps),
    ]
    nc = bacc.Bacc("TRN2", target_bir_lowering=False, num_devices=1)
    arrays, args = {}, []
    for name, a in ins:
        a = np.ascontiguousarray(a)
        arrays[f"in_{name}"] = a
        args.append(nc.dram_tensor(f"in_{name}", a.shape, mybir.dt.from_np(a.dtype), kind="ExternalInput").ap())
    args.append(nc.dram_tensor("out_0", (N, D), mybir.dt.float32, kind="ExternalOutput").ap())
    bass_gnn(nc, *args)
    return run_bass_kernel_spmd(nc, [arrays], core_ids=[0]).results[0]["out_0"]
```

```python
import concourse.bass as bass
from concourse import mybir
from contextlib import ExitStack

N, E, D, KF, STEPS = 12500, 200000, 32, 128, 6
EDGES = 128
W = 12
GT = 10
SL = W * GT
T_REAL = -(-E // EDGES)
G = -(-T_REAL // GT)
T = G * GT
RB = -(-T // 128)
MAXP = -(-EDGES // W)
P = 125
NB = N // P
NC2 = NB + 2
ZROW = G * SL
PAD_DST = 1 << 20
WIN = 128
EPS = 1e-5


def bass_gnn(nc, x, srcg, src_t, dst_t, dst_rows, ef_e, ef_t, w0, b0, lin0, lin0_b, en1, en1_b,
             en2, en2_b, conv_b, wih, whh, bih, bhh, eps, out):
    f32, i32 = mybir.dt.float32, mybir.dt.int32
    ALU, ACT, AX = mybir.AluOpType, mybir.ActivationFunctionType, mybir.AxisListType
    with ExitStack() as ctx:
        def sb(name, shape, dt=f32):
            return ctx.enter_context(nc.sbuf_tensor(name, shape, dt))

        def sem(name):
            return ctx.enter_context(nc.semaphore(name))

        def dram(name, shape, dt=f32):
            return nc.dram_tensor(name, shape, dt, kind="Internal").ap()

        feat = dram("feat", (N, D))
        slots33 = dram("slots33", (ZROW + 1, D + 1))
        slots32 = dram("slots32", (ZROW + 1, D))
        ehid = dram("ehid", (G, 128, GT * KF))
        rowtab = dram("rowtab", (RB * 128, 2 * EDGES))
        slotnode = dram("slotnode", (MAXP, (G + 1) * SL))
        slotnode0 = dram("slotnode0", (1, T * W))
        nodesum = dram("nodesum", (N + WIN, D))
        nodew = dram("nodew", (N + WIN, 2))
        homes = dram("homes", (MAXP, P, NB), i32)

        ident = sb("ident", [128, 128])
        iota_w = sb("iota_w", [128, W])
        rank_t = sb("rank_t", [128, T])
        w_t = sb("w_t", [128, T])
        xcur = sb("xcur", [P, NB, D])
        hcur = sb("hcur", [P, NB, D])
        agg = sb("agg", [P, NB, D])
        aggw = sb("aggw", [P, NB, 2])
        dstrel_t = sb("dstrel_t", [128, T])
        gsel = sb("gsel", [128, G, 2])
        gbase_i = sb("gbase_i", [1, G], i32)
        iota_n = sb("iota_n", [128, WIN])
        dense = sb("dense", [1, 1], i32)
        gat = sb("gat", [P, NB, D + 1])
        tmp = sb("tmp", [P, NB, D])
        home = sb("home", [P, NB], i32)
        cnt = sb("cnt", [P, NB])
        dis = sb("dis", [P, NB])
        mean = sb("mean", [P, NB])
        rstd = sb("rstd", [P, NB])
        eps_sb = sb("eps_sb", [P, 1])
        ln_eps = sb("ln_eps", [P, 1])
        w2 = sb("w2", [128, D, D])
        b2x4 = sb("b2x4", [4 * D, D])
        last_tile = sb("last_tile", [SL, SL])
        npass = sb("npass", [1, 1], i32)
        pool_tick = sb("pool_tick", [1, 4])
        zrow = sb("zrow", [1, 256])
        bd_a = sb("bd_a", [128, 4 * D])
        bd_b = sb("bd_b", [128, 4 * D])
        bd_lin = sb("bd_lin", [128, 4 * D])
        bd_ih = sb("bd_ih", [128, 4 * 3 * D])
        bd_hh = sb("bd_hh", [128, 4 * 3 * D])
        bias0 = sb("bias0", [P, D])
        bias_lin = sb("bias_lin", [P, D])
        bias_conv = sb("bias_conv", [4 * D, 1])
        bias_ih = sb("bias_ih", [P, 3 * D])
        bias_hh = sb("bias_hh", [P, 3 * D])

        ps = [ctx.enter_context(nc.psum_tensor(f"bank{k}", [128, 512], f32)) for k in range(8)]

        def wait(eng, s, v):
            if not isinstance(v, int) or v > 0:
                eng.wait_ge(s, v)

        def close(sems, gathers=()):
            for s in gathers:
                nc.gpsimd.dma_reset(range(s.num, s.num + 1))
                nc.gpsimd.sem_clear(s)
            for s in sems:
                nc.gpsimd.sem_clear(s)
            nc.all_engine_barrier()

        class Chain:

            def __init__(self, eng, s):
                self.eng, self.s, self.n = eng, s, 0

            def __call__(self, ins):
                ins.then_inc(self.s, 1)
                self.n += 1
                self.eng.wait_ge(self.s, self.n)

        with ExitStack() as ph:
            def sbp(name, shape, dt=f32):
                return ph.enter_context(nc.sbuf_tensor(name, shape, dt))

            drow_i = sbp("drow_i", [128, RB, EDGES], i32)
            fnode = sbp("fnode", [128, RB, EDGES])
            rank = sbp("rank", [128, RB, EDGES])
            slotn = sbp("slotn", [128, RB, W])
            junk = sbp("junk", [128, EDGES])
            junks = sbp("junks", [128, 4, EDGES])
            t0n = sbp("t0n", [P, NC2])
            c1 = sbp("c1", [P, NC2])
            d1 = sbp("d1", [P, NC2])
            idx1 = sbp("idx1", [P, NC2], i32)
            nodeid = sbp("nodeid", [P, NC2])
            rp = sbp("rp", [P, NC2])
            rr = sbp("rr", [P, NB])
            crosses = sbp("crosses", [P, NB])
            f_a = sbp("f_a", [P, NB])
            f_b = sbp("f_b", [P, NB])
            f_c = sbp("f_c", [P, NB])
            fint = sbp("fint", [P, NB], i32)

            s_in, s_zero, s_pool, s_ch, s_rk, s_tr, s_rt, s_done = [
                sem(n) for n in ("inputs_in", "zeroed", "pool_made", "dve_chain", "ranks_ready",
                                 "rank_transposed", "row_table_written", "setup_stored")]
            s_fb, s_t1, s_g1, s_u1, s_ev = [sem(n) for n in (
                "firsts_in", "tile_of_node", "tile_row_in", "tile_row_used", "rank_evacuated")]
            s_bd = sem("diagonals_in")
            lastspan = sbp("lastspan", [1, 1])
            maxshift = sbp("maxshift", [1, 1])
            sub = ExitStack()
            drow = sub.enter_context(nc.sbuf_tensor("drow", [128, RB, EDGES], f32))
            first = sub.enter_context(nc.sbuf_tensor("first", [128, RB, EDGES], f32))
            fdst = sub.enter_context(nc.sbuf_tensor("fdst", [128, RB, EDGES], f32))
            tcol_i = sub.enter_context(nc.sbuf_tensor("tcol_i", [128, 2, T], i32))
            tbc_i = sub.enter_context(nc.sbuf_tensor("tbc_i", [128, T], i32))
            base = sub.enter_context(nc.sbuf_tensor("base", [128, G], f32))
            shift = sub.enter_context(nc.sbuf_tensor("shift", [128, G], f32))
            part = sub.enter_context(nc.sbuf_tensor("part", [128, 1], f32))
            with nc.Block() as block:
                @block.sync
                def _(sp):
                    sp.dma_start(drow_i[:, :, :], dst_rows.rearrange("(r p) e -> p r e", p=128)).then_inc(s_in, 16)
                    sp.dma_start(tcol_i[:, 0, :], src_t[:, :]).then_inc(s_in, 16)
                    sp.dma_start(tcol_i[:, 1, :], dst_t[:, :]).then_inc(s_in, 16)
                    sp.dma_start(tbc_i[:, :], dst_t[0:1, :].to_broadcast([128, T])).then_inc(s_in, 16)
                    sp.dma_start(xcur[:, :, :], x.rearrange("(p b) d -> p b d", p=P)).then_inc(s_in, 16)
                    for dst, vec in ((bias0, b0), (bias_lin, lin0_b),
                                     (bias_ih, bih), (bias_hh, bhh), (eps_sb, eps)):
                        sp.dma_start(dst[:, :], vec[None, :].to_broadcast([P, vec.shape[0]])).then_inc(s_in, 16)
                    sp.dma_start(w2[:, :, :].rearrange("k i o -> k (i o)"), en2[:, :]).then_inc(s_in, 16)
                    for c in range(4):
                        sp.dma_start(b2x4[D * c:D * c + D, :], en2_b.rearrange("(i o) -> i o", o=D)).then_inc(s_in, 16)
                        sp.dma_start(bias_conv[D * c:D * c + D, :], conv_b.rearrange("(i o) -> i o", o=1)).then_inc(s_in, 16)
                    sp.wait_ge(s_zero, 5)
                    for j in range(4):
                        rows = slice(D * j, D * j + D)
                        for bd, w_in in ((bd_a, w0[0:D, :]), (bd_b, w0[D:2 * D, :]), (bd_lin, lin0)):
                            sp.dma_start(bd[rows, D * j:D * j + D], w_in).then_inc(s_bd, 16)
                        for bd, w_in in ((bd_ih, wih), (bd_hh, whh)):
                            sp.dma_start(bd[rows, 2 * D * j:2 * D * j + 2 * D], w_in[:, 0:2 * D]).then_inc(s_bd, 16)
                            sp.dma_start(bd[rows, 8 * D + D * j:8 * D + D * j + D], w_in[:, 2 * D:3 * D]).then_inc(s_bd, 16)
                    sp.wait_ge(s_rk, 1)
                    rt = rowtab.rearrange("(r p) (h e) -> p r h e", p=128, h=2)
                    sp.dma_start(rt[:, :, 0, :], drow[:, :, :]).then_inc(s_rt, 16)
                    sp.dma_start(rt[:, :, 1, :], fdst[:, :, :]).then_inc(s_rt, 16)
                    sp.wait_ge(s_zero, 6)
                    sp.dma_start(slots33[ZROW:ZROW + 1, :], zrow[0:1, 0:D + 1]).then_inc(s_done, 16)
                    sp.dma_start(slots32[ZROW:ZROW + 1, :], zrow[0:1, 0:D]).then_inc(s_done, 16)
                    sp.wait_ge(s_rt, 32)
                    sp.wait_ge(s_done, 32)
                    sp.wait_ge(s_bd, 16 * 28)

                @block.gpsimd
                def _(pool):
                    pool.memset(ident[:, :], 0.0).then_inc(s_pool, 1)
                    pool.memset(last_tile[:, :], 1.0).then_inc(s_pool, 1)
                    pool.memset(pool_tick[:, :], 0.0).then_inc(s_pool, 1)
                    pool.iota(iota_w[:, :], [[1, W]], base=0, channel_multiplier=0,
                              allow_small_or_imprecise_dtypes=True).then_inc(s_pool, 1)
                    pool.iota(nodeid[:, :], [[1, NC2]], base=0, channel_multiplier=NB,
                              allow_small_or_imprecise_dtypes=True).then_inc(s_pool, 1)
                    pool.iota(iota_n[:, :], [[1, WIN]], base=0, channel_multiplier=0,
                              allow_small_or_imprecise_dtypes=True).then_inc(s_pool, 1)
                    pool.iota(part[:, :], [[0, 1]], base=0, channel_multiplier=1,
                              allow_small_or_imprecise_dtypes=True).then_inc(s_pool, 1)
                    pool.wait_ge(s_pool, 7)
                    pool.affine_select(out=ident[:, :], in_=ident[:, :], compare_op=ALU.not_equal, fill=1.0,
                                       base=0, pattern=[[-1, 128]], channel_multiplier=1).then_inc(s_pool, 1)
                    pool.affine_select(out=last_tile[:, :], in_=last_tile[:, :], compare_op=ALU.is_ge, fill=0.0,
                                       base=-(SL - W), pattern=[[0, SL]], channel_multiplier=1).then_inc(s_pool, 1)
                    pool.wait_ge(s_pool, 9)

                @block.vector
                def _(dve):
                    link = Chain(dve, s_ch)
                    for t in (bd_a, bd_b, bd_lin, bd_ih, bd_hh):
                        dve.memset(t[:, :], 0.0).then_inc(s_zero, 1)
                    dve.memset(zrow[:, :], 0.0).then_inc(s_zero, 1)
                    dve.memset(ln_eps[:, :], EPS)
                    dve.memset(first[:, :, 0:1], 0.0)
                    link(dve.memset(junk[:, :], 1.0))
                    dve.wait_ge(s_in, 16 * 19)
                    dve.tensor_tensor(w_t[:, :], tcol_i[:, 0, :], tcol_i[:, 1, :], ALU.not_equal)
                    link(dve.tensor_copy(drow[:, :, :], drow_i[:, :, :]))
                    link(dve.tensor_tensor(first[:, :, 1:EDGES], drow[:, :, 1:EDGES], drow[:, :, 0:EDGES - 1],
                                           ALU.not_equal))
                    for r in range(RB):
                        last = dve.tensor_tensor_scan(rank[:, r, :], junk[:, :], first[:, r, :], 0.0, ALU.mult, ALU.add)
                    link(last)
                    link(dve.tensor_scalar(fdst[:, :, :], drow[:, :, :], float(PAD_DST // 2), -5000.0,
                                           ALU.is_ge, ALU.mult))
                    dve.memset(first[:, :, 0:1], 1.0)
                    link(dve.tensor_tensor(rank[:, :, :], rank[:, :, :], fdst[:, :, :], ALU.add))
                    link(dve.scalar_tensor_tensor(fnode[:, :, :], drow[:, :, :], 1.0, first[:, :, :], ALU.add, ALU.mult))
                    link(dve.tensor_scalar(fdst[:, :, :], first[:, :, :], -float(PAD_DST + 1), float(PAD_DST),
                                           ALU.mult, ALU.add))
                    dve.tensor_tensor(fdst[:, :, :], fdst[:, :, :], fnode[:, :, :], ALU.add).then_inc(s_rk, 1)
                    link(dve.tensor_copy(base[:, :], tbc_i[:, 0:T:GT]))
                    link(dve.memset(base[:, 0:1], 0.0))
                    dve.tensor_copy(gbase_i[:, :], base[0:1, :])
                    dve.tensor_tensor(dstrel_t[:, :].rearrange("p (g j) -> p g j", j=GT),
                                      tcol_i[:, 1, :].rearrange("p (g j) -> p g j", j=GT),
                                      base[:, :, None].to_broadcast([128, G, GT]), ALU.subtract)
                    dve.memset(shift[:, 0:1], -1.0)
                    dve.tensor_scalar(gsel[:, :, 0:1].rearrange("p g o -> p (g o)"), base[:, :], 1.0, None, ALU.add)
                    dve.tensor_scalar(lastspan[:, :], base[0:1, G - 1:G], -1.0, float(N), ALU.mult, ALU.add)
                    link(dve.tensor_tensor(shift[:, 1:G], base[:, 1:G], base[:, 0:G - 1], ALU.subtract))
                    dve.wait_ge(s_pool, 9)
                    dve.tensor_scalar(gsel[:, :, 1:2].rearrange("p g o -> p (g o)"), shift[:, :], part[:, 0:1], None,
                                      ALU.is_equal)
                    link(dve.tensor_reduce(maxshift[:, :], shift[0:1, :], AX.X, ALU.max))
                    for r in range(RB):
                        n = min(128, T - 128 * r)
                        dve.wait_ge(s_tr, r + 1)
                        last = dve.tensor_copy(rank_t[:, 128 * r:128 * r + n], ps[r % 8][:, 0:n])
                        last.then_inc(s_ev, 1)
                    dve.wait_ge(s_ev, RB)

                @block.tensor
                def _(pe):
                    pe.wait_ge(s_pool, 9)
                    pe.wait_ge(s_rk, 1)
                    for r in range(RB):
                        if r >= 8:
                            pe.wait_ge(s_ev, r - 7)
                        pe.transpose(ps[r % 8][:, 0:128], rank[:, r, :], ident[:, :]).then_inc(s_tr, 1)
            sub.close()

            rmax = sbp("rmax", [128, 1])
            rall = sbp("rall", [128, 1])
            thr = sbp("thr", [1, MAXP - 1])
            npf = sbp("npf", [1, 1])
            okf = sbp("okf", [1, 3])
            s_cc, s_rm, s_ra, s_th, s_sz, s_s0 = [sem(n) for n in (
                "dve_chain_2", "rank_max", "rank_max_all", "thresholds", "slot_nodes_0", "slot_nodes_0_written")]
            with nc.Block() as block:
                @block.gpsimd
                def _(pool):
                    pool.iota(thr[:, :], [[W, MAXP - 1]], base=W, channel_multiplier=0,
                              allow_small_or_imprecise_dtypes=True).then_inc(s_th, 1)
                    pool.wait_ge(s_rm, 1)
                    pool.partition_all_reduce(rall[:, :], rmax[:, :], 128, bass.bass_isa.ReduceOp.max).then_inc(s_ra, 1)

                @block.vector
                def _(dve):
                    link = Chain(dve, s_cc)
                    dve.tensor_reduce(rmax[:, :], rank[:, :, :], AX.XY, ALU.max).then_inc(s_rm, 1)
                    for r in range(RB):
                        for w in range(W):
                            last = dve.scalar_tensor_tensor(junks[:, w % 4, :], rank[:, r, :], float(w), fnode[:, r, :],
                                                            ALU.is_equal, ALU.mult, accum_out=slotn[:, r, w:w + 1])
                            if w % 4 == 3 or w == W - 1:
                                link(last)
                    dve.memset(junks[:, 0, 0:1], 0.0).then_inc(s_sz, 1)
                    dve.wait_ge(s_ra, 1)
                    dve.wait_ge(s_th, 1)
                    link(dve.tensor_scalar(thr[:, :], thr[:, :], rall[0:1, 0:1], 0.0, ALU.is_le, ALU.add,
                                           accum_out=npf[:, :]))
                    link(dve.tensor_scalar(npass[:, :], npf[:, :], 1.0, None, ALU.add))
                    dve.tensor_scalar(okf[:, 0:1], npf[:, :], 0.5, None, ALU.is_lt)
                    dve.tensor_scalar(okf[:, 1:2], maxshift[:, :], WIN - 0.5, None, ALU.is_lt)
                    link(dve.tensor_scalar(okf[:, 2:3], lastspan[:, :], WIN + 0.5, None, ALU.is_lt))
                    link(dve.tensor_tensor(okf[:, 0:1], okf[:, 0:1], okf[:, 1:2], ALU.mult))
                    link(dve.tensor_tensor(okf[:, 0:1], okf[:, 0:1], okf[:, 2:3], ALU.mult))
                    link(dve.tensor_copy(dense[:, :], okf[:, 0:1]))

                @block.sync
                def _(sp):
                    sp.wait_ge(s_sz, 1)
                    for r in range(RB):
                        n = min(128, T - 128 * r)
                        sp.dma_start(slotnode0[0:1, 128 * r * W:(128 * r + n) * W].rearrange("o (t w) -> (o t) w", w=W),
                                     slotn[0:n, r, :]).then_inc(s_s0, 16)
                    sp.wait_ge(s_s0, 16 * RB)
            nc.all_engine_barrier()
            passes = nc.values_load(npass[0:1, 0:1], min_val=1, max_val=MAXP)
            is_dense = nc.values_load(dense[0:1, 0:1], min_val=0, max_val=1)
            tfirst = sbp("tfirst", [P, T])
            tfirst_i = sbp("tfirst_i", [P, T], i32)
            junk2 = sbp("junk2", [P, T])
            rows = sbp("rows", [P, 4, 2 * EDGES])
            junk3 = sbp("junk3", [P, 2, EDGES])
            s_ch2 = sem("dve_chain_search")
            s_row = [sem(f"row_gathered{k}") for k in range(4)]
            s_sn, s_fh, s_ch3, s_pp = [sem(n) for n in ("slot_nodes_ready", "homes_ready", "dve_chain_3", "pass_tables_written")]
            neg = sbp("neg", [1, SL])
            with nc.If(is_dense < 1):
                nc.all_engine_barrier()
                with nc.Block() as block:
                    @block.sync
                    def _(sp):
                        sp.dma_start(tfirst_i[:, :], dst_t[0:1, :].to_broadcast([P, T])).then_inc(s_fb, 16)

                    @block.gpsimd
                    def _(pool):
                        for c in range(NB + 1):
                            if c == 0:
                                pool.wait_ge(s_t1, 1)
                            if c >= 4:
                                pool.wait_ge(s_u1, c - 3)
                            pool.indirect_dma_start(out=rows[:, c % 4, :], out_offset=None, in_=rowtab[:, :],
                                                    in_offset=bass.IndirectOffsetOnAxis(ap=idx1[:, c:c + 1], axis=0)
                                                    ).then_inc(s_row[c % 4], 16)

                    @block.vector
                    def _(dve):
                        link = Chain(dve, s_ch2)
                        dve.memset(d1[:, :], 0.0)
                        dve.wait_ge(s_fb, 16)
                        link(dve.tensor_copy(tfirst[:, :], tfirst_i[:, :]))
                        for c in range(NB + 1):
                            last = dve.tensor_scalar(junk2[:, :], tfirst[:, :], nodeid[:, c:c + 1], 0.0, ALU.is_lt, ALU.add,
                                                     accum_out=t0n[:, c:c + 1])
                            link(last)
                        C = NB + 1
                        link(dve.tensor_scalar(t0n[:, 0:C], t0n[:, 0:C], -1.0, 0.0, ALU.add, ALU.max))
                        dve.tensor_copy(idx1[:, 0:C], t0n[:, 0:C]).then_inc(s_t1, 1)
                        for c in range(C):
                            dve.wait_ge(s_row[c % 4], 16 * (c // 4 + 1))
                            if c >= 1:
                                dve.wait_ge(s_u1, c)
                            link(dve.tensor_scalar(junk3[:, 0, :], rows[:, c % 4, 0:EDGES], nodeid[:, c:c + 1], 0.0,
                                                   ALU.is_lt, ALU.add, accum_out=c1[:, c:c + 1]))
                            dve.tensor_scalar(junk3[:, 1, :], rows[:, c % 4, EDGES:2 * EDGES], nodeid[:, c:c + 1], 0.0,
                                              ALU.is_lt, ALU.add, accum_out=d1[:, c:c + 1]).then_inc(s_u1, 1)
                        dve.wait_ge(s_u1, C)
                        link(dve.scalar_tensor_tensor(rp[:, 0:C], t0n[:, 0:C], float(EDGES), c1[:, 0:C], ALU.mult, ALU.add))
                        link(dve.tensor_tensor(cnt[:, :], rp[:, 1:C], rp[:, 0:NB], ALU.subtract))
                        link(dve.tensor_scalar(f_a[:, :], c1[:, 0:NB], float(EDGES), None, ALU.is_equal))
                        link(dve.tensor_tensor(f_b[:, :], d1[:, 0:NB], f_a[:, :], ALU.mult))
                        dve.tensor_tensor(rr[:, :], d1[:, 0:NB], f_b[:, :], ALU.subtract)
                        link(dve.tensor_tensor(f_c[:, :], t0n[:, 0:NB], f_a[:, :], ALU.add))
                        dve.tensor_tensor(crosses[:, :], t0n[:, 1:C], f_c[:, :], ALU.is_gt)
                        link(dve.tensor_scalar(d1[:, 0:NB], f_c[:, :], float(W), -float(ZROW), ALU.mult, ALU.add))
                        link(dve.tensor_scalar(c1[:, 0:NB], t0n[:, 1:C], float(W), -float(ZROW), ALU.mult, ALU.add))
                        link(dve.tensor_scalar(t0n[:, 0:NB], cnt[:, :], 0.0, None, ALU.is_gt))

                slots_sems = (s_sn, s_fh, s_ch3, s_pp)
                with nc.Fori(0, passes) as p:
                    with nc.Block() as block:
                        @block.vector
                        def _(dve):
                            link = Chain(dve, s_ch3)
                            dve.memset(neg[:, :], -7.0).then_inc(s_sn, 1)
                            for r in range(RB):
                                for w in range(W):
                                    last = dve.scalar_tensor_tensor(junk[:, :], rank[:, r, :], float(w), fnode[:, r, :],
                                                                    ALU.is_equal, ALU.mult,
                                                                    accum_out=slotn[:, r, w:w + 1])
                                    link(last)
                            dve.memset(junk[:, 0:1], 0.0).then_inc(s_sn, 1)
                            link(dve.tensor_scalar(f_a[:, :], rr[:, :], 0.0, None, ALU.is_ge))
                            link(dve.tensor_scalar(f_b[:, :], rr[:, :], float(W), None, ALU.is_lt))
                            link(dve.tensor_tensor(f_a[:, :], f_a[:, :], f_b[:, :], ALU.mult))
                            link(dve.tensor_tensor(f_b[:, :], f_a[:, :], crosses[:, :], ALU.mult))
                            link(dve.tensor_tensor(f_a[:, :], f_a[:, :], f_b[:, :], ALU.subtract))
                            link(dve.tensor_tensor(f_b[:, :], d1[:, 0:NB], rr[:, :], ALU.add))
                            link(dve.tensor_tensor(f_a[:, :], f_a[:, :], f_b[:, :], ALU.mult))
                            link(dve.tensor_tensor(f_b[:, :], crosses[:, :], c1[:, 0:NB], ALU.mult))
                            link(dve.tensor_tensor(f_a[:, :], f_a[:, :], f_b[:, :], ALU.add))
                            link(dve.tensor_tensor(f_a[:, :], f_a[:, :], t0n[:, 0:NB], ALU.mult))
                            link(dve.tensor_scalar(f_a[:, :], f_a[:, :], float(ZROW), None, ALU.add))
                            dve.tensor_copy(fint[:, :], f_a[:, :]).then_inc(s_fh, 1)
                            dve.memset(crosses[:, :], 0.0)
                            link(dve.tensor_scalar(rr[:, :], rr[:, :], -float(W), None, ALU.add))
                            link(dve.tensor_scalar(rank[:, :, :], rank[:, :, :], -float(W), None, ALU.add))

                        @block.sync
                        def _(sp):
                            sp.wait_ge(s_sn, 2)
                            for r in range(RB):
                                n = min(128, T - 128 * r)
                                sp.dma_start(slotnode[bass.ds(p, 1), SL + 128 * r * W:SL + (128 * r + n) * W].rearrange(
                                    "o (t w) -> (o t) w", w=W), slotn[0:n, r, :]).then_inc(s_pp, 16)
                            sp.dma_start(slotnode[bass.ds(p, 1), 0:SL], neg[:, :]).then_inc(s_pp, 16)
                            sp.wait_ge(s_fh, 1)
                            sp.dma_start(homes[bass.ds(p, 1), :, :].rearrange("o q b -> (o q) b"), fint[:, :]).then_inc(s_pp, 16)
                            sp.wait_ge(s_pp, 16 * (RB + 2))
                    close(slots_sems)

        idxb = sb("idxb", [128, 4, GT], i32)
        xg = sb("xg", [128, 4, GT, D])
        wcol = sb("wcol", [128, 2, GT])
        eft = sb("eft", [2 * D + 1, 2, GT // 2 * EDGES])
        en1_bd = sb("en1_bd", [2 * D + 1, 2 * KF])
        ehg = sb("ehg", [128, 2, GT * KF])
        nrow = sb("nrow", [SL, 2, SL])
        ncol = sb("ncol", [SL, 2, 2])
        gs = sb("gs", [128, 2, 1 + WIN])
        rk = sb("rk", [128, 2, GT])
        onehot = sb("onehot", [128, 2, SL])
        same = sb("same", [SL, 2, WIN])
        carry = sb("carry", [SL, 2, SL])
        xm = sb("xm", [128, 4, D * W])
        gb = sb("gb", [128, 2, D, SL])
        sxs = sb("sxs", [D + 1, 2, SL])
        ct = sb("ct", [4 * D, 2, SL])
        ident4 = sb("ident4", [4 * D, D])
        sx4 = sb("sx4", [4 * D, 2, SL])
        cs = sb("cs", [SL, 2, D + 1])
        cp = sb("cp", [WIN, 2, D + 2])
        e_idx = [sem(f"indices_in{r}") for r in range(4)]
        e_ld = [sem(f"group_in{b}") for b in range(2)]
        e_ga = [sem(f"sources_gathered{r}") for r in range(4)]
        e_ef = [sem(f"edge_features_in{b}") for b in range(2)]
        e_hs = [sem(f"hidden_stored{b}") for b in range(2)]
        e_nc = [sem(f"slot_nodes_in{b}") for b in range(2)]
        e_st = [sem(f"slots_stored{b}") for b in range(2)]
        (e_rk, e_oh, e_mat, e_pay, e_xm, e_pt, e_s1, e_g, e_sx, e_s2, e_cs, e_ch, e_cp, e_cz, e_tk, e_hp, e_hr, e_w1, e_cq, e_ct, e_gs) = [sem(n) for n in (
            "ranks_copied", "onehot_ready", "slot_matrices_ready", "payload_ready", "spread_ready", "outer_in_psum",
            "tile_sums_done", "outer_evacuated", "slot_sums_evacuated", "group_in_psum", "group_evacuated",
            "chained_in_psum", "chained_ready", "chain_zeroed", "pool_ticked",
            "hidden_in_psum", "hidden_ready", "en1_in", "transposed_in_psum", "transposed_evacuated", "group_row_copied")]
        edge_sems = (*e_idx, *e_ld, *e_ef, *e_hs, *e_nc, e_hp, e_hr, e_cq, e_ct, e_gs, *e_st, e_rk, e_oh, e_mat, e_pay, e_xm, e_pt, e_s1, e_g, e_sx, e_s2, e_cs,
                     e_ch, e_cp, e_cz, e_tk)

        def edge_phase(kind, p):
            DW = D + 1 if kind == 0 else D
            slots = slots33 if kind == 0 else slots32
            
            def sweep(eng, step):
                def one(s):
                    step(s, s // 2, s % 2, s // 4, s % 4)

                for s in range(8):
                    one(s)
                with eng.Fori(2, G // 4) as m:
                    for r in range(4):
                        step(m * 4 + r, m * 2 + r // 2, r % 2, m, r)
                for s in range(G // 4 * 4, G + 3):
                    one(s)

            def back(k, n, b):
                return n + (b - k) // 2, (b - k) % 2

            def inside(g):
                return not isinstance(g, int) or 0 <= g < G

            with nc.Block() as block:
                @block.sync
                def _(sp):
                    def indices(g, m, r):
                        wait(sp, e_ga[r], m * (16 * GT))
                        sp.dma_start(idxb[:, r, :], srcg[bass.ds(g, 1), :, :].rearrange("o q t -> (o q) t")
                                     ).then_inc(e_idx[r], 16)

                    def features(g, b):
                        if kind == 0:
                            wait(sp, e_hp, g - 1)
                            sp.dma_start(eft[0:2 * D, b, :], ef_t[bass.ds(g, 1), :, :].rearrange("o q n -> (o q) n")
                                         ).then_inc(e_ef[b], 16)
                        if kind == 1:
                            wait(sp, e_s1, g - 1)
                            sp.dma_start(ehg[:, b, :], ehid[bass.ds(g, 1), :, :].rearrange("o q n -> (o q) n")
                                         ).then_inc(e_ld[b], 16)
                        if kind == 2:
                            wait(sp, e_pay, g - 1)
                            sp.dma_start(ehg[:, b, 0:GT * D], ef_e[bass.ds(g, 1), :, :].rearrange("o q n -> (o q) n")
                                         ).then_inc(e_ld[b], 16)

                    def slot_nodes(g, b):
                        wait(sp, e_mat, g - 1)
                        sp.dma_start(nrow[:, b, :], slotnode[bass.ds(p, 1), bass.ds(g * SL + SL, SL)].to_broadcast([SL, SL])
                                     ).then_inc(e_nc[b], 16)
                        sp.dma_start(ncol[:, b, :], slotnode[bass.ds(p, 1), bass.ds(g * SL, 2 * SL)].rearrange(
                            "o (c a) -> (o a) c", c=2),
                                     allow_slow_non_contiguous=True).then_inc(e_nc[b], 16)

                    def step(s, n, b, m, r):
                        if isinstance(s, int) and s == 0:
                            indices(0, 0, 0)
                        if inside(s + 1):
                            indices(s + 1, m + (r == 3), (r + 1) % 4)
                        if inside(s):
                            features(s, b)
                        if inside(s - 1):
                            slot_nodes(s - 1, 1 - b)
                    sweep(sp, step)

                @block.gpsimd
                def _(pool):
                    def step(g, i, b, m, r):
                        if not inside(g):
                            return
                        wait(pool, e_s1, g - 3)
                        wait(pool, e_idx[r], (m + 1) * 16)
                        wait(pool, e_tk, g - 1)
                        pool.tensor_tensor(pool_tick[0:1, b:b + 1], pool_tick[0:1, 2:3], pool_tick[0:1, 3:4], ALU.add
                                           ).then_inc(e_tk, 1)
                        for j in range(GT):
                            pool.indirect_dma_start(out=xg[:, r, j, 0:D], out_offset=None, in_=feat[:, :],
                                                    in_offset=bass.IndirectOffsetOnAxis(ap=idxb[:, r, j:j + 1], axis=0)
                                                    ).then_inc(e_ga[r], 16)
                    sweep(pool, step)
                    for r in range(4):
                        pool.wait_ge(e_ga[r], 16 * GT * len(range(r, G, 4)))

                @block.vector
                def _(dve):
                    dve.memset(cp[:, :, :], 0.0).then_inc(e_cz, 1)
                    if kind == 1:
                        dve.memset(sx4[:, :, :], 0.0).then_inc(e_cz, 1)

                    def matrices(g, i, b):
                        wait(dve, e_nc[b], (i + 1) * 32)
                        wait(dve, e_ch, g - 1)
                        dve.tensor_scalar(same[:, b, 0:SL], nrow[:, b, :], ncol[:, b, 1:2], None, ALU.is_equal)
                        dve.scalar_tensor_tensor(carry[:, b, :], nrow[:, b, :], ncol[:, b, 0:1], last_tile[:, :],
                                                 ALU.is_equal, ALU.mult).then_inc(e_mat, 1)

                    def payload(g, i, b, m, r):
                        wait(dve, e_s1, g - 1)
                        dve.tensor_copy(rk[:, b, :], rank_t[:, bass.ds(g * GT, GT)]).then_inc(e_rk, 1)
                        wait(dve, e_rk, g + 1)
                        dve.tensor_tensor(onehot[:, b, :].rearrange("p (j w) -> p j w", w=W),
                                          rk[:, b, :, None].to_broadcast([128, GT, W]),
                                          iota_w[:, None, :].to_broadcast([128, GT, W]), ALU.is_equal).then_inc(e_oh, 1)
                        if kind == 0:
                            dve.tensor_copy(wcol[:, b, :],
                                            w_t[:, bass.ds(g * GT, GT)]).then_inc(e_pay, 1)
                        wait(dve, e_ga[r], (m + 1) * (16 * GT))
                        if kind == 1:
                            for j in range(GT):
                                q = (GT * b + j) % 4
                                wait(dve, e_pt, g * GT + (j - 3))
                                dve.scalar_tensor_tensor(
                                    xm[:, q, :].rearrange("p (i w) -> p i w", w=W),
                                    iota_w[:, None, :].to_broadcast([128, D, W]), rk[:, b, j:j + 1],
                                    xg[:, r, j, 0:D, None].to_broadcast([128, D, W]),
                                    ALU.is_equal, ALU.mult).then_inc(e_xm, 1)
                        if kind == 2:
                            wait(dve, e_ld[b], (i + 1) * 16)
                            dve.tensor_tensor(xg[:, r, :, 0:D], xg[:, r, :, 0:D],
                                              ehg[:, b, 0:GT * D].rearrange("p (j d) -> p j d", d=D), ALU.add
                                              ).then_inc(e_xm, 1)
                            wait(dve, e_xm, g + 1)
                            dve.tensor_scalar(xg[:, r, :, 0:D], xg[:, r, :, 0:D], 0.0, None, ALU.max).then_inc(e_pay, 1)
                        if kind == 3:
                            dve.tensor_tensor(xg[:, r, :, 0:D], xg[:, r, :, 0:D],
                                              w_t[:, bass.ds(g * GT, GT), None].to_broadcast([128, GT, D]), ALU.mult
                                              ).then_inc(e_pay, 1)

                    def step(s, i, b, m, r):
                        if inside(s):
                            payload(s, i, b, m, r)
                        if inside(s - 2):
                            matrices(s - 2, i - 1, b)
                    sweep(dve, step)

                @block.tensor
                def _(pe):
                    pe.wait_ge(e_cz, 1)
                    if kind == 0:
                        pe.wait_ge(e_w1, 16 * 4 + 2)

                    def tiles(g, i, b, m, r):
                        pe.wait_ge(e_oh, g + 1)
                        pe.wait_ge(e_ga[r], (m + 1) * (16 * GT))
                        if kind != 1:
                            pe.wait_ge(e_pay, g + 1)
                        if kind != 1:
                            wait(pe, e_sx, g)
                        if kind == 1:
                            pe.wait_ge(e_ld[b], (i + 1) * 16)
                        for j in range(GT):
                            if kind == 1:
                                q = (GT * b + j) % 4
                                pe.wait_ge(e_xm, g * GT + (j + 1))
                                wait(pe, e_g, g * GT + (j - 3))
                                pe.matmul(ps[q][:, 0:D * W], lhsT=ehg[:, b, KF * j:KF * j + KF], rhs=xm[:, q, :],
                                          start=True, stop=True).then_inc(e_pt, 1)
                            if kind != 1:
                                last = pe.matmul(ps[4][0:D, W * j:W * j + W], lhsT=xg[:, r, j, :],
                                                 rhs=onehot[:, b, W * j:W * j + W], start=True, stop=True)
                            if kind == 0:
                                last = pe.matmul(ps[4][D:D + 1, W * j:W * j + W], lhsT=wcol[:, b, j:j + 1],
                                                 rhs=onehot[:, b, W * j:W * j + W], start=True, stop=True)
                        if kind == 1:
                            wait(pe, e_sx, g)
                            for j in range(0, GT, 4):
                                n = min(4, GT - j)
                                last = pe.matmul(ps[4][0:D * n, W * j:W * (j + n)], lhsT=xg[:, r, j:j + n, :].rearrange("p j d -> p (j d)"),
                                                 rhs=onehot[:, b, W * j:W * (j + n)], start=True, stop=True)
                        last.then_inc(e_s1, 1)

                    def combine(g, b):
                        pe.wait_ge(e_g, g * GT + GT)
                        wait(pe, e_ct, g)
                        for k in range(0, D, 4):
                            for c in range(4):
                                last = pe.matmul(ps[5][D * c:D * c + D, 0:SL], lhsT=w2[:, k + c, :],
                                                 rhs=gb[:, b, k + c, :], start=(k == 0), stop=(k == D - 4))
                        last.then_inc(e_cq, 1)

                    def fold(g, b):
                        pe.wait_ge(e_sx, g + 1)
                        wait(pe, e_cs, g)
                        out_c = ps[6][0:SL, 0:DW]
                        if kind == 1:
                            pe.wait_ge(e_ct, g + 1)
                            pe.matmul(out_c, lhsT=sx4[:, b, :], rhs=b2x4[:, :], start=True, stop=False)
                            last = pe.matmul(out_c, lhsT=ct[:, b, :], rhs=ident4[:, :], start=False, stop=True)
                        else:
                            last = pe.matmul(out_c, lhsT=sxs[0:DW, b, :], rhs=ident[0:DW, 0:DW], start=True, stop=True)
                        last.then_inc(e_s2, 1)

                    def chain(g, b):
                        pe.wait_ge(e_cs, g + 1)
                        pe.wait_ge(e_mat, g + 1)
                        wait(pe, e_cp, g)
                        out_c = ps[7][0:SL, 0:DW]
                        pe.matmul(out_c, lhsT=same[:, b, 0:SL], rhs=cs[:, b, 0:DW], start=True, stop=False)
                        pe.matmul(out_c, lhsT=carry[:, b, :], rhs=cp[0:SL, 1 - b, 0:DW], start=False, stop=True
                                  ).then_inc(e_ch, 1)

                    def hidden(g, i, b):
                        pe.wait_ge(e_ef[b], (i + 1) * 16)
                        wait(pe, e_hr, g)
                        for q in range(GT // 2):
                            last = pe.matmul(ps[q // 2][:, 2 * KF * (q % 2):2 * KF * (q % 2) + 2 * KF],
                                             lhsT=eft[:, b, EDGES * q:EDGES * q + EDGES], rhs=en1_bd[:, :],
                                             start=True, stop=True)
                        last.then_inc(e_hp, 1)

                    def step(s, i, b, m, r):
                        if kind == 0 and inside(s):
                            hidden(s, i, b)
                        if inside(s):
                            tiles(s, i, b, m, r)
                        if kind == 1 and inside(s - 1):
                            combine(s - 1, 1 - b)
                        if inside(s - 2):
                            fold(s - 2, b)
                        if inside(s - 3):
                            chain(s - 3, 1 - b)
                    sweep(pe, step)

                @block.scalar
                def _(act):
                    act.wait_ge(e_cz, 1)

                    if kind == 1:
                        act.wait_ge(e_cz, 2)

                    def step(s, i, b, m, r):
                        if inside(s):
                            if kind == 0:
                                act.wait_ge(e_hp, s + 1)
                                wait(act, e_hs[b], i * 16)
                                for q in range(-(-GT // 4)):
                                    n = min(4 * KF, GT * KF - 4 * KF * q)
                                    last = act.activation(ehg[:, b, 4 * KF * q:4 * KF * q + n], ps[q][:, 0:n], ACT.Relu)
                                last.then_inc(e_hr, 1)
                                act.wait_ge(e_hr, s + 1)
                                act.dma_start(ehid[bass.ds(s, 1), :, :].rearrange("o q n -> (o q) n"), ehg[:, b, :]
                                              ).then_inc(e_hs[b], 16)
                            if kind == 1:
                                wait(act, e_cq, s - 1)
                                for j in range(GT):
                                    act.wait_ge(e_pt, s * GT + (j + 1))
                                    act.activation(gb[:, b, :, W * j:W * j + W],
                                                   ps[(GT * b + j) % 4][:, 0:D * W].rearrange("p (i w) -> p i w", w=W),
                                                   ACT.Copy).then_inc(e_g, 1)
                            wait(act, e_s2, s - 1)
                            act.wait_ge(e_s1, s + 1)
                            if kind == 1:
                                for c in range(4):
                                    rows = slice(D * c, D * c + D)
                                    cols = lambda t: t.rearrange("p (j w) -> p j w", w=W)[:, c:GT:4, :]
                                    last = act.activation(cols(sx4[rows, b, :]), cols(ps[4][rows, 0:SL]), ACT.Copy)
                                last.then_inc(e_sx, 1)
                            else:
                                act.activation(sxs[0:DW, b, :], ps[4][0:DW, 0:SL], ACT.Copy).then_inc(e_sx, 1)
                        if kind == 1 and inside(s - 1):
                            g, c = s - 1, 1 - b
                            act.wait_ge(e_cq, g + 1)
                            wait(act, e_s2, g - 1)
                            act.activation(ct[:, c, :], ps[5][:, 0:SL], ACT.Copy).then_inc(e_ct, 1)
                        if inside(s - 2):
                            g = s - 2
                            act.wait_ge(e_s2, g + 1)
                            wait(act, e_ch, g - 1)
                            act.activation(cs[:, b, 0:DW], ps[6][0:SL, 0:DW], ACT.Copy).then_inc(e_cs, 1)
                        if inside(s - 3):
                            g, (n, c) = s - 3, back(3, i, b)
                            act.wait_ge(e_ch, g + 1)
                            wait(act, e_st[c], n * 16)
                            act.activation(cp[0:SL, c, 0:DW], ps[7][0:SL, 0:DW], ACT.Copy).then_inc(e_cp, 1)
                            act.wait_ge(e_cp, g + 1)
                            act.dma_start(slots[bass.ds(g * SL, SL), :], cp[0:SL, c, 0:DW]).then_inc(e_st[c], 16)
                    sweep(act, step)
                    if kind == 0:
                        for b in range(2):
                            act.wait_ge(e_hs[b], 16 * len(range(b, G, 2)))
                    for b in range(2):
                        act.wait_ge(e_st[b], 16 * len(range(b, G, 2)))
            close(edge_sems, e_ga)

        iw0 = sb("iw0", [128, 1])
        n_hm, n_ga, n_ad = [sem(n) for n in ("homes_in", "sums_gathered", "window_moved")]

        def bring_home(kind, p):
            DW = D + 1 if kind == 0 else D
            slots = slots33 if kind == 0 else slots32
            with nc.Block() as block:
                @block.sync
                def _(sp):
                    sp.dma_start(home[:, :], homes[bass.ds(p, 1), :, :].rearrange("o q b -> (o q) b")).then_inc(n_hm, 16)

                @block.gpsimd
                def _(pool):
                    pool.wait_ge(n_hm, 16)
                    for c in range(NB):
                        pool.indirect_dma_start(out=gat[:, c, 0:DW], out_offset=None, in_=slots[:, :],
                                                in_offset=bass.IndirectOffsetOnAxis(ap=home[:, c:c + 1], axis=0)
                                                ).then_inc(n_ga, 16)
                    pool.wait_ge(n_ga, 16 * NB)

                @block.vector
                def _(dve):
                    dve.tensor_scalar(iota_w[:, :], iota_w[:, :], float(W), None, ALU.add).then_inc(n_ad, 1)
                    dve.wait_ge(n_ga, 16 * NB)
                    dve.tensor_tensor(agg[:, :, :], agg[:, :, :], gat[:, :, 0:D], ALU.add).then_inc(n_ad, 1)
                    if kind == 0:
                        dve.tensor_tensor(aggw[:, :, 0:1], aggw[:, :, 0:1], gat[:, :, D:D + 1], ALU.add).then_inc(n_ad, 1)
                        dve.tensor_copy(aggw[:, :, 1:2], cnt[:, :, None]).then_inc(n_ad, 1)
                    dve.wait_ge(n_ad, 4 if kind == 0 else 2)
            close((n_hm, n_ad), (n_ga,))

        def dense_phase(kind):
            n_st = 32 if kind == 0 else 16
            lag = 3 if kind == 1 else 1
            DW = D + 2 if kind == 0 else D
            member = gb[:, :, :, :].rearrange("p b i s -> p (b i s)")[:, 0:2 * GT * WIN].rearrange(
                "p (b j n) -> p b j n", b=2, j=GT)
            xe = gb[:, :, :, :].rearrange("p b i s -> p (b i s)")[:, 2 * GT * WIN:2 * GT * WIN + 4 * GT * DW].rearrange(
                "p (r j d) -> p r j d", r=4, j=GT) if kind == 0 else xg
            n_set = 3 if kind < 2 else 2

            def sweep(eng, step):
                def one(s):
                    step(s, s // 2, s % 2, s // 4, s % 4)

                for s in range(8):
                    one(s)
                with eng.Fori(2, G // 4) as m:
                    for r in range(4):
                        step(m * 4 + r, m * 2 + r // 2, r % 2, m, r)
                for s in range(G // 4 * 4, G + lag):
                    one(s)

            def back(k, n, b):
                return n + (b - k) // 2, (b - k) % 2

            def inside(g):
                return not isinstance(g, int) or 0 <= g < G

            def n_tiles(g):
                return T_REAL - GT * (G - 1) if isinstance(g, int) and g == G - 1 else GT

            with nc.Block() as block:
                @block.sync
                def _(sp):
                    def indices(g, m, r):
                        wait(sp, e_ga[r], m * (16 * GT))
                        sp.dma_start(idxb[:, r, :], srcg[bass.ds(g, 1), :, :].rearrange("o q t -> (o q) t")
                                     ).then_inc(e_idx[r], 16)

                    def features(g, b):
                        if kind == 0:
                            wait(sp, e_hp, g - 1)
                            sp.dma_start(eft[0:2 * D, b, :], ef_t[bass.ds(g, 1), :, :].rearrange("o q n -> (o q) n")
                                         ).then_inc(e_ef[b], 16)
                        if kind == 1:
                            wait(sp, e_s1, g - 1)
                            sp.dma_start(ehg[:, b, :], ehid[bass.ds(g, 1), :, :].rearrange("o q n -> (o q) n")
                                         ).then_inc(e_ld[b], 16)
                        if kind == 2:
                            wait(sp, e_pay, g - 1)
                            sp.dma_start(ehg[:, b, 0:GT * D], ef_e[bass.ds(g, 1), :, :].rearrange("o q n -> (o q) n")
                                         ).then_inc(e_ld[b], 16)

                    def slot_nodes(g, b):
                        wait(sp, e_mat, g - 1)
                        sp.dma_start(ncol[:, b, 1:2], slotnode0[0:1, bass.ds(g * SL, SL)].rearrange("o (a c) -> (o a) c", c=1)
                                     ).then_inc(e_nc[b], 16)

                    def step(s, n, b, m, r):
                        if isinstance(s, int) and s == 0:
                            indices(0, 0, 0)
                        if inside(s + 1):
                            indices(s + 1, m + (r == 3), (r + 1) % 4)
                        if inside(s):
                            features(s, b)
                        if kind == 1 and inside(s - 1):
                            slot_nodes(s - 1, 1 - b)
                    sweep(sp, step)

                @block.gpsimd
                def _(pool):
                    def step(g, n, b, m, r):
                        if not inside(g):
                            return
                        wait(pool, e_s1, g - 3)
                        wait(pool, e_idx[r], (m + 1) * 16)
                        wait(pool, e_tk, g - 1)
                        pool.tensor_tensor(pool_tick[0:1, b:b + 1], pool_tick[0:1, 2:3], pool_tick[0:1, 3:4], ALU.add
                                           ).then_inc(e_tk, 1)
                        for j in range(n_tiles(g)):
                            pool.indirect_dma_start(out=xe[:, r, j, 0:D], out_offset=None, in_=feat[:, :],
                                                    in_offset=bass.IndirectOffsetOnAxis(ap=idxb[:, r, j:j + 1], axis=0)
                                                    ).then_inc(e_ga[r], 16)
                    sweep(pool, step)
                    for r in range(4):
                        pool.wait_ge(e_ga[r], 16 * sum(n_tiles(g) for g in range(r, G, 4)))

                @block.vector
                def _(dve):
                    dve.memset(gs[:, :, 2:1 + WIN], 0.0).then_inc(e_cz, 1)
                    dve.memset(cp[:, :, :], 0.0).then_inc(e_cz, 1)
                    if kind == 1:
                        dve.memset(sx4[:, :, :], 0.0).then_inc(e_cz, 1)
                    if kind == 0:
                        dve.memset(xe[:, :, :, D + 1:D + 2], 1.0).then_inc(e_cz, 1)

                    def spread(g, n, b, m, r):
                        wait(dve, e_s1, g - 1)
                        dve.tensor_copy(rk[:, b, :], rank_t[:, bass.ds(g * GT, GT)]).then_inc(e_rk, 1)
                        wait(dve, e_rk, g + 1)
                        dve.tensor_tensor(onehot[:, b, :].rearrange("p (j w) -> p j w", w=W),
                                          rk[:, b, :, None].to_broadcast([128, GT, W]),
                                          iota_w[:, None, :].to_broadcast([128, GT, W]), ALU.is_equal).then_inc(e_oh, 1)
                        wait(dve, e_ga[r], m * (16 * GT) + 16 * n_tiles(g))
                        for j in range(n_tiles(g)):
                            q = (GT * b + j) % 4
                            wait(dve, e_pt, g * GT + (j - 3))
                            dve.scalar_tensor_tensor(
                                xm[:, q, :].rearrange("p (i w) -> p i w", w=W),
                                iota_w[:, None, :].to_broadcast([128, D, W]), rk[:, b, j:j + 1],
                                xg[:, r, j, :, None].to_broadcast([128, D, W]),
                                ALU.is_equal, ALU.mult).then_inc(e_xm, 1)

                    def window(g, n, b):
                        wait(dve, e_ch, g - 1)
                        dve.tensor_copy(gs[:, b, 0:2], gsel[:, bass.ds(g, 1), :].rearrange("p g c -> p (g c)")
                                        ).then_inc(e_oh if kind != 1 else e_gs, 1)
                        if kind == 1:
                            wait(dve, e_nc[b], (n + 1) * 16)
                            wait(dve, e_gs, g + 1)
                            dve.tensor_scalar(same[:, b, :], iota_n[0:SL, :], gs[0:SL, b, 0:1], ncol[:, b, 1:2],
                                              ALU.add, ALU.is_equal).then_inc(e_mat, 1)

                    def messages(g, n, b, m, r):
                        wait(dve, e_s1, g - 1)
                        if kind == 0:
                            dve.tensor_copy(xe[:, r, :, D:D + 1].rearrange("p j o -> p (j o)"),
                                            w_t[:, bass.ds(g * GT, GT)])
                        dve.tensor_tensor(member[:, b, :, :], iota_n[:, None, :].to_broadcast([128, GT, WIN]),
                                          dstrel_t[:, bass.ds(g * GT, GT), None].to_broadcast([128, GT, WIN]), ALU.is_equal
                                          ).then_inc(e_mat, 1)
                        if kind == 2:
                            wait(dve, e_ga[r], m * (16 * GT) + 16 * n_tiles(g))
                            wait(dve, e_ld[b], (n + 1) * 16)
                            nt = n_tiles(g)
                            dve.tensor_tensor(xg[:, r, 0:nt, :], xg[:, r, 0:nt, :],
                                              ehg[:, b, 0:nt * D].rearrange("p (j d) -> p j d", d=D), ALU.add
                                              ).then_inc(e_xm, 1)
                            wait(dve, e_xm, g + 1)
                            dve.tensor_scalar(xg[:, r, 0:nt, :], xg[:, r, 0:nt, :], 0.0, None, ALU.max).then_inc(e_pay, 1)
                        if kind == 3:
                            wait(dve, e_ga[r], m * (16 * GT) + 16 * n_tiles(g))
                            nt = n_tiles(g)
                            dve.tensor_tensor(xg[:, r, 0:nt, :], xg[:, r, 0:nt, :],
                                              w_t[:, bass.ds(g * GT, nt), None].to_broadcast([128, nt, D]), ALU.mult
                                              ).then_inc(e_pay, 1)

                    def step(s, n, b, m, r):
                        if kind == 1:
                            if inside(s):
                                spread(s, n, b, m, r)
                            if inside(s - 2):
                                window(s - 2, *back(2, n, b))
                        elif inside(s):
                            window(s, n, b)
                            messages(s, n, b, m, r)
                    sweep(dve, step)

                @block.tensor
                def _(pe):
                    pe.wait_ge(e_cz, n_set)
                    if kind == 0:
                        pe.wait_ge(e_w1, 16 * 4 + 2)

                    def outer(g, n, b, m, r):
                        pe.wait_ge(e_oh, g + 1)
                        pe.wait_ge(e_ga[r], m * (16 * GT) + 16 * n_tiles(g))
                        pe.wait_ge(e_ld[b], (n + 1) * 16)
                        for j in range(n_tiles(g)):
                            q = (GT * b + j) % 4
                            pe.wait_ge(e_xm, g * GT + (j + 1))
                            wait(pe, e_g, g * GT + (j - 3))
                            pe.matmul(ps[q][:, 0:D * W], lhsT=ehg[:, b, KF * j:KF * j + KF], rhs=xm[:, q, :],
                                      start=True, stop=True).then_inc(e_pt, 1)
                        wait(pe, e_sx, g)
                        for j in range(0, n_tiles(g), 4):
                            k = min(4, GT - j)
                            last = pe.matmul(ps[4][0:D * k, W * j:W * (j + k)],
                                             lhsT=xg[:, r, j:j + k, :].rearrange("p j d -> p (j d)"),
                                             rhs=onehot[:, b, W * j:W * (j + k)], start=True, stop=True)
                        last.then_inc(e_s1, 1)

                    def combine(g, b):
                        pe.wait_ge(e_g, g * GT + n_tiles(g))
                        wait(pe, e_ct, g)
                        for k in range(0, D, 4):
                            for c in range(4):
                                last = pe.matmul(ps[5][D * c:D * c + D, 0:SL], lhsT=w2[:, k + c, :],
                                                 rhs=gb[:, b, k + c, :], start=(k == 0), stop=(k == D - 4))
                        last.then_inc(e_cq, 1)

                    def fold(g, b):
                        pe.wait_ge(e_sx, g + 1)
                        wait(pe, e_cs, g)
                        pe.wait_ge(e_ct, g + 1)
                        pe.matmul(ps[6][0:SL, 0:D], lhsT=sx4[:, b, :], rhs=b2x4[:, :], start=True, stop=False)
                        pe.matmul(ps[6][0:SL, 0:D], lhsT=ct[:, b, :], rhs=ident4[:, :], start=False, stop=True
                                  ).then_inc(e_s2, 1)

                    def chain(g, b):
                        pe.wait_ge(e_cs, g + 1)
                        pe.wait_ge(e_mat, g + 1)
                        wait(pe, e_cp, g)
                        pe.matmul(ps[7][:, 0:D], lhsT=same[:, b, :], rhs=cs[:, b, 0:D], start=True, stop=False)
                        pe.matmul(ps[7][:, 0:D], lhsT=gs[:, b, 1:1 + WIN], rhs=cp[:, 1 - b, 0:D], start=False, stop=True
                                  ).then_inc(e_ch, 1)

                    def hidden(g, n, b):
                        pe.wait_ge(e_ef[b], (n + 1) * 16)
                        wait(pe, e_hr, g)
                        for q in range(GT // 2):
                            last = pe.matmul(ps[q // 2][:, 2 * KF * (q % 2):2 * KF * (q % 2) + 2 * KF],
                                             lhsT=eft[:, b, EDGES * q:EDGES * q + EDGES], rhs=en1_bd[:, :],
                                             start=True, stop=True)
                        last.then_inc(e_hp, 1)

                    def sums(g, n, b, m, r):
                        pe.wait_ge(e_mat, g + 1)
                        pe.wait_ge(e_ga[r], m * (16 * GT) + 16 * n_tiles(g))
                        if kind != 0:
                            pe.wait_ge(e_pay, g + 1)
                        wait(pe, e_cp, g - 1)
                        for j in range(n_tiles(g)):
                            last = pe.matmul(ps[4 + 2 * b][:, 0:DW], lhsT=member[:, b, j, :], rhs=xe[:, r, j, :],
                                             start=(j == 0), stop=False)
                        last.then_inc(e_s1, 1)

                    def carry_on(g, b):
                        pe.wait_ge(e_oh, g + 1)
                        wait(pe, e_cp, g)
                        pe.matmul(ps[4 + 2 * b][:, 0:DW], lhsT=gs[:, b, 1:1 + WIN], rhs=cp[:, 1 - b, 0:DW],
                                  start=False, stop=True).then_inc(e_ch, 1)

                    def step(s, n, b, m, r):
                        if kind == 1:
                            if inside(s):
                                outer(s, n, b, m, r)
                            if inside(s - 1):
                                combine(s - 1, 1 - b)
                            if inside(s - 2):
                                fold(s - 2, b)
                            if inside(s - 3):
                                chain(s - 3, 1 - b)
                        else:
                            if kind == 0 and inside(s):
                                hidden(s, n, b)
                            if inside(s):
                                sums(s, n, b, m, r)
                            if inside(s - 1):
                                carry_on(s - 1, 1 - b)
                    sweep(pe, step)

                @block.scalar
                def _(act):
                    act.wait_ge(e_cz, n_set)

                    def store(g, n, b):
                        wait(act, e_st[b], n * n_st)
                        act.wait_ge(e_ch, g + 1)
                        if kind == 1:
                            act.activation(cp[:, b, 0:D], ps[7][:, 0:D], ACT.Copy).then_inc(e_cp, 1)
                        else:
                            act.activation(cp[:, b, 0:DW], ps[4 + 2 * b][:, 0:DW], ACT.Copy).then_inc(e_cp, 1)
                        act.wait_ge(e_cp, g + 1)
                        wait(act, e_st[1 - b], (n + b) * n_st)
                        first_node = act.value_load(gbase_i[0:1, bass.ds(g, 1)], min_val=0, max_val=N)
                        act.dma_start(nodesum[bass.ds(first_node, WIN), :], cp[:, b, 0:D]).then_inc(e_st[b], 16)
                        if kind == 0:
                            act.dma_start(nodew[bass.ds(first_node, WIN), :], cp[:, b, D:D + 2]).then_inc(e_st[b], 16)

                    def step(s, n, b, m, r):
                        if inside(s) and kind == 0:
                            act.wait_ge(e_hp, s + 1)
                            wait(act, e_hs[b], n * 16)
                            for q in range(-(-GT // 4)):
                                k = min(4 * KF, GT * KF - 4 * KF * q)
                                last = act.activation(ehg[:, b, 4 * KF * q:4 * KF * q + k], ps[q][:, 0:k], ACT.Relu)
                            last.then_inc(e_hr, 1)
                            act.wait_ge(e_hr, s + 1)
                            act.dma_start(ehid[bass.ds(s, 1), :, :].rearrange("o q n -> (o q) n"), ehg[:, b, :]
                                          ).then_inc(e_hs[b], 16)
                        if inside(s) and kind == 1:
                            wait(act, e_cq, s - 1)
                            for j in range(n_tiles(s)):
                                act.wait_ge(e_pt, s * GT + (j + 1))
                                act.activation(gb[:, b, :, W * j:W * j + W],
                                               ps[(GT * b + j) % 4][:, 0:D * W].rearrange("p (i w) -> p i w", w=W),
                                               ACT.Copy).then_inc(e_g, 1)
                            wait(act, e_s2, s - 1)
                            act.wait_ge(e_s1, s + 1)
                            for c in range(4):
                                rows = slice(D * c, D * c + D)
                                cols = lambda t: t.rearrange("p (j w) -> p j w", w=W)[:, c:GT:4, :]
                                last = act.activation(cols(sx4[rows, b, :]), cols(ps[4][rows, 0:SL]), ACT.Copy)
                            last.then_inc(e_sx, 1)
                        if kind == 1 and inside(s - 1):
                            g, c = s - 1, 1 - b
                            act.wait_ge(e_cq, g + 1)
                            wait(act, e_s2, g - 1)
                            act.activation(ct[:, c, :], ps[5][:, 0:SL], ACT.Copy).then_inc(e_ct, 1)
                        if kind == 1 and inside(s - 2):
                            g = s - 2
                            act.wait_ge(e_s2, g + 1)
                            wait(act, e_ch, g - 1)
                            act.activation(cs[:, b, 0:D], ps[6][0:SL, 0:D], ACT.Copy).then_inc(e_cs, 1)
                        if inside(s - lag):
                            store(s - lag, *back(lag, n, b))
                    sweep(act, step)
                    for b in range(2):
                        act.wait_ge(e_st[b], n_st * len(range(b, G, 2)))
                        if kind == 0:
                            act.wait_ge(e_hs[b], 16 * len(range(b, G, 2)))
            close(edge_sems, e_ga)
            with nc.Block() as block:
                @block.sync
                def _(sp):
                    sp.dma_start(agg[:, :, :], nodesum[0:N, :].rearrange("(p b) d -> p b d", p=P)).then_inc(n_hm, 16)
                    if kind == 0:
                        sp.dma_start(aggw[:, :, :], nodew[0:N, :].rearrange("(p b) d -> p b d", p=P)).then_inc(n_hm, 16)
                    sp.wait_ge(n_hm, 32 if kind == 0 else 16)
            close((n_hm,))

        def message_sums(kind):
            with nc.If(is_dense > 0):
                nc.all_engine_barrier()
                dense_phase(kind)
            nc.all_engine_barrier()
            with nc.If(is_dense < 1):
                nc.all_engine_barrier()
                with nc.Block() as block:
                    @block.vector
                    def _(dve):
                        dve.memset(agg[:, :, :], 0.0)
                        dve.memset(aggw[:, :, :], 0.0)
                        dve.tensor_copy(iw0[:, :], iota_w[:, 0:1]).then_inc(n_ad, 1)
                        dve.wait_ge(n_ad, 1)
                        dve.tensor_scalar(iota_w[:, :], iota_w[:, :], iw0[:, 0:1], None, ALU.subtract).then_inc(n_ad, 1)
                        dve.wait_ge(n_ad, 2)
                close((n_ad,))
                with nc.Fori(0, passes) as p:
                    edge_phase(kind, p)
                    bring_home(kind, p)

        m_ch, m_ac, m_ra, m_tr, m_tc, m_mm, m_mc, m_st, m_pw = [sem(n) for n in (
            "node_dve_chain", "node_act_done", "node_act_asked", "node_transposed", "node_transposed_copied",
            "node_products", "node_products_read", "features_stored", "window_reset")]
        node_sems = (m_ch, m_ac, m_ra, m_tr, m_tc, m_mm, m_mc, m_st, m_pw)
        tp = sb("tp", [128, 4, 2, P])
        QB = NB // 4
        Fl = "p b d -> p (b d)"

        def rows_of(t, q):
            return t[:, 4 * q:4 * q + 4, :].rearrange(Fl)

        def out_bank(q):
            return ps[2 + q % 6]

        def products(block, operands, weights, ready, relu_bias=None, after=lambda act, q: None):
            @block.tensor
            def _(pe):
                wait(pe, m_ra, ready)
                for q in range(QB + 2):
                    if q < QB:
                        if q >= 2:
                            pe.wait_ge(m_tc, q - 1)
                        for k, t in enumerate(operands):
                            last = pe.transpose(ps[q % 2][:, 128 * k:128 * k + P], rows_of(t, q), ident[0:P, 0:P])
                        last.then_inc(m_tr, 1)
                    if q >= 2:
                        c = q - 2
                        pe.wait_ge(m_tc, c + 1)
                        if c >= 6:
                            pe.wait_ge(m_mc, c - 5)
                        for at, width, k, wt, first, stop in weights:
                            last = pe.matmul(out_bank(c)[0:P, at:at + width], lhsT=tp[:, c % 4, k, :], rhs=wt,
                                             start=first, stop=stop)
                        last.then_inc(m_mm, 1)

            @block.scalar
            def _(act):
                for q in range(QB):
                    act.wait_ge(m_tr, q + 1)
                    if q >= 4:
                        act.wait_ge(m_mm, q - 3)
                    if relu_bias is None:
                        act.activation(tp[:, q % 4, 0:len(operands), :],
                                       ps[q % 2][:, 0:128 * len(operands)].rearrange("p (k n) -> p k n", n=128)[:, :, 0:P],
                                       ACT.Copy).then_inc(m_tc, 1)
                    else:
                        act.activation(tp[:, q % 4, 0, :], ps[q % 2][:, 0:P], ACT.Relu, bias=relu_bias[:, 0:1])
                        act.activation(tp[:, q % 4, 1, :], ps[q % 2][:, 128:128 + P], ACT.Copy).then_inc(m_tc, 1)
                    after(act, q)
                after(act, QB)

        def bcast_d(t):
            return t[:, :, None].to_broadcast([P, NB, D])

        def norm(dve, link, n_act):
            link(dve.tensor_reduce(mean[:, :], xcur[:, :, :], AX.X, ALU.add))
            link(dve.tensor_scalar(mean[:, :], mean[:, :], 1.0 / D, None, ALU.mult))
            link(dve.tensor_tensor(hcur[:, :, :], xcur[:, :, :], bcast_d(mean), ALU.subtract))
            link(dve.tensor_tensor(tmp[:, :, :], hcur[:, :, :], hcur[:, :, :], ALU.mult))
            dve.tensor_reduce(rstd[:, :], tmp[:, :, :], AX.X, ALU.add).then_inc(m_pw, 1)
            dve.wait_ge(m_ac, n_act)
            link(dve.reciprocal(rstd[:, :], rstd[:, :]))
            link(dve.tensor_tensor(hcur[:, :, :], hcur[:, :, :], bcast_d(rstd), ALU.mult))
            link(dve.tensor_scalar(hcur[:, :, :], hcur[:, :, :], 0.0, None, ALU.max))

        def root(act, n):
            act.wait_ge(m_pw, n)
            act.activation(rstd[:, :], rstd[:, :], ACT.Sqrt, bias=ln_eps[:, 0:1], scale=1.0 / D).then_inc(m_ac, 1)

        def store_features(sp, t, n):
            sp.wait_ge(m_st, n)
            sp.dma_start(feat.rearrange("(p b) d -> p b d", p=P), t[:, :, :]).then_inc(m_st, 16)
            sp.wait_ge(m_st, 16 + n)

        with nc.Block() as block:
            @block.vector
            def _(dve):
                link = Chain(dve, m_ch)
                dve.memset(en1_bd[:, :], 0.0).then_inc(e_w1, 1)
                for c in range(4):
                    dve.tensor_copy(ident4[D * c:D * c + D, :], ident[D * c:D * c + D, D * c:D * c + D])
                dve.memset(eft[2 * D:2 * D + 1, :, :], 1.0).then_inc(e_w1, 1)
                norm(dve, link, 1)
                dve.memset(mean[:, 0:1], 0.0).then_inc(m_st, 1)

            @block.scalar
            def _(act):
                root(act, 1)

            @block.sync
            def _(sp):
                sp.wait_ge(e_w1, 2)
                for j in range(2):
                    sp.dma_start(en1_bd[D * j:D * j + D, KF * j:KF * j + KF], en1[:, :]).then_inc(e_w1, 16)
                    sp.dma_start(en1_bd[2 * D:2 * D + 1, KF * j:KF * j + KF], en1_b[None, :]).then_inc(e_w1, 16)
                store_features(sp, hcur, 1)
        close(node_sems)

        message_sums(0)

        with nc.Block() as block:
            @block.vector
            def _(dve):
                link = Chain(dve, m_ch)
                link(dve.tensor_scalar(dis[:, :], aggw[:, :, 0:1].rearrange(Fl), 1.0, None, ALU.add))
                link(dve.tensor_scalar(cnt[:, :], aggw[:, :, 1:2].rearrange(Fl), 1.0, None, ALU.max))
                link(dve.reciprocal(cnt[:, :], cnt[:, :]))
                dve.tensor_tensor(tmp[:, :, :], agg[:, :, 0:D], bcast_d(cnt), ALU.mult).then_inc(m_ra, 1)
                for q in range(QB):
                    dve.wait_ge(m_mm, q + 1)
                    dve.tensor_tensor(gat[:, 4 * q:4 * q + 4, 0:D],
                                      out_bank(q)[0:P, 0:4 * D].rearrange("p (b d) -> p b d", d=D),
                                      bias0[:, None, :].to_broadcast([P, 4, D]), ALU.add).then_inc(m_mc, 1)
                dve.wait_ge(m_mc, QB)
                link(dve.scalar_tensor_tensor(xcur[:, :, :], gat[:, :, 0:D], 0.0, xcur[:, :, :], ALU.max, ALU.add))
                norm(dve, link, 2)
                dve.memset(mean[:, 0:1], 0.0).then_inc(m_st, 1)

            def scalars(act, q):
                if q < QB:
                    return
                act.activation(dis[:, :], dis[:, :], ACT.Sqrt).then_inc(m_ac, 1)
                root(act, 1)

            products(block, (hcur, tmp), ((0, 4 * D, 0, bd_a[:, :], True, False), (0, 4 * D, 1, bd_b[:, :], False, True)),
                     1, after=scalars)
        close(node_sems)

        with nc.Block() as block:
            @block.vector
            def _(dve):
                link = Chain(dve, m_ch)
                dve.reciprocal(dis[:, :], dis[:, :]).then_inc(m_ra, 1)
                dve.tensor_tensor(bias_ih[:, 0:2 * D], bias_ih[:, 0:2 * D], bias_hh[:, 0:2 * D], ALU.add)
                for q in range(QB):
                    dve.wait_ge(m_mm, q + 1)
                    dve.tensor_tensor(tmp[:, 4 * q:4 * q + 4, :],
                                      out_bank(q)[0:P, 0:4 * D].rearrange("p (b d) -> p b d", d=D),
                                      bias_lin[:, None, :].to_broadcast([P, 4, D]), ALU.add).then_inc(m_mc, 1)
                dve.wait_ge(m_mc, QB)
                dve.tensor_scalar(hcur[:, :, :], tmp[:, :, :], 0.0, None, ALU.max).then_inc(m_st, 1)

            @block.sync
            def _(sp):
                store_features(sp, hcur, 1)
            products(block, (hcur,), ((0, 4 * D, 0, bd_lin[:, :], True, True),), 1)
        close(node_sems)

        gview = gb[0:P, :, :, :].rearrange("p a i s -> p (a i s)")
        RZ = gview[:, 0:NB * 2 * D].rearrange("p (b c d) -> p b c d", c=2, d=D)
        inn = gat
        hn = sb("hn", [P, NB, D])
        CHUNKS = 5
        CQ = QB // CHUNKS
        m_ta, m_up, m_fs = [sem(n) for n in ("candidates_ready", "update_chain", "chunk_stored")]

        def chunk(c):
            return slice(4 * CQ * c, 4 * CQ * c + 4 * CQ)

        with nc.Fori(0, STEPS) as _step:
            message_sums(1)
            with nc.Block() as block:
                @block.vector
                def _(dve):
                    def gates_in(c):
                        for q in range(CQ * c, CQ * c + CQ):
                            bank = out_bank(q)
                            bs = slice(4 * q, 4 * q + 4)
                            dve.wait_ge(m_mm, q + 1)
                            dve.tensor_tensor(RZ[:, bs, :, :].rearrange("p b c d -> p b (c d)"),
                                              bank[0:P, 0:8 * D].rearrange("p (b c) -> p b c", c=2 * D),
                                              bias_ih[:, None, 0:2 * D].to_broadcast([P, 4, 2 * D]), ALU.add)
                            dve.tensor_tensor(inn[:, bs, 0:D], bank[0:P, 8 * D:12 * D].rearrange("p (b d) -> p b d", d=D),
                                              bias_ih[:, None, 2 * D:3 * D].to_broadcast([P, 4, D]), ALU.add)
                            dve.tensor_tensor(hn[:, bs, :], bank[0:P, 12 * D:16 * D].rearrange("p (b d) -> p b d", d=D),
                                              bias_hh[:, None, 2 * D:3 * D].to_broadcast([P, 4, D]), ALU.add
                                              ).then_inc(m_mc, 1)

                    def candidate_in(c):
                        bs = chunk(c)
                        dve.wait_ge(m_mc, CQ * c + CQ)
                        dve.wait_ge(m_ac, c + 1)
                        dve.tensor_tensor(hn[:, bs, :], RZ[:, bs, 0, :], hn[:, bs, :], ALU.mult).then_inc(m_ch, 1)
                        dve.wait_ge(m_ch, c + 1)
                        dve.tensor_tensor(hn[:, bs, :], hn[:, bs, :], inn[:, bs, 0:D], ALU.add).then_inc(m_pw, 1)

                    def update(c):
                        bs = chunk(c)
                        dve.wait_ge(m_ta, c + 1)
                        dve.tensor_tensor(tmp[:, bs, :], hcur[:, bs, :], hn[:, bs, :], ALU.subtract).then_inc(m_up, 1)
                        dve.wait_ge(m_up, 2 * c + 1)
                        dve.tensor_tensor(tmp[:, bs, :], tmp[:, bs, :], RZ[:, bs, 1, :], ALU.mult).then_inc(m_up, 1)
                        dve.wait_ge(m_up, 2 * c + 2)
                        dve.tensor_tensor(hcur[:, bs, :], tmp[:, bs, :], hn[:, bs, :], ALU.add).then_inc(m_st, 1)

                    for c in range(CHUNKS + 2):
                        if c < CHUNKS:
                            gates_in(c)
                        if 1 <= c <= CHUNKS:
                            candidate_in(c - 1)
                        if c >= 2:
                            update(c - 2)

                @block.sync
                def _(sp):
                    rows = feat.rearrange("(p b) d -> p b d", p=P)
                    for c in range(CHUNKS):
                        sp.wait_ge(m_st, c + 1)
                        sp.dma_start(rows[:, chunk(c), :], hcur[:, chunk(c), :]).then_inc(m_fs, 16)
                    sp.wait_ge(m_fs, 16 * CHUNKS)

                def gate_functions(act, q):
                    for c in range(CHUNKS):
                        if q == min(CQ * c + CQ + 2, QB):
                            act.wait_ge(m_mc, CQ * c + CQ)
                            act.activation(RZ[:, chunk(c), :, :].rearrange("p b c d -> p (b c d)"),
                                           RZ[:, chunk(c), :, :].rearrange("p b c d -> p (b c d)"), ACT.Sigmoid
                                           ).then_inc(m_ac, 1)
                    for c in range(CHUNKS):
                        if q == min(CQ * c + 2 * CQ + 2, QB):
                            act.wait_ge(m_pw, c + 1)
                            act.activation(hn[:, chunk(c), :], hn[:, chunk(c), :], ACT.Tanh).then_inc(m_ta, 1)

                products(block, (agg, hcur), (
                    (0, 8 * D, 0, bd_ih[:, 0:8 * D], True, False), (0, 8 * D, 1, bd_hh[:, 0:8 * D], False, True),
                    (8 * D, 4 * D, 0, bd_ih[:, 8 * D:12 * D], True, True),
                    (12 * D, 4 * D, 1, bd_hh[:, 8 * D:12 * D], True, True)), 0, bias_conv, gate_functions)
            close((*node_sems, m_ta, m_up, m_fs))

        with nc.Block() as block:
            @block.vector
            def _(dve):
                link = Chain(dve, m_ch)
                link(dve.tensor_tensor(xcur[:, :, :], xcur[:, :, :], hcur[:, :, :], ALU.add))
                link(dve.tensor_scalar(eps_sb[:, :], eps_sb[:, :], 1.0, None, ALU.add))
                norm(dve, link, 1)
                dve.memset(mean[:, 0:1], 0.0).then_inc(m_st, 1)

            @block.scalar
            def _(act):
                root(act, 1)

            @block.sync
            def _(sp):
                store_features(sp, hcur, 1)
        close(node_sems)
        message_sums(2)

        with nc.Block() as block:
            @block.vector
            def _(dve):
                link = Chain(dve, m_ch)
                link(dve.scalar_tensor_tensor(tmp[:, :, :], hcur[:, :, :], eps_sb[:, 0:1], agg[:, :, 0:D],
                                              ALU.mult, ALU.add))
                link(dve.tensor_tensor(xcur[:, :, :], xcur[:, :, :], tmp[:, :, :], ALU.add))
                norm(dve, link, 1)
                dve.tensor_tensor(hcur[:, :, :], hcur[:, :, :], bcast_d(dis), ALU.mult).then_inc(m_st, 1)

            @block.scalar
            def _(act):
                root(act, 1)

            @block.sync
            def _(sp):
                store_features(sp, hcur, 1)
        close(node_sems)
        message_sums(3)

        with nc.Block() as block:
            @block.vector
            def _(dve):
                link = Chain(dve, m_ch)
                link(dve.tensor_tensor(tmp[:, :, :], agg[:, :, 0:D], hcur[:, :, :], ALU.add))
                link(dve.tensor_tensor(tmp[:, :, :], tmp[:, :, :], bcast_d(dis), ALU.mult))
                dve.tensor_tensor(xcur[:, :, :], xcur[:, :, :], tmp[:, :, :], ALU.add).then_inc(m_st, 1)

            @block.sync
            def _(sp):
                sp.wait_ge(m_st, 1)
                sp.dma_start(out.rearrange("(p b) d -> p b d", p=P), xcur[:, :, :]).then_inc(m_st, 16)
                sp.wait_ge(m_st, 17)


def kernel(x, src, dst, edge_attr_32, L0_gnn_W, L0_gnn_b, L1_gnn_lin0_w, L1_gnn_lin0_b, L1_gnn_en1_w, L1_gnn_en1_b,
           L1_gnn_en2_w, L1_gnn_en2_b, L1_gnn_conv_bias, L1_gnn_gru_wih, L1_gnn_gru_whh, L1_gnn_gru_bih,
           L1_gnn_gru_bhh, L2_gnn_eps):
    import numpy as np
    import concourse.bacc as bacc
    from concourse.bass_utils import run_bass_kernel_spmd

    src, dst, ef = np.asarray(src), np.asarray(dst), np.asarray(edge_attr_32)
    src_p = np.zeros((T, EDGES), np.int32)
    src_p.reshape(-1)[:E] = src
    dst_p = np.full((RB * 128, EDGES), PAD_DST, np.int32)
    dst_p.reshape(-1)[:E] = dst
    ef_p = np.zeros((T * EDGES, D), np.float32)
    ef_p[:E] = ef
    ef_p = ef_p.reshape(G, GT, EDGES, D)
    ins = [
        ("x", x), ("srcg", src_p.reshape(G, GT, EDGES).transpose(0, 2, 1)), ("src_t", src_p.T), ("dst_t", dst_p[:T].T),
        ("dst_rows", dst_p),
        ("ef_e", ef_p.transpose(0, 2, 1, 3).reshape(G, EDGES, GT * D)),
        ("ef_t", ef_p.reshape(G, GT // 2, 2, EDGES, D).transpose(0, 2, 4, 1, 3).reshape(G, 2 * D, GT // 2 * EDGES)),
        ("w0", L0_gnn_W), ("b0", L0_gnn_b), ("lin0", np.asarray(L1_gnn_lin0_w).T), ("lin0_b", L1_gnn_lin0_b),
        ("en1", np.asarray(L1_gnn_en1_w).T), ("en1_b", L1_gnn_en1_b), ("en2", np.asarray(L1_gnn_en2_w).T),
        ("en2_b", L1_gnn_en2_b), ("conv_b", L1_gnn_conv_bias), ("wih", np.asarray(L1_gnn_gru_wih).T),
        ("whh", np.asarray(L1_gnn_gru_whh).T), ("bih", L1_gnn_gru_bih), ("bhh", L1_gnn_gru_bhh), ("eps", L2_gnn_eps),
    ]
    nc = bacc.Bacc("TRN2", target_bir_lowering=False, num_devices=1)
    arrays, args = {}, []
    for name, a in ins:
        a = np.ascontiguousarray(a)
        arrays[f"in_{name}"] = a
        args.append(nc.dram_tensor(f"in_{name}", a.shape, mybir.dt.from_np(a.dtype), kind="ExternalInput").ap())
    args.append(nc.dram_tensor("out_0", (N, D), mybir.dt.float32, kind="ExternalOutput").ap())
    bass_gnn(nc, *args)
    return run_bass_kernel_spmd(nc, [arrays], core_ids=[0]).results[0]["out_0"]
```
